# Optimizing a Trainium2 kernel written in Bass

```python
import numpy as np
import jax
import jax.numpy as jnp

def _softmax(x, axis=-1):
    return jax.nn.softmax(x, axis=axis)

def _gelu(x):
    return jax.nn.gelu(x, approximate=True)

def _silu(x):
    return jax.nn.silu(x)

def _sigmoid(x):
    return jax.nn.sigmoid(x)

def _layernorm(x, axis=-1, eps=1e-05):
    m = jnp.mean(x, axis=axis, keepdims=True)
    v = jnp.var(x, axis=axis, keepdims=True)
    return (x - m) / jnp.sqrt(v + eps)

def _scatter_add(tgt, idx, src, axis=0):
    return tgt.at[idx].add(src)

def _segment_sum(src, seg, n):
    return jax.ops.segment_sum(src, seg, n)
kernel_name = 'mk_flamingo_gated_d2_seqx_r8_b66513'

def setup_inputs(seed: int=0):
    np.random.seed(seed)
    _w = jnp.asarray

    def _rec_inputs():
        import jax
        import jax.numpy as jnp
        _rk = jax.random.key(seed)
        x = -0.0003929 + 0.9999 * jax.random.normal(jax.random.fold_in(_rk, 1), (4, 256, 512), jnp.float32)
        _lenS = 256 - jax.random.randint(jax.random.fold_in(_rk, 7), (4,), 0, max(1, 256 // 4) + 1, jnp.int32)
        _lenS2 = 64 - jax.random.randint(jax.random.fold_in(_rk, 8), (4,), 0, max(1, 64 // 4) + 1, jnp.int32)
        _ctx_4096P = jax.random.normal(jax.random.fold_in(_rk, 11), (4, 16, 512), jnp.float32)
        _ctx_4096c = jax.random.dirichlet(jax.random.fold_in(_rk, 511), 0.3 * jnp.ones((16,), jnp.float32), (4, 64))
        _ctx_4096t = jnp.einsum('bsk,bkd->bsd', _ctx_4096c, _ctx_4096P)
        _ctx_4096t = _ctx_4096t * jax.lax.rsqrt(jnp.mean(jnp.square(_ctx_4096t)) + 1e-12) * 0.953939
        ctx_4096 = 2.81802e-05 + 1.00001 * (_ctx_4096t + 0.3 * jax.random.normal(jax.random.fold_in(_rk, 611), (4, 64, 512), jnp.float32))
        _g = jax.random.normal(jax.random.fold_in(_rk, 9001), (2, 2), jnp.float32)
        _g = jnp.sign(_g) * jnp.maximum(jnp.abs(_g), 1.0) + (_g == 0) * 1.0
        g_xattn = _g[0]
        g_ffn = _g[1]
        return (x, ctx_4096, g_xattn, g_ffn)
    x, ctx_4096, g_xattn, g_ffn = _rec_inputs()

    def _L0_xattn_setup():
        import jax, jax.numpy as jnp
        import numpy as np
        HID = 512
        NHEAD = 32
        NKV = 8
        HDIM = 128
        G = NHEAD // NKV
        key = jax.random.key(seed)
        ks = jax.random.split(key, 6)
        s = 0.02
        B, L = (2, 256)
        return {'query': jax.random.normal(ks[0], (B, L, HID), jnp.float32), 'kv': jax.random.normal(ks[1], (B, L, HID), jnp.float32), 'Wq': jax.random.normal(ks[2], (HID, NHEAD * HDIM), jnp.float32) * s, 'bq': jnp.zeros((NHEAD * HDIM,), jnp.float32), 'Wkv': jax.random.normal(ks[3], (HID, 2 * NKV * HDIM), jnp.float32) * s, 'bkv': jnp.zeros((2 * NKV * HDIM,), jnp.float32), 'Wo': jax.random.normal(ks[4], (NHEAD * HDIM, HID), jnp.float32) * s, 'bo': jnp.zeros((HID,), jnp.float32)}
    _L0_xattn_all = _L0_xattn_setup()
    _L0_xattn_in = {k: v for k, v in _L0_xattn_all.items() if k in ('Wq', 'bq', 'Wkv', 'bkv', 'Wo', 'bo')}
    del _L0_xattn_all

    def _L0_ffn_setup():
        import jax, jax.numpy as jnp
        import numpy as np
        H = 512
        I = 1376
        B, S = (2, 256)
        key = jax.random.key(seed)
        k1, k2, k3 = jax.random.split(key, 3)
        x = jax.random.normal(k1, (B, S, H), dtype=jnp.float32)
        w_gate_up = jax.random.normal(k2, (2 * I, H), dtype=jnp.float32) * 0.02
        w_down = jax.random.normal(k3, (H, I), dtype=jnp.float32) * 0.02
        return {'x': x, 'w_gate_up': w_gate_up, 'w_down': w_down}
    _L0_ffn_all = _L0_ffn_setup()
    _L0_ffn_in = {k: v for k, v in _L0_ffn_all.items() if k in ('w_gate_up', 'w_down')}
    del _L0_ffn_all

    def _L1_xattn_setup():
        import jax, jax.numpy as jnp
        import numpy as np
        HEADS = 32
        KV_HEADS = 8
        HEAD_DIM = 128
        EPS = 1e-06

        def rms_norm(x, w):
            var = jnp.mean(jnp.square(x.astype(jnp.float32)), axis=-1, keepdims=True)
            return (x.astype(jnp.float32) * jax.lax.rsqrt(var + EPS)).astype(x.dtype) * w
        key = jax.random.key(seed)
        ks = jax.random.split(key, 6)
        bsz, n_lat, seq, hidden = (8, 64, 512, 512)
        return {'latents': jax.random.normal(ks[0], (bsz, n_lat, hidden), jnp.float32), 'context': jax.random.normal(ks[1], (bsz, seq, hidden), jnp.float32), 'Wq': jax.random.normal(ks[2], (hidden, HEADS * HEAD_DIM), jnp.float32) * 0.02, 'Wk': jax.random.normal(ks[3], (hidden, KV_HEADS * HEAD_DIM), jnp.float32) * 0.02, 'Wv': jax.random.normal(ks[4], (hidden, KV_HEADS * HEAD_DIM), jnp.float32) * 0.02, 'Wo': jax.random.normal(ks[5], (HEADS * HEAD_DIM, hidden), jnp.float32) * 0.02, 'q_norm_w': jnp.ones((HEAD_DIM,), jnp.float32), 'k_norm_w': jnp.ones((HEAD_DIM,), jnp.float32)}
    _L1_xattn_all = _L1_xattn_setup()
    _L1_xattn_in = {k: v for k, v in _L1_xattn_all.items() if k in ('Wq', 'Wk', 'Wv', 'Wo', 'q_norm_w', 'k_norm_w')}
    del _L1_xattn_all

    def _L1_ffn_setup():
        import jax, jax.numpy as jnp
        import numpy as np
        N_EXPERTS = 28
        TOP_K = 2
        RANK = 8
        LORA_ALPHA = 16
        SCALING = LORA_ALPHA / RANK
        TEMP = 1.0
        key = jax.random.key(seed)
        ks = jax.random.split(key, 5)
        B, S, D_IN, D_OUT = (4, 256, 512, 512)
        x = jax.random.normal(ks[0], (B, S, D_IN), dtype=jnp.float32)
        base_W = jax.random.normal(ks[1], (D_OUT, D_IN), dtype=jnp.float32) * (1.0 / np.sqrt(D_IN))
        gate_W = jax.random.normal(ks[2], (N_EXPERTS, D_IN), dtype=jnp.float32) * (1.0 / np.sqrt(D_IN))
        lora_A = jax.random.normal(ks[3], (N_EXPERTS, RANK, D_IN), dtype=jnp.float32) * (1.0 / np.sqrt(D_IN))
        lora_B = jax.random.normal(ks[4], (N_EXPERTS, D_OUT, RANK), dtype=jnp.float32) * 0.01
        return {'x': x, 'base_W': base_W, 'gate_W': gate_W, 'lora_A': lora_A, 'lora_B': lora_B}
    _L1_ffn_all = _L1_ffn_setup()
    _L1_ffn_in = {k: v for k, v in _L1_ffn_all.items() if k in ('base_W', 'gate_W', 'lora_A', 'lora_B')}
    del _L1_ffn_all
    return {'x': x, 'ctx_4096': ctx_4096, 'g_xattn': g_xattn, 'g_ffn': g_ffn, 'L0_xattn_Wq': _L0_xattn_in['Wq'], 'L0_xattn_bq': _L0_xattn_in['bq'], 'L0_xattn_Wkv': _L0_xattn_in['Wkv'], 'L0_xattn_bkv': _L0_xattn_in['bkv'], 'L0_xattn_Wo': _L0_xattn_in['Wo'], 'L0_xattn_bo': _L0_xattn_in['bo'], 'L0_ffn_w_gate_up': _L0_ffn_in['w_gate_up'], 'L0_ffn_w_down': _L0_ffn_in['w_down'], 'L1_xattn_Wq': _L1_xattn_in['Wq'], 'L1_xattn_Wk': _L1_xattn_in['Wk'], 'L1_xattn_Wv': _L1_xattn_in['Wv'], 'L1_xattn_Wo': _L1_xattn_in['Wo'], 'L1_xattn_q_norm_w': _L1_xattn_in['q_norm_w'], 'L1_xattn_k_norm_w': _L1_xattn_in['k_norm_w'], 'L1_ffn_base_W': _L1_ffn_in['base_W'], 'L1_ffn_gate_W': _L1_ffn_in['gate_W'], 'L1_ffn_lora_A': _L1_ffn_in['lora_A'], 'L1_ffn_lora_B': _L1_ffn_in['lora_B']}

def reference(x, ctx_4096, g_xattn, g_ffn, L0_xattn_Wq, L0_xattn_bq, L0_xattn_Wkv, L0_xattn_bkv, L0_xattn_Wo, L0_xattn_bo, L0_ffn_w_gate_up, L0_ffn_w_down, L1_xattn_Wq, L1_xattn_Wk, L1_xattn_Wv, L1_xattn_Wo, L1_xattn_q_norm_w, L1_xattn_k_norm_w, L1_ffn_base_W, L1_ffn_gate_W, L1_ffn_lora_A, L1_ffn_lora_B):
    import jax
    import jax.numpy as jnp

    def _L0_xattn_ref(query, kv, Wq, bq, Wkv, bkv, Wo, bo):
        import jax, jax.numpy as jnp
        import numpy as np
        HID = 512
        NHEAD = 32
        NKV = 8
        HDIM = 128
        G = NHEAD // NKV
        B, L, _ = query.shape
        Lk = kv.shape[1]
        scale = jnp.asarray(1.0 / np.sqrt(HDIM), query.dtype)
        q = (query @ Wq + bq).reshape(B, L, NKV, G, HDIM)
        k_, v_ = jnp.split(kv @ Wkv + bkv, 2, axis=-1)
        k = k_.reshape(B, Lk, NKV, HDIM)
        v = v_.reshape(B, Lk, NKV, HDIM)
        scores = jnp.einsum('blkgd,bmkd->bkglm', q, k) * scale
        attn = jax.nn.softmax(scores, axis=-1)
        o = jnp.einsum('bkglm,bmkd->blkgd', attn, v).reshape(B, L, NHEAD * HDIM)
        return o @ Wo + bo

    def _L0_ffn_ref(x, w_gate_up, w_down):
        import jax, jax.numpy as jnp
        import numpy as np
        H = 512
        I = 1376
        B, S = (2, 256)
        gate_up = jnp.einsum('bsh,oh->bso', x, w_gate_up)
        d = gate_up.shape[-1] // 2
        h = jax.nn.silu(gate_up[..., :d]) * gate_up[..., d:]
        return jnp.einsum('bsi,hi->bsh', h, w_down)

    def _L1_xattn_ref(latents, context, Wq, Wk, Wv, Wo, q_norm_w, k_norm_w):
        import jax, jax.numpy as jnp
        import numpy as np
        HEADS = 32
        KV_HEADS = 8
        HEAD_DIM = 128
        EPS = 1e-06

        def rms_norm(x, w):
            var = jnp.mean(jnp.square(x.astype(jnp.float32)), axis=-1, keepdims=True)
            return (x.astype(jnp.float32) * jax.lax.rsqrt(var + EPS)).astype(x.dtype) * w
        bsz, q_len, hidden = latents.shape
        kv = jnp.concatenate([context, latents], axis=1)
        kv_len = kv.shape[1]
        groups = HEADS // KV_HEADS
        q = (latents @ Wq).reshape(bsz, q_len, HEADS, HEAD_DIM).transpose(0, 2, 1, 3)
        k = (kv @ Wk).reshape(bsz, kv_len, KV_HEADS, HEAD_DIM).transpose(0, 2, 1, 3)
        v = (kv @ Wv).reshape(bsz, kv_len, KV_HEADS, HEAD_DIM).transpose(0, 2, 1, 3)
        q = rms_norm(q, q_norm_w)
        k = rms_norm(k, k_norm_w)
        qg = q.reshape(bsz, KV_HEADS, groups, q_len, HEAD_DIM)
        scale = 1.0 / np.sqrt(HEAD_DIM)
        scores = jnp.einsum('bhgqd,bhkd->bhgqk', qg, k) * scale
        probs = jax.nn.softmax(scores.astype(jnp.float32), axis=-1).astype(q.dtype)
        out = jnp.einsum('bhgqk,bhkd->bhgqd', probs, v)
        out = out.reshape(bsz, HEADS, q_len, HEAD_DIM).transpose(0, 2, 1, 3)
        out = out.reshape(bsz, q_len, HEADS * HEAD_DIM)
        return out @ Wo

    def _L1_ffn_ref(x, base_W, gate_W, lora_A, lora_B):
        import jax, jax.numpy as jnp
        import numpy as np
        N_EXPERTS = 28
        TOP_K = 2
        RANK = 8
        LORA_ALPHA = 16
        SCALING = LORA_ALPHA / RANK
        TEMP = 1.0
        B, S, D_in = x.shape
        xf = x.reshape(B * S, D_in)
        base = xf @ base_W.T
        logits = xf @ gate_W.T
        top_vals, top_idx = jax.lax.top_k(logits, TOP_K)
        top_probs = jax.nn.softmax(top_vals / TEMP, axis=-1)
        N = xf.shape[0]
        gate_full = jnp.zeros((N, N_EXPERTS), dtype=xf.dtype).at[jnp.arange(N)[:, None], top_idx].add(top_probs)
        h = jnp.einsum('nd,erd->ner', xf, lora_A)
        h = h * (gate_full * SCALING)[:, :, None]
        lora_out = jnp.einsum('ner,eor->no', h, lora_B)
        out = base + lora_out
        return out.reshape(B, S, -1)
    x = x + jnp.tanh(g_xattn[0]) * _L0_xattn_ref(_layernorm(x, axis=-1), ctx_4096, L0_xattn_Wq, L0_xattn_bq, L0_xattn_Wkv, L0_xattn_bkv, L0_xattn_Wo, L0_xattn_bo)
    x = x + jnp.tanh(g_ffn[0]) * _L0_ffn_ref(_layernorm(x, axis=-1), L0_ffn_w_gate_up, L0_ffn_w_down)
    x = x + jnp.tanh(g_xattn[1]) * _L1_xattn_ref(_layernorm(x, axis=-1), ctx_4096, L1_xattn_Wq, L1_xattn_Wk, L1_xattn_Wv, L1_xattn_Wo, L1_xattn_q_norm_w, L1_xattn_k_norm_w)
    x = x + jnp.tanh(g_ffn[1]) * _L1_ffn_ref(_layernorm(x, axis=-1), L1_ffn_base_W, L1_ffn_gate_W, L1_ffn_lora_A, L1_ffn_lora_B)
    return x

_drawn_inputs = setup_inputs


def setup_inputs(seed=0):
    import zlib

    import numpy as np

    out = dict(_drawn_inputs(seed))
    spreads = {'g_ffn': (-1.0, 0.2),
     'L0_xattn_bq': (0.0, 0.8),
     'L0_xattn_bkv': (0.0, 0.1),
     'L0_xattn_bo': (0.0, 0.1),
     'L1_xattn_q_norm_w': (1.0, 0.6),
     'L1_xattn_k_norm_w': (1.0, 0.6)}
    factors = {'L0_xattn_Wq': 3.45}
    for name, (base, spread) in spreads.items():
        noise = np.random.default_rng([zlib.crc32(name.encode()), seed]).standard_normal(out[name].shape)
        drawn = base * np.exp(spread * noise) if base else spread * noise
        out[name] = jnp.asarray(drawn.astype(out[name].dtype))
    for name, factor in factors.items():
        out[name] = (out[name] * factor).astype(out[name].dtype)
    return out
```

```python
import concourse.bass as bass
from concourse import mybir
from contextlib import ExitStack

F32 = mybir.dt.float32
F32R = mybir.dt.float32r
ALU = mybir.AluOpType
ACT = mybir.ActivationFunctionType
AX = mybir.AxisListType

PART = 128
BATCH, SEQ, HID = 4, 256, 512
CTX = 64
CH = HID // PART
NT = BATCH * SEQ // PART
HD = 128
NKV = 8
GH = 4
INNER = 1376
IC = 11
ILAST = INNER - (IC - 1) * PART
NEXP, RANK = 28, 8
LR = NEXP * RANK
LN_EPS, RMS_EPS = 1e-5, 1e-6
SCALE = float(HD) ** -0.5
LORA_SCALE = 16.0 / RANK


def f(ap):
    return ap.bitcast(F32)


def mm3(pe, out, w, m, start, stop):
    pe.matmul(out, w[1], m[0], start=start, stop=False)
    pe.matmul(out, w[0], m[1], start=False, stop=False)
    return pe.matmul(out, w[0], m[0], start=False, stop=stop)


KVRING = 0


class Kernel:
    pass


def load_phase(nc, k, sem):
    in_x, in_small, in_ctx = sem("in_x"), sem("in_small"), sem("in_ctx")
    ident0, ident = sem("ident0"), sem("ident")
    gates = sem("gates")
    ctx_hi, ctx_lo = sem("ctx_hi"), sem("ctx_lo")
    ones_set = sem("ones_set")
    with nc.Block() as block:
        @block.sync
        def _(sp):
            sp.dma_start(k.x[:, :, :], k.d["x"].rearrange("(t p) c -> p t c", p=PART)).then_inc(in_x, 16)
            sp.dma_start(k.gate_raw[:, :], k.d["gates"].to_broadcast([PART, 4])).then_inc(in_small, 16)
            sp.dma_start(k.bo[:, :], k.d["bo"].to_broadcast([PART, HID])).then_inc(in_small, 16)
            sp.dma_start(k.normw[:, :], k.d["normw"]).then_inc(in_small, 16)
            sp.dma_start(k.raw_q[:, 0:CH * BATCH * CTX], k.d["ctxT"]).then_inc(in_ctx, 16)
            sp.wait_ge(in_x, 16)

        @block.gpsimd
        def _(pool):
            pool.memset(k.ident[:, :], 0.0).then_inc(ident0, 1)
            pool.memset(k.minus_half[:, :], -0.5)
            pool.wait_ge(ident0, 1)
            pool.affine_select(out=k.ident[:, :], in_=k.ident[:, :], compare_op=ALU.not_equal, fill=1.0,
                               base=0, pattern=[[-1, PART]], channel_multiplier=1).then_inc(ident, 1)
            pool.wait_ge(ctx_hi, 1)
            pool.tensor_tensor(k.ctxT[1][:, :], k.raw_q[:, 0:CH * BATCH * CTX], f(k.ctxT[0][:, :]),
                               ALU.subtract).then_inc(ctx_lo, 1)
            pool.wait_ge(ident, 1)

        @block.scalar
        def _(act):
            act.wait_ge(in_small, 48)
            act.activation(k.gate[:, :], k.gate_raw[:, :], ACT.Tanh).then_inc(gates, 1)
            act.wait_ge(gates, 1)
            act.activation(k.gbo[:, :], k.bo[:, :], ACT.Copy, scale=k.gate[:, 0:1])

        @block.vector
        def _(dve):
            dve.wait_ge(in_ctx, 16)
            dve.tensor_copy(k.ctxT[0][:, :], k.raw_q[:, 0:CH * BATCH * CTX]).then_inc(ctx_hi, 1)
            dve.memset(k.ones_f[:, :], 1.0).then_inc(ones_set, 1)
            dve.wait_ge(ones_set, 1)
            dve.tensor_copy(k.ones[:, :], k.ones_f[:, :])
            dve.wait_ge(in_small, 48)
            dve.scalar_tensor_tensor(out=k.qkw[:, :], in0=k.normw[:, 0:1], scalar=float(HD) ** 0.5, in1=k.normw[:, 1:2],
                                     op0=ALU.mult, op1=ALU.mult)
            dve.wait_ge(ctx_lo, 1)


def ln_phase(nc, k, count, add_bo=False):
    stats, mv, ms, rstd, xn_ready, tr_full, xn_hi, tr_free, bo_added = k.ln_sems
    N, M = NT * count, count
    with nc.Block() as block:
        def lo(dve, t):
            dve.wait_ge(xn_hi, N + t + 1)
            dve.tensor_tensor(k.xnT[1][:, :, t * PART:(t + 1) * PART],
                              k.bank[t % 4][:, :].rearrange("p (c q) -> p c q", c=CH),
                              f(k.xnT[0][:, :, t * PART:(t + 1) * PART]), ALU.subtract).then_inc(tr_free, 1)

        @block.vector
        def _(dve):
            for t in range(NT):
                dve.bn_stats(k.ln_st[:, t, :], k.x[:, t, :]).then_inc(stats, 1)
            for t in range(NT):
                dve.wait_ge(stats, N + t + 1)
                dve.bn_aggr(k.ln_mv[:, t, :], k.ln_st[:, t, :]).then_inc(mv, 1)
            for t in range(NT):
                if t == 0:
                    dve.wait_ge(rstd, M + 1)
                if t >= 4:
                    dve.wait_ge(tr_full, N + t - 3)
                dve.tensor_scalar(k.xn_tok[:, t % 4, :], k.x[:, t, :], k.ln_mv[:, t, 0:1], k.ln_rs[:, t:t + 1],
                                  ALU.subtract, ALU.mult).then_inc(xn_ready, 1)
                if t >= 2:
                    lo(dve, t - 2)
            lo(dve, NT - 2)
            lo(dve, NT - 1)

        @block.gpsimd
        def _(pool):
            pool.wait_ge(mv, N + NT)
            pool.tensor_scalar(k.ln_rs[:, :], k.ln_mv[:, :, 1], LN_EPS, None, ALU.add).then_inc(ms, 1)
            pool.wait_ge(ms, M + 1)
            pool.tensor_tensor(k.ln_rs[:, :], k.ln_rs[:, :], k.minus_half[:, 0:NT], ALU.pow).then_inc(rstd, 1)
            if add_bo:
                for t in range(NT):
                    pool.wait_ge(xn_ready, N + t + 1)
                    pool.tensor_tensor(k.x[:, t, :], k.x[:, t, :], k.gbo[:, :], ALU.add).then_inc(bo_added, 1)
                pool.wait_ge(bo_added, NT)

        @block.tensor
        def _(pe):
            for t in range(NT):
                pe.wait_ge(xn_ready, N + t + 1)
                if t >= 4:
                    pe.wait_ge(tr_free, N + t - 3)
                for c in range(CH):
                    last = pe.transpose(k.bank[t % 4][:, c * PART:(c + 1) * PART],
                                        k.xn_tok[:, t % 4, c * PART:(c + 1) * PART], k.ident[:, :])
                last.then_inc(tr_full, 1)

        @block.scalar
        def _(act):
            for t in range(NT):
                act.wait_ge(tr_full, N + t + 1)
                act.activation(k.xnT[0][:, :, t * PART:(t + 1) * PART],
                               k.bank[t % 4][:, :].rearrange("p (c q) -> p c q", c=CH),
                               ACT.Copy).then_inc(xn_hi, 1)
            act.wait_ge(tr_free, N + NT)


def attn0_phase(nc, k, sem):
    q_in, o_in, kv_in = sem("a0_q_in"), sem("a0_o_in"), sem("a0_kv_in")
    kv_hi, q_hi, o_hi = sem("a0_kv_hi"), sem("a0_q_hi"), sem("a0_o_hi")
    kv_lo, q_lo, o_lo = sem("a0_kv_lo"), sem("a0_q_lo"), sem("a0_o_lo")
    bqr_hi, bqr_lo = sem("a0_bqr_hi"), sem("a0_bqr_lo")
    prep_full, prep_hi, prep_free = sem("a0_prep_full"), sem("a0_prep_hi"), sem("a0_prep_free")
    s_full, s_max, s_sub, p_exp = sem("a0_s_full"), sem("a0_s_max"), sem("a0_s_sub"), sem("a0_p_exp")
    p_sum, p_rec, p_ready = sem("a0_p_sum"), sem("a0_p_rec"), sem("a0_p_ready")
    pt_full, pt_hi, pt_lo = sem("a0_pt_full"), sem("a0_pt_hi"), sem("a0_pt_lo")
    o_full, x_done = sem("a0_o_full"), sem("a0_x_done")
    bias_in, bqk_zero = sem("a0_bias_in"), sem("a0_bqk_zero")

    FIRST = 0
    FILLS, WK0, BQ, VW0, KV = 18, 0, 8, 9, 17
    CONV = {"kv": 2, "q": 4, "o": 4}
    KVW = CH * 2 * HD

    wq, wo, wkv = k.w_q, k.w_o, k.w_kv
    wq4 = [w[:, :].rearrange("p (h c) -> p h c", h=GH) for w in wq]
    wo4 = [w[:, :].rearrange("p (h c) -> p h c", h=GH) for w in wo]
    wkv4 = [w[:, :].rearrange("p (c n) -> p c n", c=CH) for w in wkv]
    ctx4 = [w[:, :].rearrange("p (c n) -> p c n", c=CH) for w in k.ctxT]
    prep = [k.bank[n] for n in range(3)]
    s_bank, o_bank, pt_bank = [k.bank[3], k.bank[4]], [k.bank[6], k.bank[7]], k.bank[5]

    def s_view(bank):
        return bank[:, 0:GH * CTX]

    def heads(ap):
        return ap.rearrange("p (h n) -> p h n", h=GH)

    with nc.Block() as block:
        def ring(n):
            return prep[n % 3]

        def wk_view(w, c, hp):
            return w[:, c, :, 2 * hp:2 * hp + 2, :].rearrange("p b h k -> p h b k")

        def wk_bank(bank):
            return bank[:, :].rearrange("p (h b k) -> p h b k", h=2, b=BATCH)

        def bq_bank(bank, h):
            return bank[32 * h:32 * h + 1, 0:BATCH * CTX].rearrange("p (b k) -> p b k", b=BATCH)

        @block.sync
        def _(sp):
            sp.dma_start(k.raw_kv[:, :], k.d["w0kv"][0:PART, :]).then_inc(kv_in, 16)
            sp.dma_start(k.raw_q[:, :], k.d["w0q"][0:PART, :]).then_inc(q_in, 16)
            sp.dma_start(k.raw_o[:, :], k.d["w0o"][0:PART, :]).then_inc(o_in, 16)
            with sp.Fori(1, NKV) as g:
                sp.wait_ge(kv_lo, g * CONV["kv"])
                sp.dma_start(k.raw_kv[:, :], k.d["w0kv"][bass.ts(g, PART), :]).then_inc(kv_in, 16)
                sp.wait_ge(q_lo, g * CONV["q"])
                sp.dma_start(k.raw_q[:, :], k.d["w0q"][bass.ts(g, PART), :]).then_inc(q_in, 16)
                sp.wait_ge(o_lo, g * CONV["o"])
                sp.dma_start(k.raw_o[:, :], k.d["w0o"][bass.ts(g, PART), :]).then_inc(o_in, 16)

        @block.gpsimd
        def _(pool):
            def lo_piece(kind, g, i):
                raw, w, hi, lo, cols = {"kv": (k.raw_kv, wkv, kv_hi, kv_lo, KVW), "q": (k.raw_q, wq, q_hi, q_lo, GH * HID),
                                        "o": (k.raw_o, wo, o_hi, o_lo, GH * HID)}[kind]
                n = cols // CONV[kind]
                if i == 0:
                    pool.wait_ge(hi, g + 1)
                s = slice(i * n, (i + 1) * n)
                pool.tensor_tensor(w[1][:, s], raw[:, s], f(w[0][:, s]), ALU.subtract).then_inc(lo, 1)

            def bq_rows(g):
                pool.wait_ge(bqr_hi, g + 1)
                pool.tensor_tensor(heads(k.bq_rep[1][:, :]), k.bias[:, 0:GH].unsqueeze(2).to_broadcast([PART, GH, 32]),
                                   heads(f(k.bq_rep[0][:, :])), ALU.subtract).then_inc(bqr_lo, 1)

            def body(g, nxt):
                sched = {0: [("kv", 0), ("kv", 1)], 1: [("q", 0)], 2: [("q", 1)], 3: [("q", 2)], 4: [("q", 3)],
                         5: [("o", 0), ("o", 1)], 6: [("o", 2)], 7: [("o", 3)]}
                for t in range(NT):
                    pool.wait_ge(p_rec, NT * g + t + 1)
                    p = heads(k.p0[:, t % 4, :])
                    pool.tensor_tensor(p, p, k.rinv0[:, t % 4, :].unsqueeze(2).to_broadcast([PART, GH, CTX]),
                                       ALU.mult).then_inc(p_ready, 1)
                    if nxt:
                        for kind, i in sched[t]:
                            lo_piece(kind, g + 1, i)
                        if t == 0:
                            bq_rows(g + 1)

            pool.memset(f(k.bqk[:, :, :, :]), 0.0).then_inc(bqk_zero, 1)
            for kind in ("kv", "q", "o"):
                for i in range(CONV[kind]):
                    lo_piece(kind, 0, i)
                if kind == "kv":
                    bq_rows(0)
            body(0, True)
            with pool.Fori(1, NKV - 1) as g:
                body(g, True)
            body(NKV - 1, False)

        @block.vector
        def _(dve):
            def conv(kind, g):
                raw, w, arrived, hi = {"kv": (k.raw_kv, wkv, kv_in, kv_hi), "q": (k.raw_q, wq, q_in, q_hi),
                                       "o": (k.raw_o, wo, o_in, o_hi)}[kind]
                n = KVW if kind == "kv" else GH * HID
                dve.wait_ge(arrived, 16 * g + 16)
                if kind == "kv":
                    dve.tensor_copy(k.bias[:, :], raw[:, KVW:KVW + GH + 2]).then_inc(bias_in, 1)
                dve.tensor_copy(w[0][:, :], raw[:, 0:n]).then_inc(hi, 1)
                if kind == "kv":
                    dve.wait_ge(bias_in, g + 1)
                    dve.tensor_copy(heads(k.bq_rep[0][:, :]),
                                    k.bias[:, 0:GH].unsqueeze(2).to_broadcast([PART, GH, 32])).then_inc(bqr_hi, 1)

            def kv_lo_evac(n, g):
                dve.wait_ge(prep_hi, n + 1)
                bank = ring(KVRING)
                for j in range(2):
                    last = dve.scalar_tensor_tensor(
                        out=k.kvT[1][:, j, :], in0=bank[:, j * 256:(j + 1) * 256], scalar=k.bias[:, GH + j:GH + j + 1],
                        in1=f(k.kvT[0][:, j, :]), op0=ALU.add, op1=ALU.subtract)
                last.then_inc(prep_free, 1)

            def body(g, nxt):
                base = FILLS * g + 1
                for j in range(8):
                    c, hp = divmod(j, 2)
                    dve.wait_ge(prep_hi, base + WK0 + j + 1)
                    dve.tensor_tensor(wk_view(k.WK[1], c, hp), wk_bank(ring(1 + WK0 + j)), f(wk_view(k.WK[0], c, hp)),
                                      ALU.subtract).then_inc(prep_free, 1)
                dve.wait_ge(prep_hi, base + BQ + 1)
                for h in range(GH):
                    last = dve.tensor_tensor(k.bqk[32:33, :, h, :], bq_bank(ring(1 + BQ), h), f(k.bqk[0:1, :, h, :]),
                                             ALU.subtract)
                last.then_inc(prep_free, 1)
                for j in range(8):
                    h, pr = divmod(j, 2)
                    dve.wait_ge(prep_hi, base + VW0 + j + 1)
                    for bp in range(2):
                        r = slice(64 * (h % 2), 64 * (h % 2) + 64)
                        last = dve.tensor_tensor(k.VW[1][r, h // 2, 2 * pr + bp, :], ring(1 + VW0 + j)[64 * bp:64 * bp + 64, :],
                                                 f(k.VW[0][r, h // 2, 2 * pr + bp, :]), ALU.subtract)
                    last.then_inc(prep_free, 1)
                for s in range(NT + 3):
                    n = NT * g + s
                    if s < NT:
                        S = s_view(s_bank[s % 2])
                        dve.wait_ge(s_full, n + 1)
                        dve.tensor_reduce(k.mx0[:, s % 2, :], heads(S), AX.X, ALU.max).then_inc(s_max, 1)
                        dve.wait_ge(s_max, n + 1)
                        dve.tensor_tensor(heads(k.p0[:, s % 4, :]), heads(S),
                                          k.mx0[:, s % 2, :].unsqueeze(2).to_broadcast([PART, GH, CTX]),
                                          ALU.subtract).then_inc(s_sub, 1)
                    if 1 <= s <= NT:
                        dve.wait_ge(p_exp, n)
                        dve.tensor_reduce(k.sum0[:, s % 2, :], heads(k.p0[:, (s - 1) % 4, :]), AX.X, ALU.add)\
                           .then_inc(p_sum, 1)
                        dve.wait_ge(p_sum, n)
                        dve.reciprocal(k.rinv0[:, (s - 1) % 4, :], k.sum0[:, s % 2, :]).then_inc(p_rec, 1)
                    if s == NT and nxt:
                        kv_lo_evac(FILLS * (g + 1), g + 1)
                    if 2 <= s < NT + 2:
                        t = s - 2
                        dve.wait_ge(pt_hi, n - 1)
                        dve.tensor_tensor(k.pT0[1][:, t % 2, :], pt_bank[:, 0:256], f(k.pT0[0][:, t % 2, :]),
                                          ALU.subtract).then_inc(pt_lo, 1)
                    if s >= 3:
                        t = s - 3
                        dve.wait_ge(o_full, n - 2)
                        dve.scalar_tensor_tensor(out=k.x[:, t, :], in0=o_bank[t % 2][:, :], scalar=k.gate[:, 0:1],
                                                 in1=k.x[:, t, :], op0=ALU.mult, op1=ALU.add).then_inc(x_done, 1)
                    if nxt and s in (0, 1, 3):
                        conv({0: "kv", 1: "q", 3: "o"}[s], g + 1)

            dve.wait_ge(bqk_zero, 1)
            conv("kv", 0)
            kv_lo_evac(0, 0)
            conv("q", 0)
            conv("o", 0)
            body(0, True)
            with dve.Fori(1, NKV - 1) as g:
                body(g, True)
            body(NKV - 1, False)

        @block.scalar
        def _(act):
            def kv_evac(n):
                act.wait_ge(prep_full, n + 1)
                for j in range(2):
                    last = act.activation(k.kvT[0][:, j, :], ring(KVRING)[:, j * 256:(j + 1) * 256], ACT.Identity,
                                          bias=k.bias[:, GH + j:GH + j + 1])
                last.then_inc(prep_hi, 1)

            def body(g, nxt):
                base = FILLS * g + 1
                for j in range(8):
                    c, hp = divmod(j, 2)
                    act.wait_ge(prep_full, base + WK0 + j + 1)
                    act.activation(wk_view(k.WK[0], c, hp), wk_bank(ring(1 + WK0 + j)), ACT.Copy).then_inc(prep_hi, 1)
                act.wait_ge(prep_full, base + BQ + 1)
                for h in range(GH):
                    last = act.activation(k.bqk[0:1, :, h, :], bq_bank(ring(1 + BQ), h), ACT.Copy)
                last.then_inc(prep_hi, 1)
                for j in range(8):
                    h, pr = divmod(j, 2)
                    act.wait_ge(prep_full, base + VW0 + j + 1)
                    for bp in range(2):
                        r = slice(64 * (h % 2), 64 * (h % 2) + 64)
                        last = act.activation(k.VW[0][r, h // 2, 2 * pr + bp, :],
                                              ring(1 + VW0 + j)[64 * bp:64 * bp + 64, :], ACT.Copy)
                    last.then_inc(prep_hi, 1)
                for s in range(NT + 2):
                    n = NT * g + s
                    if s < NT:
                        act.wait_ge(s_sub, n + 1)
                        act.activation(k.p0[:, s % 4, :], k.p0[:, s % 4, :], ACT.Exp, scale=SCALE).then_inc(p_exp, 1)
                    if s == NT and nxt:
                        kv_evac(FILLS * (g + 1))
                    if s >= 2:
                        act.wait_ge(pt_full, n - 1)
                        act.activation(k.pT0[0][:, s % 2, :], pt_bank[:, 0:256], ACT.Copy).then_inc(pt_hi, 1)

            act.wait_ge(bqk_zero, 1)
            act.wait_ge(bias_in, 1)
            kv_evac(0)
            body(0, True)
            with act.Fori(1, NKV - 1) as g:
                body(g, True)
            body(NKV - 1, False)

        @block.tensor
        def _(pe):
            def room(n, always=False):
                pe.wait_ge(prep_free, n - 2)

            def kv_proj(n, g, first=False):
                if not first:
                    room(n)
                pe.wait_ge(kv_lo, CONV["kv"] * (g + 1))
                for j in range(2):
                    for c in range(CH):
                        cols = slice(j * HD, (j + 1) * HD)
                        last = mm3(pe, ring(KVRING)[:, j * 256:(j + 1) * 256], [w[:, c, cols] for w in wkv4],
                                   [w[:, c, :] for w in ctx4], c == 0, c == CH - 1)
                last.then_inc(prep_full, 1)

            def body(g, nxt):
                base = FILLS * g + 1
                pe.wait_ge(prep_free, base)
                pe.wait_ge(q_lo, CONV["q"] * (g + 1))
                for j in range(8):
                    c, hp = divmod(j, 2)
                    room(base + WK0 + j) if j >= 2 else None
                    for h in range(2):
                        last = mm3(pe, ring(1 + WK0 + j)[:, h * 256:(h + 1) * 256],
                                   [w[:, 2 * hp + h, c * PART:(c + 1) * PART] for w in wq4],
                                   [w[:, 0, :] for w in k.kvT], True, True)
                    last.then_inc(prep_full, 1)
                room(base + BQ)
                pe.wait_ge(bqr_lo, g + 1)
                mm3(pe, ring(1 + BQ)[:, 0:256], [w[:, :] for w in k.bq_rep], [w[:, 0, :] for w in k.kvT],
                    True, True).then_inc(prep_full, 1)
                pe.wait_ge(o_lo, CONV["o"] * (g + 1))
                for j in range(8):
                    h, pr = divmod(j, 2)
                    room(base + VW0 + j)
                    mm3(pe, ring(1 + VW0 + j)[:, :], [w[:, 1, pr * PART:(pr + 1) * PART] for w in k.kvT],
                        [w[:, h, :] for w in wo4], True, True).then_inc(prep_full, 1)
                for s in range(NT + 3):
                    n = NT * g + s
                    if s < NT:
                        if s == 0:
                            pe.wait_ge(prep_free, base + BQ + 1)
                            if g is not FIRST:
                                pe.wait_ge(s_sub, n)
                        elif s >= 2:
                            pe.wait_ge(s_sub, n - 1)
                        S, b = s_view(s_bank[s % 2]), s // 2
                        for c in range(CH):
                            mm3(pe, S, [w[:, c, s * PART:(s + 1) * PART] for w in k.xnT],
                                [w[:, c, b, :, :] for w in k.WK], c == 0, False)
                        pe.matmul(S, k.ones[:, :], k.bqk[:, b, :, :], start=False, stop=True).then_inc(s_full, 1)
                    if s == NT and nxt:
                        kv_proj(FILLS * (g + 1), g + 1)
                    if 2 <= s < NT + 2:
                        t = s - 2
                        pe.wait_ge(p_ready, n - 1)
                        if not (g is FIRST and t == 0):
                            pe.wait_ge(pt_lo, n - 2)
                        for hp in range(2):
                            last = pe.transpose(pt_bank[:, hp * PART:(hp + 1) * PART],
                                                k.p0[:, t % 4, hp * PART:(hp + 1) * PART], k.ident[:, :])
                        last.then_inc(pt_full, 1)
                    if s >= 3:
                        t = s - 3
                        pe.wait_ge(pt_lo, n - 2)
                        if s == 3:
                            pe.wait_ge(prep_free, base + VW0 + 8)
                            if g is not FIRST:
                                pe.wait_ge(x_done, NT * g)
                        elif t >= 2:
                            pe.wait_ge(x_done, n - 4)
                        for hp in range(2):
                            last = mm3(pe, o_bank[t % 2][:, :], [w[:, t % 2, hp * PART:(hp + 1) * PART] for w in k.pT0],
                                       [w[:, hp, t // 2, :] for w in k.VW], hp == 0, hp == 1)
                        last.then_inc(o_full, 1)

            kv_proj(0, 0, first=True)
            body(0, True)
            with pe.Fori(1, NKV - 1) as g:
                body(g, True)
            body(NKV - 1, False)



def ffn0_buffers(k, scope, sb, pair):
    k.raw_gu1 = sb(scope, "raw_gu1", [CH * 2 * PART])
    k.w_gu = [pair(scope, f"w_gu{n}", [CH * 2 * PART]) for n in range(2)]
    k.w_dn = pair(scope, "w_dn", [IC, HID])
    k.hT = pair(scope, "hT", [IC, 512])
    k.f_tanh, k.f_a, k.f_h = (sb(scope, n, [2, 512]) for n in ("f_tanh", "f_a", "f_h"))


def ffn0_phase(nc, k, sem):
    gu_in = [sem(f"f0_gu_in{n}") for n in range(2)]
    gu_whi, gu_wlo = sem("f0_gu_whi"), sem("f0_gu_wlo")
    dn_in = [sem(f"f0_dn_in{n}") for n in range(3)]
    dn_hi, dn_lo = sem("f0_dn_hi"), sem("f0_dn_lo")
    gu_full, tanh_done, a_done, h_done = sem("f0_gu_full"), sem("f0_tanh"), sem("f0_a"), sem("f0_h")
    h_hi, h_lo, o_full, x_done = sem("f0_h_hi"), sem("f0_h_lo"), sem("f0_o_full"), sem("f0_x_done")
    STEPS = [(half, i) for half in range(2) for i in range(IC)]
    raws = [k.raw_kv, k.raw_gu1]
    DN = [(k.raw_q, 0, 4), (k.raw_o, 4, 8), (k.raw_q, 8, 11)]
    gate_bank, up_bank, o_bank = [k.bank[0], k.bank[2]], [k.bank[1], k.bank[3]], k.bank[4:8]

    def width(i):
        return ILAST if i == IC - 1 else PART

    def dn_slices(i0, i1):
        full = min(i1, IC - 1) - i0
        out = [(slice(0, PART), i0, full)]
        if i1 == IC:
            out.append((slice(0, ILAST), IC - 1, 1))
        return out

    with nc.Block() as block:
        @block.sync
        def _(sp):
            def gu(n):
                _, i = STEPS[n]
                w = CH * 2 * width(i)
                if n >= 2:
                    sp.wait_ge(gu_wlo, n - 1)
                sp.dma_start(raws[n % 2][:, 0:w], k.d["w_gu"][:, i * 1024:i * 1024 + w]).then_inc(gu_in[n % 2], 16)

            gu(0)
            gu(1)
            for j, (raw, i0, i1) in enumerate(DN):
                if j == 2:
                    sp.wait_ge(dn_lo, 1)
                for rows, i, n in dn_slices(i0, i1):
                    src = k.d["w_down"][i * PART:i * PART + rows.stop * n, :].rearrange("(n p) c -> p n c", n=n)
                    dst = raw[rows, (i - i0) * HID:(i - i0 + n) * HID].rearrange("p (n c) -> p n c", n=n)
                    sp.dma_start(dst, src).then_inc(dn_in[j], 16)
                gu(2 + j)
            for n in range(5, len(STEPS)):
                gu(n)

        @block.gpsimd
        def _(pool):
            def w_lo(n):
                w = CH * 2 * width(STEPS[n][1])
                pool.wait_ge(gu_whi, n + 1)
                pool.tensor_tensor(k.w_gu[n % 2][1][:, 0:w], raws[n % 2][:, 0:w], f(k.w_gu[n % 2][0][:, 0:w]),
                                   ALU.subtract).then_inc(gu_wlo, 1)

            def dn(j):
                raw, i0, i1 = DN[j]
                pool.wait_ge(dn_hi, j + 1)
                for rows, i, n in dn_slices(i0, i1):
                    last = pool.tensor_tensor(k.w_dn[1][rows, i:i + n, :],
                                              raw[rows, (i - i0) * HID:(i - i0 + n) * HID].rearrange("p (n c) -> p n c", n=n),
                                              f(k.w_dn[0][rows, i:i + n, :]), ALU.subtract)
                last.then_inc(dn_lo, 1)

            w_lo(0)
            for n, (half, i) in enumerate(STEPS):
                if n + 1 < len(STEPS):
                    w_lo(n + 1)
                if n in (1, 3, 5):
                    dn(n // 2)
                p = slice(0, width(i))
                pool.wait_ge(h_hi, n + 1)
                pool.tensor_tensor(k.hT[1][p, i, :], k.f_h[p, n % 2, :], f(k.hT[0][p, i, :]), ALU.subtract).then_inc(h_lo, 1)

        @block.vector
        def _(dve):
            def w_hi(n):
                w = CH * 2 * width(STEPS[n][1])
                dve.wait_ge(gu_in[n % 2], 16 * (n // 2 + 1))
                if n >= 2:
                    dve.wait_ge(gu_full, n - 1)
                dve.tensor_copy(k.w_gu[n % 2][0][:, 0:w], raws[n % 2][:, 0:w]).then_inc(gu_whi, 1)

            def dn(j):
                raw, i0, i1 = DN[j]
                dve.wait_ge(dn_in[j], 16 * len(dn_slices(i0, i1)))
                for rows, i, n in dn_slices(i0, i1):
                    last = dve.tensor_copy(k.w_dn[0][rows, i:i + n, :],
                                           raw[rows, (i - i0) * HID:(i - i0 + n) * HID].rearrange("p (n c) -> p n c", n=n))
                last.then_inc(dn_hi, 1)

            w_hi(0)
            for n, (half, i) in enumerate(STEPS):
                if n + 1 < len(STEPS):
                    w_hi(n + 1)
                if n in (1, 3, 5):
                    dn(n // 2)
                p, s = slice(0, width(i)), n % 2
                dve.wait_ge(tanh_done, n + 1)
                dve.scalar_tensor_tensor(out=k.f_a[p, s, :], in0=k.f_tanh[p, s, :], scalar=1.0, in1=gate_bank[s][p, :],
                                         op0=ALU.add, op1=ALU.mult).then_inc(a_done, 1)
                dve.wait_ge(a_done, n + 1)
                if n >= 2:
                    dve.wait_ge(h_lo, n - 1)
                dve.scalar_tensor_tensor(out=k.f_h[p, s, :], in0=k.f_a[p, s, :], scalar=0.5, in1=up_bank[s][p, :],
                                         op0=ALU.mult, op1=ALU.mult).then_inc(h_done, 1)
                if i == IC - 1:
                    for j in range(4):
                        dve.wait_ge(o_full, 4 * half + j + 1)
                        t = 4 * half + j
                        dve.scalar_tensor_tensor(out=k.x[:, t, :], in0=o_bank[j][:, :], scalar=k.gate[:, 2:3],
                                                 in1=k.x[:, t, :], op0=ALU.mult, op1=ALU.add).then_inc(x_done, 1)
            dve.wait_ge(x_done, 8)

        @block.scalar
        def _(act):
            def hi(n):
                half, i = STEPS[n]
                p = slice(0, width(i))
                act.wait_ge(h_done, n + 1)
                act.activation(k.hT[0][p, i, :], k.f_h[p, n % 2, :], ACT.Copy).then_inc(h_hi, 1)

            for n, (half, i) in enumerate(STEPS):
                p = slice(0, width(i))
                act.wait_ge(gu_full, n + 1)
                act.activation(k.f_tanh[p, n % 2, :], gate_bank[n % 2][p, :], ACT.Tanh, scale=0.5).then_inc(tanh_done, 1)
                if i >= 1:
                    hi(n - 1)
                if i == IC - 1:
                    hi(n)

        @block.tensor
        def _(pe):
            for n, (half, i) in enumerate(STEPS):
                w, s = width(i), n % 2
                pe.wait_ge(gu_wlo, n + 1)
                if n >= 2:
                    pe.wait_ge(h_done, n - 1)
                wg = [v[:, 0:CH * 2 * w].rearrange("p (c n) -> p c n", c=CH) for v in k.w_gu[s]]
                for j, bank in enumerate((gate_bank[s], up_bank[s])):
                    for c in range(CH):
                        last = mm3(pe, bank[0:w, :], [v[:, c, j * w:(j + 1) * w] for v in wg],
                                   [v[:, c, half * 512:(half + 1) * 512] for v in k.xnT], c == 0, c == CH - 1)
                last.then_inc(gu_full, 1)
                if i == IC - 1:
                    if half == 0:
                        pe.wait_ge(dn_lo, len(DN))
                    for j in range(4):
                        if half == 1:
                            pe.wait_ge(x_done, j + 1)
                        for m in range(IC):
                            p = slice(0, width(m))
                            if j == 0:
                                pe.wait_ge(h_lo, IC * half + m + 1)
                            last = mm3(pe, o_bank[j][:, :], [v[p, m, j * PART:(j + 1) * PART] for v in k.hT],
                                       [v[p, m, :] for v in k.w_dn], m == 0, m == IC - 1)
                        last.then_inc(o_full, 1)


def attn1_buffers(k, scope, sb, pair):
    k.w_q, k.w_kv, k.w_o = pair(scope, "w1q", [CH, GH * HD]), pair(scope, "w1kv", [CH, 2 * HD]), pair(scope, "w1o", [GH, HID])
    k.qT = pair(scope, "qT1", [2, GH, PART])
    k.kT = pair(scope, "kT1", [BATCH, SEQ + CTX])
    k.v = pair(scope, "v1", [BATCH, 3, HD])
    k.pT = pair(scope, "pT1", [3, GH, SEQ])
    k.oT = pair(scope, "oT1", [GH, SEQ])
    k.q_raw, k.k_raw = sb(scope, "q_raw", [2, GH * HD]), sb(scope, "k_raw", [3, HD])
    k.p1 = sb(scope, "p1", [2, GH, SEQ + CTX])
    k.dump, k.rms_eps = sb(scope, "dump", [2 * GH + 3, HD]), sb(scope, "rms_eps", [2 * GH])
    k.ssk, k.rk = sb(scope, "ssk", [3]), sb(scope, "rk", [3])
    k.ssq, k.rq, k.mx, k.nb, k.rs, k.rinv = (sb(scope, n, [2 * GH]) for n in ("ssq", "rq", "mx", "nb", "rs", "rinv"))


def attn1_phase(nc, k, sem):
    def sems(*names):
        return [sem("a1_" + n) for n in names]

    q_in, kv_in, o_in, q_whi, kv_whi, o_whi, q_wlo, kv_wlo, o_wlo = sems(
        "q_in", "kv_in", "o_in", "q_whi", "kv_whi", "o_whi", "q_wlo", "kv_wlo", "o_wlo")
    kv_full, kv_hi, kv_split, cx_full, cx_hi, cx_split = sems("kv_full", "kv_hi", "kv_split", "cx_full", "cx_hi", "cx_split")
    q_full, q_copied, pv_full, pv_hi, pv_split, d_full, x_added = sems(
        "q_full", "q_copied", "pv_full", "pv_hi", "pv_split", "d_full", "x_added")
    t_full, t_hi, t_split, kt_full, kt_hi, kt_split, qt_full, qt_hi, qt_split = sems(
        "t_full", "t_hi", "t_split", "kt_full", "kt_hi", "kt_split", "qt_full", "qt_hi", "qt_split")
    ssk_ready, rk_ms, rk_ready, k_scaled, ssq_ready, rq_ms, rq_ready = sems(
        "ssk", "rk_ms", "rk", "k_scaled", "ssq", "rq_ms", "rq")
    s_full, mx_ready, nb_ready, exp_done, rinv_ready, p_scaled, pad_zero = sems(
        "s_full", "mx", "nb", "exp", "rinv", "p_scaled", "pad_zero")

    CONV = {"kv": 2, "q": 4, "o": 4}
    KEYS = SEQ + CTX
    bx, by = k.bank[4:6], k.bank[6:8]
    PAIRS = [(0, 0), (1, 0), (0, 1), (1, 1)]
    ctx4 = [w[:, :].rearrange("p (c n) -> p c n", c=CH) for w in k.ctxT]
    flat = {"kv": [w[:, :, :].rearrange("p a b -> p (a b)") for w in k.w_kv],
            "q": [w[:, :, :].rearrange("p a b -> p (a b)") for w in k.w_q],
            "o": [w[:, :, :].rearrange("p a b -> p (a b)") for w in k.w_o]}
    cols = {"kv": CH * 2 * HD, "q": CH * GH * HD, "o": GH * HID}
    raw = {"kv": k.raw_kv, "q": k.raw_q, "o": k.raw_o}
    arrived = {"kv": kv_in, "q": q_in, "o": o_in}
    whi, wlo = {"kv": kv_whi, "q": q_whi, "o": o_whi}, {"kv": kv_wlo, "q": q_wlo, "o": o_wlo}

    def y_start(b):
        return (0, 8, 15, 23)[b]

    def y_bank(b, kind, j=0):
        order = ["kv"] + (["cx"] if b % 2 == 0 else []) + ["q0", "q1", "pv0", "pv1", "d0", "d1"]
        name = kind if kind in ("kv", "cx") else f"{kind}{j}"
        return by[(y_start(b) + order.index(name)) % 2]

    def x_bank(b, kind, j=0):
        at = {"t": j, "k": 6, "q": 7 + j}[kind]
        return bx[(9 * b + at) % 2]

    def s_pair(j):
        return k.psum[:, (j % 2) * 1024:(j % 2) * 1024 + 1024].rearrange("p (h n) -> p h n", h=2)[:, :, 0:KEYS]

    def stat(j):
        tile, hp = PAIRS[j]
        return slice(tile * GH + 2 * hp, tile * GH + 2 * hp + 2)

    def loop(eng, body, tail):
        body(0, True, True)
        with eng.Fori(1, NKV - 1) as g:
            body(g, False, True)
        body(NKV - 1, False, False)
        tail(NKV * BATCH)

    with nc.Block() as block:
        @block.sync
        def _(sp):
            for kind, src in (("kv", "w1kv"), ("q", "w1q"), ("o", "w1o")):
                sp.dma_start(raw[kind][:, 0:cols[kind]], k.d[src][0:PART, :]).then_inc(arrived[kind], 16)
            with sp.Fori(1, NKV) as g:
                for kind, src in (("o", "w1o"), ("kv", "w1kv"), ("q", "w1q")):
                    sp.wait_ge(wlo[kind], g * CONV[kind])
                    sp.dma_start(raw[kind][:, 0:cols[kind]], k.d[src][bass.ts(g, PART), :]).then_inc(arrived[kind], 16)

        @block.gpsimd
        def _(pool):
            def w_lo(kind, g):
                n = cols[kind] // CONV[kind]
                pool.wait_ge(whi[kind], g + 1)
                for i in range(CONV[kind]):
                    s = slice(i * n, (i + 1) * n)
                    pool.tensor_tensor(flat[kind][1][:, s], raw[kind][:, s], f(flat[kind][0][:, s]),
                                       ALU.subtract).then_inc(wlo[kind], 1)

            def body(g, first, nxt):
                for b in range(BATCH):
                    n = BATCH * g + b
                    pool.wait_ge(ssk_ready, n + 1)
                    pool.tensor_tensor(k.rk[:, :], k.ssk[:, :], k.rms_eps[:, 0:3], ALU.add).then_inc(rk_ms, 1)
                    pool.wait_ge(rk_ms, n + 1)
                    pool.tensor_tensor(k.rk[:, :], k.rk[:, :], k.minus_half[:, 0:3], ALU.pow).then_inc(rk_ready, 1)
                    pool.wait_ge(ssq_ready, n + 1)
                    pool.tensor_tensor(k.rq[:, :], k.ssq[:, :], k.rms_eps[:, :], ALU.add).then_inc(rq_ms, 1)
                    pool.wait_ge(rq_ms, n + 1)
                    pool.tensor_tensor(k.rq[:, :], k.rq[:, :], k.minus_half[:, 0:8], ALU.pow).then_inc(rq_ready, 1)
                    if b == 0:
                        w_lo("o", g)
                    if b == BATCH - 1 and nxt:
                        w_lo("kv", g + 1)
                        w_lo("q", g + 1)

            pool.memset(f(k.v[0][64:PART, :, 2, :]), 0.0)
            pool.memset(f(k.v[1][64:PART, :, 2, :]), 0.0)
            pool.memset(f(k.pT[0][64:PART, 2, :, :]), 0.0)
            pool.memset(f(k.pT[1][64:PART, 2, :, :]), 0.0).then_inc(pad_zero, 1)
            pool.wait_ge(pad_zero, 1)
            pool.memset(k.rms_eps[:, :], HD * RMS_EPS)
            pool.memset(k.ssk[:, :], 1.0).then_inc(pad_zero, 1)
            w_lo("kv", 0)
            w_lo("q", 0)
            loop(pool, body, lambda n: None)

        @block.vector
        def _(dve):
            def w_hi(kind, g):
                dve.wait_ge(arrived[kind], 16 * g + 16)
                dve.tensor_copy(flat[kind][0][:, :], raw[kind][:, 0:cols[kind]]).then_inc(whi[kind], 1)

            def t_lo(n, b, j):
                hp, kt = divmod(j, 3)
                p = slice(0, 64 if kt == 2 else PART)
                dve.wait_ge(t_hi, 6 * (n - 1) + j + 1)
                dve.tensor_tensor(k.pT[1][p, kt, 2 * hp:2 * hp + 2, :],
                                  x_bank(b, "t", j)[p, :].rearrange("p (h q) -> p h q", h=2),
                                  f(k.pT[0][p, kt, 2 * hp:2 * hp + 2, :]), ALU.subtract).then_inc(t_split, 1)

            def pv_lo(n, b, hp):
                dve.wait_ge(pv_hi, 2 * (n - 1) + hp + 1)
                dve.tensor_tensor(k.oT[1][:, 2 * hp:2 * hp + 2, :],
                                  y_bank(b, "pv", hp)[:, :].rearrange("p (h q) -> p h q", h=2),
                                  f(k.oT[0][:, 2 * hp:2 * hp + 2, :]), ALU.subtract).then_inc(pv_split, 1)

            def x_add(n, b, j):
                t = 2 * ((b - 1) % BATCH) + j
                dve.wait_ge(d_full, 2 * (n - 1) + j + 1)
                dve.scalar_tensor_tensor(out=k.x[:, t, :], in0=y_bank(b, "d", j)[:, :], scalar=k.gate[:, 1:2],
                                         in1=k.x[:, t, :], op0=ALU.mult, op1=ALU.add).then_inc(x_added, 1)

            def q_squares(n, b, tile):
                dve.wait_ge(q_copied, 2 * n + tile + 1)
                for h in range(GH):
                    q = k.q_raw[:, tile, h * HD:(h + 1) * HD]
                    last = dve.tensor_tensor_reduce(k.dump[:, tile * GH + h, :], q, q, 1.0, 0.0, ALU.mult, ALU.add,
                                                    k.ssq[:, tile * GH + h:tile * GH + h + 1])
                if tile == 1:
                    last.then_inc(ssq_ready, 1)

            def row_max(n, j):
                dve.wait_ge(s_full, 4 * n + j + 1)
                dve.tensor_reduce(k.mx[:, stat(j)], s_pair(j), AX.X, ALU.max).then_inc(mx_ready, 1)
                if j == 0:
                    dve.wait_ge(rq_ready, n + 1)
                dve.wait_ge(mx_ready, 4 * n + j + 1)
                dve.scalar_tensor_tensor(out=k.nb[:, stat(j)], in0=k.mx[:, stat(j)], scalar=-1.0, in1=k.rq[:, stat(j)],
                                         op0=ALU.mult, op1=ALU.mult).then_inc(nb_ready, 1)

            def scale_p(n, j):
                tile, hp = PAIRS[j]
                dve.wait_ge(exp_done, 4 * n + j + 1)
                dve.reciprocal(k.rinv[:, stat(j)], k.rs[:, stat(j)]).then_inc(rinv_ready, 1)
                dve.wait_ge(rinv_ready, 4 * n + j + 1)
                for h in (2 * hp, 2 * hp + 1):
                    last = dve.tensor_scalar(k.p1[:, tile, h, :], k.p1[:, tile, h, :],
                                             k.rinv[:, tile * GH + h:tile * GH + h + 1], None, ALU.mult)
                last.then_inc(p_scaled, 1)

            def body(g, first, nxt):
                for b in range(BATCH):
                    n, prev = BATCH * g + b, not (first and b == 0)
                    dve.wait_ge(kv_hi, n + 1)
                    bank = y_bank(b, "kv")[:, :].rearrange("p (t n) -> p t n", t=2)
                    dve.tensor_tensor(k.v[1][:, b, 0:2, :], bank[:, :, HD:2 * HD], f(k.v[0][:, b, 0:2, :]),
                                      ALU.subtract).then_inc(kv_split, 1)
                    if b % 2 == 0:
                        dve.wait_ge(cx_hi, 2 * g + b // 2 + 1)
                        for i in range(2):
                            last = dve.tensor_tensor(k.v[1][0:64, b + i, 2, :],
                                                     y_bank(b, "cx")[64 * i:64 * i + 64, HD:2 * HD],
                                                     f(k.v[0][0:64, b + i, 2, :]), ALU.subtract)
                        last.then_inc(cx_split, 1)
                    nk = 3 if b % 2 == 0 else 2
                    for i in range(nk):
                        last = dve.tensor_tensor_reduce(k.dump[:, 2 * GH + i, :], k.k_raw[:, i, :], k.k_raw[:, i, :], 1.0, 0.0,
                                                        ALU.mult, ALU.add, k.ssk[:, i:i + 1])
                    last.then_inc(ssk_ready, 1)
                    if prev:
                        t_lo(n, b, 0)
                        t_lo(n, b, 1)
                    dve.wait_ge(rk_ready, n + 1)
                    for i in range(nk):
                        last = dve.tensor_scalar(k.k_raw[:, i, :], k.k_raw[:, i, :], k.rk[:, i:i + 1], None, ALU.mult)
                    last.then_inc(k_scaled, 1)
                    q_squares(n, b, 0)
                    if prev:
                        t_lo(n, b, 2)
                        t_lo(n, b, 3)
                    q_squares(n, b, 1)
                    if b == BATCH - 1 and nxt:
                        w_hi("kv", g + 1)
                        w_hi("q", g + 1)
                    if prev:
                        t_lo(n, b, 4)
                        t_lo(n, b, 5)
                    dve.wait_ge(kt_hi, n + 1)
                    bank = x_bank(b, "k")
                    last = dve.scalar_tensor_tensor(out=k.kT[1][:, b, 0:SEQ], in0=bank[:, 0:SEQ], scalar=k.qkw[:, 0:1],
                                                    in1=f(k.kT[0][:, b, 0:SEQ]), op0=ALU.mult, op1=ALU.subtract)
                    if b % 2 == 0:
                        last = dve.scalar_tensor_tensor(
                            out=k.kT[1][:, b:b + 2, SEQ:KEYS], in0=bank[:, SEQ:SEQ + 128].rearrange("p (b k) -> p b k", b=2),
                            scalar=k.qkw[:, 0:1], in1=f(k.kT[0][:, b:b + 2, SEQ:KEYS]), op0=ALU.mult, op1=ALU.subtract)
                    last.then_inc(kt_split, 1)
                    for tile in range(2):
                        dve.wait_ge(qt_hi, 2 * n + tile + 1)
                        dve.tensor_tensor(k.qT[1][:, tile, :, :],
                                          x_bank(b, "q", tile)[:, :].rearrange("p (h q) -> p h q", h=GH),
                                          f(k.qT[0][:, tile, :, :]), ALU.subtract).then_inc(qt_split, 1)
                        if prev:
                            pv_lo(n, b, tile)
                    row_max(n, 0)
                    row_max(n, 1)
                    scale_p(n, 0)
                    if prev:
                        x_add(n, b, 0)
                    row_max(n, 2)
                    scale_p(n, 1)
                    if prev:
                        x_add(n, b, 1)
                    row_max(n, 3)
                    scale_p(n, 2)
                    scale_p(n, 3)
                    if b == 0:
                        w_hi("o", g)

            def tail(n):
                for j in range(6):
                    t_lo(n, 0, j)
                for hp in range(2):
                    pv_lo(n, 0, hp)
                for j in range(2):
                    x_add(n, 0, j)
                dve.wait_ge(x_added, 2 * n)

            dve.wait_ge(pad_zero, 2)
            w_hi("kv", 0)
            w_hi("q", 0)
            loop(dve, body, tail)

        @block.scalar
        def _(act):
            def t_evac(n, b, j):
                hp, kt = divmod(j, 3)
                p = slice(0, 64 if kt == 2 else PART)
                act.wait_ge(t_full, 6 * (n - 1) + j + 1)
                act.activation(k.pT[0][p, kt, 2 * hp:2 * hp + 2, :],
                               x_bank(b, "t", j)[p, :].rearrange("p (h q) -> p h q", h=2), ACT.Copy).then_inc(t_hi, 1)

            def pv_evac(n, b, hp):
                act.wait_ge(pv_full, 2 * (n - 1) + hp + 1)
                act.activation(k.oT[0][:, 2 * hp:2 * hp + 2, :],
                               y_bank(b, "pv", hp)[:, :].rearrange("p (h q) -> p h q", h=2), ACT.Copy).then_inc(pv_hi, 1)

            def body(g, first, nxt):
                for b in range(BATCH):
                    n, prev = BATCH * g + b, not (first and b == 0)
                    act.wait_ge(kv_full, n + 1)
                    bank = y_bank(b, "kv")[:, :].rearrange("p (t n) -> p t n", t=2)
                    act.activation(k.k_raw[:, 0:2, :], bank[:, :, 0:HD], ACT.Copy)
                    act.activation(k.v[0][:, b, 0:2, :], bank[:, :, HD:2 * HD], ACT.Copy).then_inc(kv_hi, 1)
                    if b % 2 == 0:
                        act.wait_ge(cx_full, 2 * g + b // 2 + 1)
                        act.activation(k.k_raw[:, 2, :], y_bank(b, "cx")[:, 0:HD], ACT.Copy)
                        for i in range(2):
                            last = act.activation(k.v[0][0:64, b + i, 2, :],
                                                  y_bank(b, "cx")[64 * i:64 * i + 64, HD:2 * HD], ACT.Copy)
                        last.then_inc(cx_hi, 1)
                    for j in range(6):
                        if prev:
                            t_evac(n, b, j)
                        if j in (1, 3):
                            act.wait_ge(q_full, 2 * n + j // 2 + 1)
                            act.activation(k.q_raw[:, j // 2, :], y_bank(b, "q", j // 2)[:, :], ACT.Copy)\
                               .then_inc(q_copied, 1)
                    act.wait_ge(kt_full, n + 1)
                    bank = x_bank(b, "k")
                    last = act.activation(k.kT[0][:, b, 0:SEQ], bank[:, 0:SEQ], ACT.Copy, scale=k.qkw[:, 0:1])
                    if b % 2 == 0:
                        last = act.activation(k.kT[0][:, b:b + 2, SEQ:KEYS],
                                              bank[:, SEQ:SEQ + 128].rearrange("p (b k) -> p b k", b=2),
                                              ACT.Copy, scale=k.qkw[:, 0:1])
                    last.then_inc(kt_hi, 1)
                    for tile in range(2):
                        act.wait_ge(qt_full, 2 * n + tile + 1)
                        act.activation(k.qT[0][:, tile, :, :],
                                       x_bank(b, "q", tile)[:, :].rearrange("p (h q) -> p h q", h=GH),
                                       ACT.Copy).then_inc(qt_hi, 1)
                        if prev:
                            pv_evac(n, b, tile)
                    for j, (tile, hp) in enumerate(PAIRS):
                        act.wait_ge(nb_ready, 4 * n + j + 1)
                        for h in (2 * hp, 2 * hp + 1):
                            i = tile * GH + h
                            last = act.activation(k.p1[:, tile, h, :], s_pair(j)[:, h % 2, :], ACT.Exp,
                                                  bias=k.nb[:, i:i + 1], scale=k.rq[:, i:i + 1],
                                                  accum_out=k.rs[:, i:i + 1])
                        last.then_inc(exp_done, 1)

            def tail(n):
                for j in range(6):
                    t_evac(n, 0, j)
                for hp in range(2):
                    pv_evac(n, 0, hp)

            act.wait_ge(pad_zero, 2)
            loop(act, body, tail)

        @block.tensor
        def _(pe):
            def turn(n, b, j, alone=False):
                hp, kt = divmod(j, 3)
                if kt == 0:
                    pe.wait_ge(p_scaled, 4 * (n - 1) + 2 * (hp + 1))
                if j < 2:
                    pe.wait_ge(qt_split, 2 * n - 1 + j)
                elif j == 4:
                    pe.wait_ge(t_split, 6 * (n - 1) + 4)
                elif j == 3 or alone and j == 2:
                    pe.wait_ge(t_split, 6 * (n - 1) + j - 1)
                rows = 64 if kt == 2 else PART
                for hh in range(2):
                    for tile in range(2):
                        last = pe.transpose(x_bank(b, "t", j)[0:rows, (2 * hh + tile) * PART:(2 * hh + tile + 1) * PART],
                                            k.p1[:, tile, 2 * hp + hh, kt * PART:kt * PART + rows], k.ident[:, :])
                last.then_inc(t_full, 1)

            def p_v(n, b, hp, alone=False):
                pb = (b - 1) % BATCH
                pe.wait_ge(t_split, 6 * (n - 1) + 3 * (hp + 1))
                if not alone:
                    pe.wait_ge(q_copied, 2 * n + hp + 1)
                for kt in range(3):
                    last = mm3(pe, y_bank(b, "pv", hp)[:, :], [w[:, pb, kt, :] for w in k.v],
                               [w[:, kt, 2 * hp:2 * hp + 2, :] for w in k.pT], kt == 0, kt == 2)
                last.then_inc(pv_full, 1)

            def out(n, b, j):
                pe.wait_ge(pv_split, 2 * n)
                for h in range(GH):
                    last = mm3(pe, y_bank(b, "d", j)[:, :], [w[:, h, j * PART:(j + 1) * PART] for w in k.oT],
                               [w[:, h, :] for w in k.w_o], h == 0, h == GH - 1)
                last.then_inc(d_full, 1)

            def scores(n, b, j):
                tile, hp = PAIRS[j]
                if j == 0:
                    pe.wait_ge(kt_split, n + 1)
                    pe.wait_ge(qt_split, 2 * n + 2)
                if not (isinstance(n, int) and 4 * n + j < 2):
                    pe.wait_ge(exp_done, 4 * n + j - 1)
                for hh in range(2):
                    last = mm3(pe, s_pair(j)[:, hh, :], [w[:, tile, 2 * hp + hh, :] for w in k.qT],
                               [w[:, b, :] for w in k.kT], True, True)
                last.then_inc(s_full, 1)

            def body(g, first, nxt):
                for b in range(BATCH):
                    n, prev = BATCH * g + b, not (first and b == 0)
                    deep = not (first and b < 2)
                    if b == 0:
                        pe.wait_ge(kv_wlo, CONV["kv"] * (g + 1))
                    if deep:
                        pe.wait_ge(x_added, 2 * (n - 2) + 1)
                    for tile in range(2):
                        t = 2 * b + tile
                        for c in range(CH):
                            last = mm3(pe, y_bank(b, "kv")[:, tile * 256:tile * 256 + 256],
                                       [w[:, c, t * PART:(t + 1) * PART] for w in k.xnT],
                                       [w[:, c, :] for w in k.w_kv], c == 0, c == CH - 1)
                    last.then_inc(kv_full, 1)
                    if deep:
                        pe.wait_ge(x_added, 2 * (n - 2) + 2)
                    if b % 2 == 0:
                        for c in range(CH):
                            last = mm3(pe, y_bank(b, "cx")[:, 0:256], [w[:, c, b * CTX:(b + 2) * CTX] for w in ctx4],
                                       [w[:, c, :] for w in k.w_kv], c == 0, c == CH - 1)
                        last.then_inc(cx_full, 1)
                    if b == 0:
                        pe.wait_ge(q_wlo, CONV["q"] * (g + 1))
                    for tile in range(2):
                        if prev:
                            turn(n, b, 2 * tile)
                            turn(n, b, 2 * tile + 1)
                        if b % 2 == 0:
                            pe.wait_ge(kv_split if tile == 0 else cx_split, n + 1 if tile == 0 else 2 * g + b // 2 + 1)
                        elif tile == 1:
                            pe.wait_ge(kv_split, n + 1)
                        t = 2 * b + tile
                        for c in range(CH):
                            if prev and tile == 0 and c == CH - 1:
                                pe.wait_ge(t_split, 6 * (n - 1) + 1)
                            last = mm3(pe, y_bank(b, "q", tile)[:, :], [w[:, c, t * PART:(t + 1) * PART] for w in k.xnT],
                                       [w[:, c, :] for w in k.w_q], c == 0, c == CH - 1)
                        last.then_inc(q_full, 1)
                    if prev:
                        turn(n, b, 4)
                        turn(n, b, 5)
                        pe.wait_ge(t_split, 6 * (n - 1) + 5)
                    pe.wait_ge(k_scaled, n + 1)
                    nk = 3 if b % 2 == 0 else 2
                    for i in range(nk):
                        last = pe.transpose(x_bank(b, "k")[:, i * PART:(i + 1) * PART], k.k_raw[:, i, :], k.ident[:, :])
                    last.then_inc(kt_full, 1)
                    for tile in range(2):
                        pe.wait_ge(q_copied, 2 * n + tile + 1)
                        if tile == 1:
                            pe.wait_ge(kt_split, n + 1)
                        elif prev:
                            pe.wait_ge(t_split, 6 * n)
                        for h in range(GH):
                            last = pe.transpose(x_bank(b, "q", tile)[:, h * PART:(h + 1) * PART],
                                                k.q_raw[:, tile, h * HD:(h + 1) * HD], k.ident[:, :])
                        last.then_inc(qt_full, 1)
                        if prev:
                            p_v(n, b, tile)
                    scores(n, b, 0)
                    scores(n, b, 1)
                    if prev:
                        if b == 1:
                            pe.wait_ge(o_wlo, CONV["o"] * (g + 1))
                        out(n, b, 0)
                    scores(n, b, 2)
                    if prev:
                        out(n, b, 1)
                    scores(n, b, 3)

            def tail(n):
                for j in range(6):
                    turn(n, 0, j, alone=True)
                pe.wait_ge(x_added, 2 * (n - 1))
                for hp in range(2):
                    p_v(n, 0, hp, alone=True)
                for j in range(2):
                    out(n, 0, j)

            pe.wait_ge(pad_zero, 2)
            loop(pe, body, tail)


def ffn1_buffers(k, scope, sb, pair):
    k.w_base, k.w_ag, k.w_b = pair(scope, "w_base", [CH, HID]), pair(scope, "w_ag", [CH, 256]), pair(scope, "w_b", [2, HID])
    k.ag = sb(scope, "ag", [2, 256])
    k.top, k.idx, k.idxf = sb(scope, "top", [2, 8]), sb(scope, "idx", [2, 8], mybir.dt.uint32), sb(scope, "idxf", [2, 2])
    k.iota_i, k.iota = sb(scope, "iota_i", [NEXP], mybir.dt.int32), sb(scope, "iota", [NEXP])
    k.gap, k.eg, k.pr = sb(scope, "gap", [2, 1]), sb(scope, "eg", [2, 1]), sb(scope, "pr", [2, 4])
    k.ga, k.gb, k.gm = (sb(scope, n, [2, NEXP]) for n in ("ga", "gb", "gm"))
    k.hg = sb(scope, "hg", [2, LR])
    k.hgT = pair(scope, "hgT", [2, 2, PART])


def ffn1_phase(nc, k, sem):
    def sems(*names):
        return [sem("f1_" + n) for n in names]

    w_in, b_in, ag_in, base_hi, ag_hi, b_hi, w_lo, pad = sems("w_in", "b_in", "ag_in", "base_hi", "ag_hi", "b_hi", "w_lo", "pad")
    ag_full, ag_out, o_full, t_full, t_hi, t_lo, x_done, stored = sems(
        "ag_full", "ag_out", "o_full", "t_full", "t_hi", "t_lo", "x_done", "stored")
    route, t_gap, exp_done, hg_done, iota_i = sems("route", "gap", "exp", "hg", "iota_i")
    R1 = LR - PART
    o_bank, ag_bank, t_bank = k.bank[0:3], k.bank[3:5], k.bank[5:7]

    with nc.Block() as block:
        @block.sync
        def _(sp):
            sp.dma_start(k.raw_kv[:, 0:CH * (LR + NEXP)], k.d["w_ag"]).then_inc(ag_in, 16)
            sp.dma_start(k.raw_q[:, :], k.d["w_base"]).then_inc(w_in, 16)
            sp.dma_start(k.raw_o[:, 0:HID], k.d["w_b"][0:PART, :]).then_inc(b_in, 16)
            sp.dma_start(k.raw_o[0:R1, HID:2 * HID], k.d["w_b"][PART:LR, :]).then_inc(b_in, 16)
            for t in range(NT):
                sp.wait_ge(x_done, t + 1)
                sp.dma_start(k.out[t * PART:(t + 1) * PART, :], k.x[:, t, :]).then_inc(stored, 16)
            sp.wait_ge(stored, 16 * NT)

        raw_ag = k.raw_kv[:, 0:CH * (LR + NEXP)].rearrange("p (c n) -> p c n", c=CH)
        raw_base = k.raw_q[:, :].rearrange("p (c n) -> p c n", c=CH)

        @block.gpsimd
        def _(pool):
            pool.iota(k.iota_i[:, :], pattern=[[1, NEXP]], base=0, channel_multiplier=0).then_inc(iota_i, 1)
            for w in k.w_ag:
                last = pool.memset(f(w[:, :, LR + NEXP:256]), 0.0)
            last.then_inc(pad, 1)
            pool.wait_ge(ag_hi, 1)
            pool.tensor_tensor(k.w_ag[1][:, :, 0:LR + NEXP], raw_ag, f(k.w_ag[0][:, :, 0:LR + NEXP]),
                               ALU.subtract).then_inc(w_lo, 1)
            pool.wait_ge(base_hi, 1)
            pool.tensor_tensor(k.w_base[1][:, :, :], raw_base, f(k.w_base[0][:, :, :]), ALU.subtract).then_inc(w_lo, 1)
            pool.wait_ge(b_hi, 1)
            pool.tensor_tensor(k.w_b[1][:, 0, :], k.raw_o[:, 0:HID], f(k.w_b[0][:, 0, :]), ALU.subtract)
            pool.tensor_tensor(k.w_b[1][0:R1, 1, :], k.raw_o[0:R1, HID:2 * HID], f(k.w_b[0][0:R1, 1, :]),
                               ALU.subtract).then_inc(w_lo, 1)

        @block.vector
        def _(dve):
            links = [0]

            def link(ins):
                links[0] += 1
                ins.then_inc(route, 1)
                dve.wait_ge(route, links[0])

            dve.wait_ge(ag_in, 16)
            dve.tensor_copy(k.w_ag[0][:, :, 0:LR + NEXP], raw_ag).then_inc(ag_hi, 1)
            dve.wait_ge(w_in, 16)
            dve.tensor_copy(k.w_base[0][:, :, :], raw_base).then_inc(base_hi, 1)
            dve.wait_ge(b_in, 32)
            dve.tensor_copy(k.w_b[0][:, 0, :], k.raw_o[:, 0:HID])
            dve.tensor_copy(k.w_b[0][0:R1, 1, :], k.raw_o[0:R1, HID:2 * HID]).then_inc(b_hi, 1)
            dve.wait_ge(iota_i, 1)
            link(dve.tensor_copy(k.iota[:, :], k.iota_i[:, :]))

            for s in range(NT + 2):
                if s < NT:
                    u = s % 2
                    logits = k.ag[:, u, LR:LR + NEXP]
                    dve.wait_ge(ag_out, s + 1)
                    link(dve.max(k.top[:, u, :], logits))
                    dve.tensor_scalar(k.gap[:, u, :], k.top[:, u, 1:2], k.top[:, u, 0:1], None, ALU.subtract)\
                       .then_inc(t_gap, 1)
                    link(dve.max_index(k.idx[:, u, :], k.top[:, u, :], logits))
                    link(dve.tensor_copy(k.idxf[:, u, :], k.idx[:, u, 0:2]))
                    dve.wait_ge(exp_done, s + 1)
                    link(dve.tensor_scalar(k.pr[:, u, 0:1], k.eg[:, u, :], 1.0, 1.0 / LORA_SCALE, ALU.add, ALU.mult))
                    link(dve.reciprocal(k.pr[:, u, 1:2], k.pr[:, u, 0:1]))
                    link(dve.tensor_tensor(k.pr[:, u, 2:3], k.pr[:, u, 1:2], k.eg[:, u, :], ALU.mult))
                    dve.tensor_scalar(k.ga[:, u, :], k.iota[:, :], k.idxf[:, u, 0:1], k.pr[:, u, 1:2],
                                      ALU.is_equal, ALU.mult)
                    link(dve.tensor_scalar(k.gb[:, u, :], k.iota[:, :], k.idxf[:, u, 1:2], k.pr[:, u, 2:3],
                                           ALU.is_equal, ALU.mult))
                    link(dve.tensor_tensor(k.gm[:, u, :], k.ga[:, u, :], k.gb[:, u, :], ALU.add))
                    if s >= 2:
                        dve.wait_ge(t_full, s - 1)
                    dve.tensor_tensor(k.hg[:, u, :].rearrange("p (e r) -> p e r", r=RANK),
                                      k.ag[:, u, 0:LR].rearrange("p (e r) -> p e r", r=RANK),
                                      k.gm[:, u, :].unsqueeze(2).to_broadcast([PART, NEXP, RANK]),
                                      ALU.mult).then_inc(hg_done, 1)
                if 1 <= s <= NT:
                    u = (s - 1) % 2
                    dve.wait_ge(t_hi, s)
                    dve.tensor_tensor(k.hgT[1][:, u, 0, :], t_bank[u][:, 0:PART], f(k.hgT[0][:, u, 0, :]), ALU.subtract)
                    dve.tensor_tensor(k.hgT[1][0:R1, u, 1, :], t_bank[u][0:R1, PART:2 * PART],
                                      f(k.hgT[0][0:R1, u, 1, :]), ALU.subtract).then_inc(t_lo, 1)
                if s >= 2:
                    t = s - 2
                    dve.wait_ge(o_full, t + 1)
                    dve.scalar_tensor_tensor(out=k.x[:, t, :], in0=o_bank[t % 3][:, :], scalar=k.gate[:, 3:4],
                                             in1=k.x[:, t, :], op0=ALU.mult, op1=ALU.add).then_inc(x_done, 1)

        @block.scalar
        def _(act):
            for s in range(NT + 1):
                if s < NT:
                    act.wait_ge(ag_full, s + 1)
                    if s >= 2:
                        act.wait_ge(hg_done, s - 1)
                    act.activation(k.ag[:, s % 2, :], ag_bank[s % 2][:, 0:256], ACT.Copy).then_inc(ag_out, 1)
                    act.wait_ge(t_gap, s + 1)
                    act.activation(k.eg[:, s % 2, :], k.gap[:, s % 2, :], ACT.Exp).then_inc(exp_done, 1)
                if s >= 1:
                    u = (s - 1) % 2
                    act.wait_ge(t_full, s)
                    act.activation(k.hgT[0][:, u, 0, :], t_bank[u][:, 0:PART], ACT.Copy)
                    act.activation(k.hgT[0][0:R1, u, 1, :], t_bank[u][0:R1, PART:2 * PART], ACT.Copy).then_inc(t_hi, 1)

        @block.tensor
        def _(pe):
            pe.wait_ge(pad, 1)
            for s in range(NT + 2):
                if s < NT:
                    tok = slice(s * PART, (s + 1) * PART)
                    if s == 0:
                        pe.wait_ge(w_lo, 1)
                    if s >= 2:
                        pe.wait_ge(ag_out, s - 1)
                    for c in range(CH):
                        last = mm3(pe, ag_bank[s % 2][:, 0:256], [w[:, c, tok] for w in k.xnT],
                                   [w[:, c, :] for w in k.w_ag], c == 0, c == CH - 1)
                    last.then_inc(ag_full, 1)
                    if s == 0:
                        pe.wait_ge(w_lo, 2)
                    if s >= 3:
                        pe.wait_ge(x_done, s - 2)
                    for c in range(CH):
                        mm3(pe, o_bank[s % 3][:, :], [w[:, c, tok] for w in k.xnT], [w[:, c, :] for w in k.w_base],
                            c == 0, False)
                if 1 <= s <= NT:
                    u = (s - 1) % 2
                    pe.wait_ge(hg_done, s)
                    if s >= 3:
                        pe.wait_ge(t_lo, s - 2)
                    pe.transpose(t_bank[u][:, 0:PART], k.hg[:, u, 0:PART], k.ident[:, :])
                    pe.transpose(t_bank[u][0:R1, PART:2 * PART], k.hg[:, u, PART:LR], k.ident[:, :]).then_inc(t_full, 1)
                if s >= 2:
                    t = s - 2
                    if s == 2:
                        pe.wait_ge(w_lo, 3)
                    pe.wait_ge(t_lo, t + 1)
                    mm3(pe, o_bank[t % 3][:, :], [w[:, t % 2, 0, :] for w in k.hgT], [w[:, 0, :] for w in k.w_b], False, False)
                    mm3(pe, o_bank[t % 3][:, :], [w[0:R1, t % 2, 1, :] for w in k.hgT],
                        [w[0:R1, 1, :] for w in k.w_b], False, True).then_inc(o_full, 1)


def build(nc, d, out, phases=("attn0", "ffn0", "attn1", "ffn1")):
    k = Kernel()
    k.d = d
    with ExitStack() as stack:
        def sem(name):
            return stack.enter_context(nc.semaphore(name))

        def sb(scope, name, shape, dtype=F32):
            return scope.enter_context(nc.sbuf_tensor(name, [PART] + shape, dtype))

        def pair(scope, name, shape):
            return [sb(scope, name + part, shape, F32R) for part in ("_hi", "_lo")]

        k.x = sb(stack, "x", [NT, HID])
        k.ctxT = pair(stack, "ctxT", [CH * BATCH * CTX])
        k.xnT = pair(stack, "xnT", [CH, BATCH * SEQ])
        k.ident, k.ones_f = sb(stack, "ident", [PART]), sb(stack, "ones_f", [PART])
        k.ones = sb(stack, "ones", [PART], F32R)
        k.minus_half = sb(stack, "minus_half", [16])
        k.gate_raw, k.gate = sb(stack, "gate_raw", [4]), sb(stack, "gate", [4])
        k.normw, k.qkw = sb(stack, "normw", [2]), sb(stack, "qkw", [1])
        k.raw_q, k.raw_o = sb(stack, "raw_q", [GH * HID]), sb(stack, "raw_o", [GH * HID])
        k.raw_kv = sb(stack, "raw_kv", [CH * 2 * HD + GH + 2])
        k.psum = stack.enter_context(nc.psum_tensor("psum", [PART, 8 * 512], F32))
        k.bank = [k.psum[:, n * 512:(n + 1) * 512] for n in range(8)]
        k.out = out
        k.ln_st, k.ln_mv, k.ln_rs = sb(stack, "ln_st", [NT, 6]), sb(stack, "ln_mv", [NT, 2]), sb(stack, "ln_rs", [NT])

        k.ln_sems = [sem("ln_" + n) for n in ("stats", "mv", "ms", "rstd", "xn", "tr_full", "xn_hi", "tr_free", "bo")]

        calls = []

        def ln(add_bo=False):
            with ExitStack() as scope:
                k.xn_tok = sb(scope, f"xn_tok{len(calls)}", [4, HID])
                ln_phase(nc, k, len(calls), add_bo)
                calls.append(None)

        with ExitStack() as outer:
            k.bo, k.gbo = sb(outer, "bo", [HID]), sb(outer, "gbo", [HID])
            load_phase(nc, k, sem)
            ln(add_bo=True)
        if "attn0" in phases:
            with ExitStack() as scope:
                k.w_q, k.w_o = pair(scope, "w0q", [GH * HID]), pair(scope, "w0o", [GH * HID])
                k.w_kv = pair(scope, "w0kv", [CH * 2 * HD])
                k.bias, k.bq_rep = sb(scope, "bias", [GH + 2]), pair(scope, "bq_rep", [PART])
                k.bqk = sb(scope, "bqk", [BATCH, GH, CTX], F32R)
                k.kvT = pair(scope, "kvT0", [2, BATCH * CTX])
                k.WK = pair(scope, "WK", [CH, BATCH, GH, CTX])
                k.VW = pair(scope, "VW", [GH // 2, BATCH, HID])
                k.p0 = sb(scope, "p0", [4, GH * CTX])
                k.mx0, k.sum0, k.rinv0 = sb(scope, "mx0", [2, GH]), sb(scope, "sum0", [2, GH]), sb(scope, "rinv0", [4, GH])
                k.pT0 = pair(scope, "pT0", [2, 2 * PART])
                attn0_phase(nc, k, sem)
        if "ffn0" in phases:
            ln()
            with ExitStack() as scope:
                ffn0_buffers(k, scope, sb, pair)
                ffn0_phase(nc, k, sem)
        if "attn1" in phases:
            ln()
            with ExitStack() as scope:
                attn1_buffers(k, scope, sb, pair)
                attn1_phase(nc, k, sem)
        if "ffn1" in phases:
            ln()
            with ExitStack() as scope:
                ffn1_buffers(k, scope, sb, pair)
                ffn1_phase(nc, k, sem)
                return
        done = sem("out_done")
        with nc.Block() as block:
            @block.sync
            def _(sp):
                sp.dma_start(out.rearrange("(t p) c -> p t c", p=PART), k.x[:, :, :]).then_inc(done, 16)
                sp.wait_ge(done, 16)


def layouts(inputs):
    import numpy as np
    a = {n: np.asarray(v) for n, v in inputs.items()}

    def chunked(w):
        return np.ascontiguousarray(w.reshape(-1, PART, w.shape[1]).transpose(1, 0, 2))

    def by_group(w):
        return np.ascontiguousarray(w.reshape(NKV, GH, HD, w.shape[1]).transpose(0, 2, 1, 3)).reshape(NKV * HD, -1)

    def kv_by_group(wk, wv):
        w = np.stack([wk, wv], 0).reshape(2, CH, PART, NKV, HD)
        return np.ascontiguousarray(w.transpose(3, 2, 1, 0, 4)).reshape(NKV * PART, -1)

    wkv, bkv = a["L0_xattn_Wkv"], a["L0_xattn_bkv"]
    half = NKV * HD
    biases = np.concatenate([a["L0_xattn_bq"].reshape(NKV, GH, HD).transpose(0, 2, 1),
                             bkv.reshape(2, NKV, HD).transpose(1, 2, 0)], 2).reshape(NKV * HD, GH + 2)
    gu = a["L0_ffn_w_gate_up"]
    chunks = []
    for i in range(IC):
        s = slice(i * PART, min((i + 1) * PART, INNER))
        chunks.append(np.concatenate([chunked(gu[:INNER][s].T), chunked(gu[INNER:][s].T)], 2).reshape(PART, -1))
    wd = a["L0_ffn_w_down"].T
    return {
        "x": a["x"].reshape(BATCH * SEQ, HID),
        "ctxT": chunked(a["ctx_4096"].reshape(BATCH * CTX, HID).T).reshape(PART, -1),
        "gates": np.concatenate([a["g_xattn"], a["g_ffn"]]).reshape(1, 4),
        "bo": a["L0_xattn_bo"].reshape(1, HID),
        "normw": np.stack([a["L1_xattn_q_norm_w"], a["L1_xattn_k_norm_w"]], 1),
        "w0q": by_group(a["L0_xattn_Wq"].T),
        "w0kv": np.concatenate([kv_by_group(wkv[:, :half], wkv[:, half:]), biases], 1),
        "w0o": by_group(a["L0_xattn_Wo"]),
        "w_gu": np.concatenate(chunks, 1),
        "w_down": wd,
        "w1q": np.ascontiguousarray(a["L1_xattn_Wq"].reshape(CH, PART, NKV, GH * HD).transpose(2, 1, 0, 3)).reshape(NKV * PART, -1),
        "w1kv": kv_by_group(a["L1_xattn_Wk"], a["L1_xattn_Wv"]),
        "w1o": by_group(a["L1_xattn_Wo"]),
        "w_base": chunked(a["L1_ffn_base_W"].T).reshape(PART, -1),
        "w_ag": chunked(np.concatenate([a["L1_ffn_lora_A"].reshape(LR, HID).T, a["L1_ffn_gate_W"].T], 1)).reshape(PART, -1),
        "w_b": np.ascontiguousarray(a["L1_ffn_lora_B"].transpose(0, 2, 1)).reshape(LR, HID),
    }


def kernel(**inputs):
    import numpy as _np
    import concourse.bacc as _bacc
    from concourse import mybir as _mybir
    from concourse.bass_utils import run_bass_kernel_spmd as _run

    nc = _bacc.Bacc("TRN2", target_bir_lowering=False, num_devices=1)
    arrays, d = {}, {}
    for name, a in layouts(inputs).items():
        a = _np.ascontiguousarray(a)
        arrays[f"in_{name}"] = a
        d[name] = nc.dram_tensor(f"in_{name}", a.shape, _mybir.dt.from_np(a.dtype), kind="ExternalInput").ap()
    out = nc.dram_tensor("out_x", (BATCH * SEQ, HID), F32, kind="ExternalOutput").ap()
    build(nc, d, out)
    r = _run(nc, [arrays], core_ids=[0])
    return r.results[0]["out_x"].reshape(BATCH, SEQ, HID)
```

```python
import concourse.bass as bass
from concourse import mybir
from contextlib import ExitStack

F32 = mybir.dt.float32
F32R = mybir.dt.float32r
ALU = mybir.AluOpType
ACT = mybir.ActivationFunctionType
AX = mybir.AxisListType

PART = 128
BATCH, SEQ, HID = 4, 256, 512
CTX = 64
CH = HID // PART
NT = BATCH * SEQ // PART
HD = 128
NKV = 8
GH = 4
INNER = 1376
IC = 11
ILAST = INNER - (IC - 1) * PART
NEXP, RANK = 28, 8
LR = NEXP * RANK
LN_EPS, RMS_EPS = 1e-5, 1e-6
SCALE = float(HD) ** -0.5
LORA_SCALE = 16.0 / RANK
KVW = CH * 2 * HD
QW = GH * HID


def f(ap):
    return ap.bitcast(F32)


def mm3(pe, out, w, m, start, stop):
    pe.matmul(out, w[1], m[0], start=start, stop=False)
    pe.matmul(out, w[0], m[1], start=False, stop=False)
    return pe.matmul(out, w[0], m[0], start=False, stop=stop)


def run(nc, sync, gpsimd, vector, scalar, tensor):
    with nc.Block() as block:
        block.sync(sync)
        block.gpsimd(gpsimd)
        block.vector(vector)
        block.scalar(scalar)
        block.tensor(tensor)


def by_head(ap):
    return ap.rearrange("p (h n) -> p h n", h=GH)


class Kernel:
    pass


class LayerNorm:

    def __init__(self, k, sem):
        self.k = k
        self.stats, self.mv, self.ms, self.rstd, self.xn, self.turned, self.hi_done, self.split = (
            sem("ln_" + n) for n in ("stats", "mv", "ms", "rstd", "xn", "turned", "hi", "split"))

    def dve_stats(self, dve, c, t):
        k, m = self.k, NT * c + t
        dve.bn_stats(k.ln_st[:, t, :], k.x[:, t, :]).then_inc(self.stats, 1)
        dve.wait_ge(self.stats, m + 1)
        dve.bn_aggr(k.ln_mv[:, t, :], k.ln_st[:, t, :]).then_inc(self.mv, 1)

    def pool_rstd(self, pool, c, t):
        k, m = self.k, NT * c + t
        pool.wait_ge(self.mv, m + 1)
        pool.tensor_scalar(k.ln_rs[:, t:t + 1], k.ln_mv[:, t, 1:2], LN_EPS, None, ALU.add).then_inc(self.ms, 1)
        pool.wait_ge(self.ms, m + 1)
        pool.tensor_tensor(k.ln_rs[:, t:t + 1], k.ln_rs[:, t:t + 1], k.minus_half[:, 0:1], ALU.pow).then_inc(self.rstd, 1)

    def dve_norm(self, dve, c, t):
        k, m = self.k, NT * c + t
        dve.wait_ge(self.rstd, m + 1)
        if m >= 2:
            dve.wait_ge(self.turned, m - 1)
        dve.tensor_scalar(k.xn_tok[:, t % 2, :], k.x[:, t, :], k.ln_mv[:, t, 0:1], k.ln_rs[:, t:t + 1],
                          ALU.subtract, ALU.mult).then_inc(self.xn, 1)

    def pe_turn(self, pe, c, t, bank):
        k, m = self.k, NT * c + t
        pe.wait_ge(self.xn, m + 1)
        if m >= 2:
            pe.wait_ge(self.split, m - 1)
        for i in range(CH):
            last = pe.transpose(bank[:, i * PART:(i + 1) * PART], k.xn_tok[:, t % 2, i * PART:(i + 1) * PART], k.ident[:, :])
        last.then_inc(self.turned, 1)

    def act_hi(self, act, c, t, bank):
        k, m = self.k, NT * c + t
        act.wait_ge(self.turned, m + 1)
        act.activation(k.xnT[0][:, :, t * PART:(t + 1) * PART], bank.rearrange("p (c q) -> p c q", c=CH),
                       ACT.Copy).then_inc(self.hi_done, 1)

    def dve_lo(self, dve, c, t, bank):
        k, m = self.k, NT * c + t
        dve.wait_ge(self.hi_done, m + 1)
        dve.tensor_tensor(k.xnT[1][:, :, t * PART:(t + 1) * PART], bank.rearrange("p (c q) -> p c q", c=CH),
                          f(k.xnT[0][:, :, t * PART:(t + 1) * PART]), ALU.subtract).then_inc(self.split, 1)


def attn0_phase(nc, k, sem, ln):
    in_ctx, in_x, in_small = sem("in_ctx"), [sem(f"in_x{t}") for t in range(4)], sem("in_small")
    ident0, ident, gates, gbo_done, ctx_hi, ctx_lo, bo_added = (
        sem(n) for n in ("ident0", "ident", "gates", "gbo", "ctx_hi", "ctx_lo", "bo_added"))
    kv_in, q_in, o_in, kv_hi, q_hi, o_hi, kv_lo, q_lo, o_lo, bqr_hi, bqr_lo, bias_in, bqk_zero = (
        sem("a0_" + n) for n in ("kv_in", "q_in", "o_in", "kv_hi", "q_hi", "o_hi", "kv_lo", "q_lo", "o_lo",
                                 "bqr_hi", "bqr_lo", "bias_in", "bqk_zero"))
    prep_full, prep_hi, prep_free, s_full, s_max, nb_ready, p_exp, p_rec, p_ready, pt_full, pt_hi, pt_lo, o_full, x_done = (
        sem("a0_" + n) for n in ("prep_full", "prep_hi", "prep_free", "s_full", "s_max", "nb", "p_exp", "p_rec",
                                 "p_ready", "pt_full", "pt_hi", "pt_lo", "o_full", "x_done"))

    NEXT_PREP = {6: [("kv",)], 8: [("bq",), ("wk", 0), ("wk", 1)], 9: [("vw", 0, 0), ("wk", 2), ("wk", 3)],
                 10: [("wk", 4), ("wk", 5), ("wk", 6), ("wk", 7), ("vw", 1, 0)]}
    OWN_PREP = {0: [("vw", 2, 0), ("vw", 3, 0)], 1: [("vw", 0, 1)], 2: [("vw", 1, 1)], 3: [("vw", 2, 1)], 4: [("vw", 3, 1)]}
    ORDER = sum(OWN_PREP.values(), []) + sum(NEXT_PREP.values(), [])
    FILLS, OWN = len(ORDER), sum(map(len, OWN_PREP.values()))
    HEAD = FILLS - OWN
    START = HEAD - FILLS
    FREE0 = 2
    CONV = {"kv": 2, "q": 4, "o": 4}
    wq4, wo4 = [by_head(w[:, :]) for w in k.w_q], [by_head(w[:, :]) for w in k.w_o]
    wkv4 = [w[:, :].rearrange("p (c n) -> p c n", c=CH) for w in k.w_kv]
    ctx4 = [w[:, :].rearrange("p (c n) -> p c n", c=CH) for w in k.ctxT]
    s_bank, pt_bank, o_bank = [k.bank[3], k.bank[4]], k.bank[5], [k.bank[6], k.bank[7]]
    raw = {"kv": k.raw_kv, "q": k.raw_q, "o": k.raw_o}
    wts = {"kv": k.w_kv, "q": k.w_q, "o": k.w_o}
    width = {"kv": KVW, "q": QW, "o": QW}
    arrived, hi_of, lo_of = {"kv": kv_in, "q": q_in, "o": o_in}, {"kv": kv_hi, "q": q_hi, "o": o_hi}, {"kv": kv_lo, "q": q_lo, "o": o_lo}

    def ring(fill):
        return k.bank[(HEAD + ORDER.index(fill)) % 3]

    def steps_fills(s, nxt):
        return OWN_PREP.get(s, []) + (NEXT_PREP.get(s, []) if nxt else [])

    def wk_view(w, c, hp):
        return w[:, c, :, 2 * hp:2 * hp + 2, :].rearrange("p b h k -> p h b k")

    def wk_bank(bank):
        return bank.rearrange("p (h b k) -> p h b k", h=2, b=BATCH)

    def bq_bank(bank, h):
        return bank[32 * h:32 * h + 1, 0:BATCH * CTX].rearrange("p (b k) -> p b k", b=BATCH)

    def ln_bank(t):
        return k.bank[t % 2]

    def spread(stat):
        return stat.unsqueeze(2).to_broadcast([PART, GH, CTX])

    def sync(sp):
        sp.dma_start(k.xn_tok[:, :, :].rearrange("p a b -> p (a b)"), k.d["ctxT"]).then_inc(in_ctx, 16)
        for kind in ("kv", "q", "o"):
            sp.dma_start(raw[kind][:, :], k.d["w0" + kind][0:PART, :]).then_inc(arrived[kind], 16)
        for i in range(4):
            sp.dma_start(k.x[:, 2 * i:2 * i + 2, :],
                         k.d["x"][i * 256:(i + 1) * 256, :].rearrange("(t p) c -> p t c", p=PART)).then_inc(in_x[i], 16)
        sp.dma_start(k.gate_raw[:, :], k.d["gates"].to_broadcast([PART, 4])).then_inc(in_small, 16)
        sp.dma_start(k.bo[:, :], k.d["bo"].to_broadcast([PART, HID])).then_inc(in_small, 16)
        sp.dma_start(k.normw[:, :], k.d["normw"]).then_inc(in_small, 16)
        with sp.Fori(1, NKV) as g:
            for kind in ("kv", "q", "o"):
                sp.wait_ge(lo_of[kind], g * CONV[kind])
                sp.dma_start(raw[kind][:, :], k.d["w0" + kind][bass.ts(g, PART), :]).then_inc(arrived[kind], 16)

    def gpsimd(pool):
        def lo_piece(kind, g, i):
            n = width[kind] // CONV[kind]
            if i == 0:
                pool.wait_ge(hi_of[kind], g + 1)
            s = slice(i * n, (i + 1) * n)
            pool.tensor_tensor(wts[kind][1][:, s], raw[kind][:, s], f(wts[kind][0][:, s]), ALU.subtract).then_inc(lo_of[kind], 1)

        def bq_rows(g):
            pool.wait_ge(bqr_hi, g + 1)
            pool.tensor_tensor(by_head(k.bq_rep[1][:, :]), k.bias[:, 0:GH].unsqueeze(2).to_broadcast([PART, GH, 32]),
                               by_head(f(k.bq_rep[0][:, :])), ALU.subtract).then_inc(bqr_lo, 1)

        def body(g, nxt):
            sched = {1: [("kv", 0)], 2: [("kv", 1)], 3: [("q", 0)], 4: [("q", 1)], 5: [("q", 2), ("o", 0)],
                     6: [("q", 3), ("o", 1)], 7: [("o", 2), ("o", 3)]}
            for t in range(NT):
                pool.wait_ge(p_rec, NT * g + t + 1)
                p = by_head(k.p0[:, t % 4, :])
                pool.tensor_tensor(p, p, spread(k.rinv0[:, t % 4, :]), ALU.mult).then_inc(p_ready, 1)
                if nxt:
                    for kind, i in sched.get(t, []):
                        lo_piece(kind, g + 1, i)
                    if t == 2:
                        bq_rows(g + 1)
                elif t >= 3:
                    ln.pool_rstd(pool, 1, t - 3)

        pool.memset(k.ident[:, :], 0.0).then_inc(ident0, 1)
        pool.memset(k.minus_half[:, :], -0.5)
        pool.wait_ge(ident0, 1)
        pool.affine_select(out=k.ident[:, :], in_=k.ident[:, :], compare_op=ALU.not_equal, fill=1.0,
                           base=0, pattern=[[-1, PART]], channel_multiplier=1).then_inc(ident, 1)
        pool.memset(f(k.bqk[:, :, :, :]), 0.0).then_inc(bqk_zero, 1)
        bq_rows(0)
        for i in range(CONV["q"]):
            lo_piece("q", 0, i)
        pool.wait_ge(gbo_done, 1)
        for t in range(NT):
            ln.pool_rstd(pool, 0, t)
        for t in range(NT):
            pool.wait_ge(ln.xn, t + 1)
            pool.tensor_tensor(k.x[:, t, :], k.x[:, t, :], k.gbo[:, :], ALU.add).then_inc(bo_added, 1)
        body(0, True)
        with pool.Fori(1, NKV - 1) as g:
            body(g, True)
        body(NKV - 1, False)
        for t in range(NT - 3, NT):
            ln.pool_rstd(pool, 1, t)

    def vector(dve):
        def conv(kind, g):
            dve.wait_ge(arrived[kind], 16 * g + 16)
            if kind == "kv":
                dve.tensor_copy(k.bias[:, :], k.raw_kv[:, KVW:KVW + GH + 2]).then_inc(bias_in, 1)
            dve.tensor_copy(wts[kind][0][:, :], raw[kind][:, 0:width[kind]]).then_inc(hi_of[kind], 1)
            if kind == "kv":
                dve.wait_ge(bias_in, g + 1)
                dve.tensor_copy(by_head(k.bq_rep[0][:, :]),
                                k.bias[:, 0:GH].unsqueeze(2).to_broadcast([PART, GH, 32])).then_inc(bqr_hi, 1)

        def own_lo(kind, pieces):
            dve.wait_ge(hi_of[kind], 1)
            dve.tensor_tensor(wts[kind][1][:, :], raw[kind][:, 0:width[kind]], f(wts[kind][0][:, :]),
                              ALU.subtract).then_inc(lo_of[kind], pieces)

        def prep(base, fill):
            bank, kind = ring(fill), fill[0]
            dve.wait_ge(prep_hi, base + ORDER.index(fill) + 1)
            if kind == "kv":
                for j in range(2):
                    last = dve.scalar_tensor_tensor(
                        out=k.kvT[1][:, j, :], in0=bank[:, j * 256:(j + 1) * 256], scalar=k.bias[:, GH + j:GH + j + 1],
                        in1=f(k.kvT[0][:, j, :]), op0=ALU.add, op1=ALU.subtract)
            elif kind == "bq":
                for h in range(GH):
                    last = dve.tensor_tensor(k.bqk[32:33, :, h, :], bq_bank(bank, h), f(k.bqk[0:1, :, h, :]), ALU.subtract)
            elif kind == "wk":
                c, hp = divmod(fill[1], 2)
                last = dve.tensor_tensor(wk_view(k.WK[1], c, hp), wk_bank(bank), f(wk_view(k.WK[0], c, hp)), ALU.subtract)
            else:
                _, h, pr = fill
                r = slice(64 * (h % 2), 64 * (h % 2) + 64)
                for bp in range(2):
                    last = dve.tensor_tensor(k.VW[1][r, h // 2, 2 * pr + bp, :], bank[64 * bp:64 * bp + 64, :],
                                             f(k.VW[0][r, h // 2, 2 * pr + bp, :]), ALU.subtract)
            last.then_inc(prep_free, 1)

        def x_add(g, t):
            dve.wait_ge(o_full, NT * g + t + 1)
            dve.scalar_tensor_tensor(out=k.x[:, t, :], in0=o_bank[t % 2], scalar=k.gate[:, 0:1],
                                     in1=k.x[:, t, :], op0=ALU.mult, op1=ALU.add).then_inc(x_done, 1)

        def body(g, nxt):
            base = HEAD + FILLS * g
            for s in range(NT + 3):
                n = NT * g + s
                if s >= 4:
                    x_add(g, s - 4)
                    if not nxt:
                        dve.wait_ge(x_done, n - 3)
                        ln.dve_stats(dve, 1, s - 4)
                if 1 <= s <= NT:
                    dve.wait_ge(p_exp, n)
                    dve.reciprocal(k.rinv0[:, (s - 1) % 4, :], k.sum0[:, (s - 1) % 2, :]).then_inc(p_rec, 1)
                if s < NT:
                    dve.wait_ge(s_full, n + 1)
                    dve.tensor_reduce(k.mx0[:, s % 2, :], by_head(s_bank[s % 2][:, 0:GH * CTX]), AX.X, ALU.max)\
                       .then_inc(s_max, 1)
                    dve.wait_ge(s_max, n + 1)
                    dve.tensor_scalar(k.nb0[:, s % 2, :], k.mx0[:, s % 2, :], -SCALE, None, ALU.mult).then_inc(nb_ready, 1)
                for fill in steps_fills(s, nxt):
                    prep(base, fill)
                if 2 <= s < NT + 2:
                    t = s - 2
                    dve.wait_ge(pt_hi, n - 1)
                    dve.tensor_tensor(k.pT0[1][:, t % 2, :], pt_bank[:, 0:256], f(k.pT0[0][:, t % 2, :]),
                                      ALU.subtract).then_inc(pt_lo, 1)
                if nxt and s in (1, 3, 5):
                    conv({1: "kv", 3: "q", 5: "o"}[s], g + 1)
                if not nxt and s >= 5:
                    ln.dve_norm(dve, 1, s - 5)
                if not nxt and s >= 7:
                    ln.dve_lo(dve, 1, s - 7, ln_bank(s - 7))
            x_add(g, NT - 1)

        dve.wait_ge(in_ctx, 16)
        ctx_raw = k.xn_tok[:, :, :].rearrange("p a b -> p (a b)")
        dve.tensor_copy(k.ctxT[0][:, :], ctx_raw).then_inc(ctx_hi, 1)
        conv("kv", 0)
        dve.wait_ge(ctx_hi, 1)
        dve.tensor_tensor(k.ctxT[1][:, :], ctx_raw, f(k.ctxT[0][:, :]), ALU.subtract).then_inc(ctx_lo, 1)
        own_lo("kv", CONV["kv"])
        conv("q", 0)
        dve.memset(k.ones_f[:, :], 1.0).then_inc(gates, 1)
        conv("o", 0)
        dve.wait_ge(bqk_zero, 1)
        prep(START, ("kv",))
        prep(START, ("bq",))
        own_lo("o", CONV["o"])
        dve.wait_ge(gates, 1)
        dve.tensor_copy(k.ones[:, :], k.ones_f[:, :])
        dve.wait_ge(in_small, 48)
        dve.scalar_tensor_tensor(out=k.qkw[:, :], in0=k.normw[:, 0:1], scalar=float(HD) ** 0.5, in1=k.normw[:, 1:2],
                                 op0=ALU.mult, op1=ALU.mult)
        for i in range(4):
            dve.wait_ge(in_x[i], 16)
            for t in (2 * i, 2 * i + 1):
                ln.dve_stats(dve, 0, t)
            for fill in ORDER[OWN + 2 + 3 * i:][:1 if i == 3 else 3]:
                prep(START, fill)
        dve.wait_ge(ctx_lo, 1)
        for t in range(NT):
            ln.dve_norm(dve, 0, t)
            if t >= 1:
                ln.dve_lo(dve, 0, t - 1, o_bank[(t - 1) % 2])
        ln.dve_lo(dve, 0, NT - 1, o_bank[(NT - 1) % 2])
        dve.wait_ge(bo_added, NT)
        body(0, True)
        with dve.Fori(1, NKV - 1) as g:
            body(g, True)
        body(NKV - 1, False)
        dve.wait_ge(x_done, NT * NKV)
        ln.dve_stats(dve, 1, NT - 1)
        for t in range(NT - 4, NT):
            if t >= NT - 2:
                ln.dve_norm(dve, 1, t)
            ln.dve_lo(dve, 1, t, ln_bank(t))

    def scalar(act):
        def prep(base, fill):
            bank, kind = ring(fill), fill[0]
            act.wait_ge(prep_full, base + ORDER.index(fill) + 1)
            if kind == "kv":
                for j in range(2):
                    last = act.activation(k.kvT[0][:, j, :], bank[:, j * 256:(j + 1) * 256], ACT.Identity,
                                          bias=k.bias[:, GH + j:GH + j + 1])
            elif kind == "bq":
                for h in range(GH):
                    last = act.activation(k.bqk[0:1, :, h, :], bq_bank(bank, h), ACT.Copy)
            elif kind == "wk":
                c, hp = divmod(fill[1], 2)
                last = act.activation(wk_view(k.WK[0], c, hp), wk_bank(bank), ACT.Copy)
            else:
                _, h, pr = fill
                r = slice(64 * (h % 2), 64 * (h % 2) + 64)
                for bp in range(2):
                    last = act.activation(k.VW[0][r, h // 2, 2 * pr + bp, :], bank[64 * bp:64 * bp + 64, :], ACT.Copy)
            last.then_inc(prep_hi, 1)

        def body(g, nxt):
            base = HEAD + FILLS * g
            for s in range(NT + 3):
                n = NT * g + s
                for fill in steps_fills(s, nxt):
                    prep(base, fill)
                if 2 <= s < NT + 2:
                    act.wait_ge(pt_full, n - 1)
                    act.activation(k.pT0[0][:, s % 2, :], pt_bank[:, 0:256], ACT.Copy).then_inc(pt_hi, 1)
                if s < NT:
                    act.wait_ge(nb_ready, n + 1)
                    for h in range(GH):
                        last = act.activation(k.p0[:, s % 4, h * CTX:(h + 1) * CTX],
                                              s_bank[s % 2][:, h * CTX:(h + 1) * CTX], ACT.Exp, scale=SCALE,
                                              bias=k.nb0[:, s % 2, h:h + 1], accum_out=k.sum0[:, s % 2, h:h + 1])
                    last.then_inc(p_exp, 1)
                if not nxt and s >= 6:
                    ln.act_hi(act, 1, s - 6, ln_bank(s - 6))

        act.wait_ge(bqk_zero, 1)
        act.wait_ge(bias_in, 1)
        prep(START, ("kv",))
        prep(START, ("bq",))
        act.wait_ge(in_small, 48)
        act.activation(k.gate[:, :], k.gate_raw[:, :], ACT.Tanh).then_inc(gates, 1)
        act.wait_ge(gates, 2)
        act.activation(k.gbo[:, :], k.bo[:, :], ACT.Copy, scale=k.gate[:, 0:1]).then_inc(gbo_done, 1)
        for fill in ORDER[OWN + 2:]:
            prep(START, fill)
        for t in range(NT):
            ln.act_hi(act, 0, t, o_bank[t % 2])
        body(0, True)
        with act.Fori(1, NKV - 1) as g:
            body(g, True)
        body(NKV - 1, False)
        for t in range(NT - 3, NT):
            ln.act_hi(act, 1, t, ln_bank(t))

    def tensor(pe):
        def prep(base, fill, g):
            bank, at, kind = ring(fill), base + ORDER.index(fill), fill[0]
            if not (isinstance(at, int) and at < 3):
                pe.wait_ge(prep_free, at - 2)
            if kind == "kv":
                pe.wait_ge(kv_lo, CONV["kv"] * (g + 1))
                for j in range(2):
                    for c in range(CH):
                        last = mm3(pe, bank[:, j * 256:(j + 1) * 256], [w[:, c, j * HD:(j + 1) * HD] for w in wkv4],
                                   [w[:, c, :] for w in ctx4], c == 0, c == CH - 1)
            elif kind == "bq":
                pe.wait_ge(prep_free, base + ORDER.index(("kv",)) + 1)
                pe.wait_ge(bqr_lo, g + 1)
                last = mm3(pe, bank[:, 0:256], [w[:, :] for w in k.bq_rep], [w[:, 0, :] for w in k.kvT], True, True)
            elif kind == "wk":
                c, hp = divmod(fill[1], 2)
                if fill[1] == 0:
                    pe.wait_ge(q_lo, CONV["q"] * (g + 1))
                for h in range(2):
                    last = mm3(pe, bank[:, h * 256:(h + 1) * 256],
                               [w[:, 2 * hp + h, c * PART:(c + 1) * PART] for w in wq4],
                               [w[:, 0, :] for w in k.kvT], True, True)
            else:
                _, h, pr = fill
                if (h, pr) == (0, 0):
                    pe.wait_ge(o_lo, CONV["o"] * (g + 1))
                last = mm3(pe, bank, [w[:, 1, pr * PART:(pr + 1) * PART] for w in k.kvT],
                           [w[:, h, :] for w in wo4], True, True)
            last.then_inc(prep_full, 1)

        def body(g, first, nxt):
            base = HEAD + FILLS * g
            for s in range(NT + 3):
                n = NT * g + s
                for fill in OWN_PREP.get(s, []):
                    prep(base, fill, g)
                for fill in NEXT_PREP.get(s, []) if nxt else []:
                    prep(base, fill, g + 1)
                if s < NT:
                    if s == 0:
                        pe.wait_ge(prep_free, base)
                    if not (first and s < 2):
                        pe.wait_ge(p_exp, n - 1)
                    S, b = s_bank[s % 2][:, 0:GH * CTX], s // 2
                    for c in range(CH):
                        mm3(pe, S, [w[:, c, s * PART:(s + 1) * PART] for w in k.xnT],
                            [w[:, c, b, :, :] for w in k.WK], c == 0, False)
                    pe.matmul(S, k.ones[:, :], k.bqk[:, b, :, :], start=False, stop=True).then_inc(s_full, 1)
                if 2 <= s < NT + 2:
                    t = s - 2
                    pe.wait_ge(p_ready, n - 1)
                    if not (first and t == 0):
                        pe.wait_ge(pt_lo, n - 2)
                    for hp in range(2):
                        last = pe.transpose(pt_bank[:, hp * PART:(hp + 1) * PART],
                                            k.p0[:, t % 4, hp * PART:(hp + 1) * PART], k.ident[:, :])
                    last.then_inc(pt_full, 1)
                if s >= 3:
                    t = s - 3
                    pe.wait_ge(pt_lo, n - 2)
                    if t == 0:
                        pe.wait_ge(prep_free, base + FREE0)
                    if t == 4:
                        pe.wait_ge(prep_free, base + OWN)
                    if not (first and t < 2):
                        pe.wait_ge(x_done, n - 4)
                    for hp in range(2):
                        last = mm3(pe, o_bank[t % 2], [w[:, t % 2, hp * PART:(hp + 1) * PART] for w in k.pT0],
                                   [w[:, hp, t // 2, :] for w in k.VW], hp == 0, hp == 1)
                    last.then_inc(o_full, 1)
                if not nxt and s == 6:
                    pe.wait_ge(prep_free, base + OWN)
                if not nxt and s >= 6:
                    ln.pe_turn(pe, 1, s - 6, ln_bank(s - 6))

        pe.wait_ge(ctx_lo, 1)
        for fill in ORDER[OWN:]:
            prep(START, fill, 0)
        pe.wait_ge(ident, 1)
        for t in range(NT):
            ln.pe_turn(pe, 0, t, o_bank[t % 2])
        pe.wait_ge(ln.split, NT)
        body(0, True, True)
        with pe.Fori(1, NKV - 1) as g:
            body(g, False, True)
        body(NKV - 1, False, False)
        for t in range(NT - 3, NT):
            ln.pe_turn(pe, 1, t, ln_bank(t))

    run(nc, sync, gpsimd, vector, scalar, tensor)



def ffn0_buffers(k, scope, sb, pair):
    k.raw_gu1 = sb(scope, "raw_gu1", [CH * 2 * PART])
    k.w_gu = [pair(scope, f"w_gu{n}", [CH * 2 * PART]) for n in range(2)]
    k.w_dn = pair(scope, "w_dn", [IC, HID])
    k.hT = pair(scope, "hT", [IC, 512])
    k.f_tanh, k.f_a, k.f_h = (sb(scope, n, [2, 512]) for n in ("f_tanh", "f_a", "f_h"))


def ffn0_phase(nc, k, sem, ln):
    gu_in = [sem(f"f0_gu_in{n}") for n in range(2)]
    gu_whi, gu_wlo = sem("f0_gu_whi"), sem("f0_gu_wlo")
    dn_in = [sem(f"f0_dn_in{n}") for n in range(3)]
    dn_hi, dn_lo = sem("f0_dn_hi"), sem("f0_dn_lo")
    gu_full, tanh_done, a_done, h_done = sem("f0_gu_full"), sem("f0_tanh"), sem("f0_a"), sem("f0_h")
    h_hi, h_lo, o_full, x_done = sem("f0_h_hi"), sem("f0_h_lo"), sem("f0_o_full"), sem("f0_x_done")
    STEPS = [(half, i) for half in range(2) for i in range(IC)]
    raws = [k.raw_kv, k.raw_gu1]
    DN = [(k.raw_q, 0, 4), (k.raw_o, 4, 8), (k.raw_q, 8, 11)]
    gate_bank, up_bank, o_bank = [k.bank[0], k.bank[2]], [k.bank[1], k.bank[3]], k.bank[4:8]

    def ln_bank(j):
        return k.bank[j]

    def width(i):
        return ILAST if i == IC - 1 else PART

    def dn_slices(i0, i1):
        full = min(i1, IC - 1) - i0
        out = [(slice(0, PART), i0, full)]
        if i1 == IC:
            out.append((slice(0, ILAST), IC - 1, 1))
        return out

    with nc.Block() as block:
        @block.sync
        def _(sp):
            def gu(n):
                _, i = STEPS[n]
                w = CH * 2 * width(i)
                if n >= 2:
                    sp.wait_ge(gu_wlo, n - 1)
                sp.dma_start(raws[n % 2][:, 0:w], k.d["w_gu"][:, i * 1024:i * 1024 + w]).then_inc(gu_in[n % 2], 16)

            def dn(j):
                raw, i0, i1 = DN[j]
                if j == 2:
                    sp.wait_ge(dn_lo, 4)
                for rows, i, n in dn_slices(i0, i1):
                    src = k.d["w_down"][i * PART:i * PART + rows.stop * n, :].rearrange("(n p) c -> p n c", n=n)
                    dst = raw[rows, (i - i0) * HID:(i - i0 + n) * HID].rearrange("p (n c) -> p n c", n=n)
                    sp.dma_start(dst, src).then_inc(dn_in[j], 16)

            gu(0)
            gu(1)
            dn(0)
            dn(1)
            for n in range(2, len(STEPS)):
                gu(n)
                if n == 6:
                    dn(2)

        @block.gpsimd
        def _(pool):
            def w_lo(n):
                w = CH * 2 * width(STEPS[n][1])
                pool.wait_ge(gu_whi, n + 1)
                pool.tensor_tensor(k.w_gu[n % 2][1][:, 0:w], raws[n % 2][:, 0:w], f(k.w_gu[n % 2][0][:, 0:w]),
                                   ALU.subtract).then_inc(gu_wlo, 1)

            def dn(i):
                j, p = i // 4, slice(0, width(i))
                raw, i0, _ = DN[j]
                pool.wait_ge(dn_hi, j + 1)
                pool.tensor_tensor(k.w_dn[1][p, i, :], raw[p, (i - i0) * HID:(i - i0 + 1) * HID],
                                   f(k.w_dn[0][p, i, :]), ALU.subtract).then_inc(dn_lo, 1)

            w_lo(0)
            w_lo(1)
            for n, (half, i) in enumerate(STEPS):
                if n + 2 < len(STEPS):
                    w_lo(n + 2)
                if n < IC - 1:
                    dn(n)
                if n == IC - 2:
                    dn(IC - 1)
                p = slice(0, width(i))
                pool.wait_ge(h_hi, n + 1)
                pool.tensor_tensor(k.hT[1][p, i, :], k.f_h[p, n % 2, :], f(k.hT[0][p, i, :]), ALU.subtract).then_inc(h_lo, 1)
                if IC + 1 <= n < IC + 5:
                    ln.pool_rstd(pool, 2, n - IC - 1)
            for t in range(4, NT):
                ln.pool_rstd(pool, 2, t)

        @block.vector
        def _(dve):
            def w_hi(n):
                w = CH * 2 * width(STEPS[n][1])
                dve.wait_ge(gu_in[n % 2], 16 * (n // 2 + 1))
                if n >= 2:
                    dve.wait_ge(gu_full, n - 1)
                dve.tensor_copy(k.w_gu[n % 2][0][:, 0:w], raws[n % 2][:, 0:w]).then_inc(gu_whi, 1)

            def dn(j):
                raw, i0, i1 = DN[j]
                dve.wait_ge(dn_in[j], 16 * len(dn_slices(i0, i1)))
                for rows, i, n in dn_slices(i0, i1):
                    last = dve.tensor_copy(k.w_dn[0][rows, i:i + n, :],
                                           raw[rows, (i - i0) * HID:(i - i0 + n) * HID].rearrange("p (n c) -> p n c", n=n))
                last.then_inc(dn_hi, 1)

            w_hi(0)
            w_hi(1)
            for n, (half, i) in enumerate(STEPS):
                if n + 2 < len(STEPS):
                    w_hi(n + 2)
                if n in (0, 2, 6):
                    dn({0: 0, 2: 1, 6: 2}[n])
                p, s = slice(0, width(i)), n % 2
                dve.wait_ge(tanh_done, n + 1)
                dve.scalar_tensor_tensor(out=k.f_a[p, s, :], in0=k.f_tanh[p, s, :], scalar=1.0, in1=gate_bank[s][p, :],
                                         op0=ALU.add, op1=ALU.mult).then_inc(a_done, 1)
                dve.wait_ge(a_done, n + 1)
                if n >= 2:
                    dve.wait_ge(h_lo, n - 1)
                dve.scalar_tensor_tensor(out=k.f_h[p, s, :], in0=k.f_a[p, s, :], scalar=0.5, in1=up_bank[s][p, :],
                                         op0=ALU.mult, op1=ALU.mult).then_inc(h_done, 1)
                if IC + 1 <= n < IC + 5:
                    ln.dve_stats(dve, 2, n - IC - 1)
                if IC + 2 <= n < IC + 6:
                    ln.dve_norm(dve, 2, n - IC - 2)
                if IC + 3 <= n < IC + 7:
                    ln.dve_lo(dve, 2, n - IC - 3, o_bank[n - IC - 3])
                if i == IC - 1:
                    for j in range(4):
                        dve.wait_ge(o_full, 4 * half + j + 1)
                        t = 4 * half + j
                        dve.scalar_tensor_tensor(out=k.x[:, t, :], in0=o_bank[j][:, :], scalar=k.gate[:, 2:3],
                                                 in1=k.x[:, t, :], op0=ALU.mult, op1=ALU.add).then_inc(x_done, 1)
                        dve.wait_ge(x_done, t + 1)
                        if half == 1:
                            ln.dve_stats(dve, 2, t)
                            ln.dve_norm(dve, 2, t)
                            if j >= 1:
                                ln.dve_lo(dve, 2, t - 1, ln_bank(j - 1))
            ln.dve_lo(dve, 2, NT - 1, ln_bank(3))

        @block.scalar
        def _(act):
            def hi(n):
                half, i = STEPS[n]
                p = slice(0, width(i))
                act.wait_ge(h_done, n + 1)
                act.activation(k.hT[0][p, i, :], k.f_h[p, n % 2, :], ACT.Copy).then_inc(h_hi, 1)

            for n, (half, i) in enumerate(STEPS):
                p = slice(0, width(i))
                act.wait_ge(gu_full, n + 1)
                act.activation(k.f_tanh[p, n % 2, :], gate_bank[n % 2][p, :], ACT.Tanh, scale=0.5).then_inc(tanh_done, 1)
                hi(n)
                if IC + 3 <= n < IC + 7:
                    ln.act_hi(act, 2, n - IC - 3, o_bank[n - IC - 3])
            for j in range(4):
                ln.act_hi(act, 2, 4 + j, ln_bank(j))

        @block.tensor
        def _(pe):
            for n, (half, i) in enumerate(STEPS):
                w, s = width(i), n % 2
                pe.wait_ge(gu_wlo, n + 1)
                if n >= 2:
                    pe.wait_ge(h_done, n - 1)
                wg = [v[:, 0:CH * 2 * w].rearrange("p (c n) -> p c n", c=CH) for v in k.w_gu[s]]
                for j, bank in enumerate((gate_bank[s], up_bank[s])):
                    for c in range(CH):
                        last = mm3(pe, bank[0:w, :], [v[:, c, j * w:(j + 1) * w] for v in wg],
                                   [v[:, c, half * 512:(half + 1) * 512] for v in k.xnT], c == 0, c == CH - 1)
                last.then_inc(gu_full, 1)
                if IC + 3 <= n < IC + 7:
                    ln.pe_turn(pe, 2, n - IC - 3, o_bank[n - IC - 3])
                if i == IC - 1:
                    if half == 0:
                        pe.wait_ge(dn_lo, IC)
                    for j in range(4):
                        if half == 1:
                            pe.wait_ge(ln.split, 2 * NT + j + 1)
                        for m in range(IC):
                            p = slice(0, width(m))
                            if j == 0:
                                pe.wait_ge(h_lo, IC * half + m + 1)
                            last = mm3(pe, o_bank[j][:, :], [v[p, m, j * PART:(j + 1) * PART] for v in k.hT],
                                       [v[p, m, :] for v in k.w_dn], m == 0, m == IC - 1)
                        last.then_inc(o_full, 1)
                        if half == 1 and j >= 1:
                            if j == 1:
                                pe.wait_ge(h_done, len(STEPS))
                            ln.pe_turn(pe, 2, 3 + j, ln_bank(j - 1))
            ln.pe_turn(pe, 2, NT - 1, ln_bank(3))


def attn1_buffers(k, scope, sb, pair):
    k.w_q, k.w_kv, k.w_o = pair(scope, "w1q", [CH, GH * HD]), pair(scope, "w1kv", [CH, 2 * HD]), pair(scope, "w1o", [GH, HID])
    k.qT = pair(scope, "qT1", [2, GH, PART])
    k.kT = pair(scope, "kT1", [BATCH, SEQ + CTX])
    k.v = pair(scope, "v1", [BATCH, 3, HD])
    k.pT = pair(scope, "pT1", [3, GH, SEQ])
    k.oT = pair(scope, "oT1", [GH, SEQ])
    k.q_raw, k.k_raw = sb(scope, "q_raw", [2, GH * HD]), sb(scope, "k_raw", [3, HD])
    k.p1 = sb(scope, "p1", [2, GH, SEQ + CTX])
    k.dump, k.rms_eps = sb(scope, "dump", [2 * GH + 3, HD]), sb(scope, "rms_eps", [2 * GH])
    k.ssk, k.rk = sb(scope, "ssk", [3]), sb(scope, "rk", [3])
    k.ssq, k.rq, k.mx, k.nb, k.rs, k.rinv = (sb(scope, n, [2 * GH]) for n in ("ssq", "rq", "mx", "nb", "rs", "rinv"))


def attn1_phase(nc, k, sem, ln):
    def sems(*names):
        return [sem("a1_" + n) for n in names]

    q_in, kv_in, o_in, q_whi, kv_whi, o_whi, q_wlo, kv_wlo, o_wlo = sems(
        "q_in", "kv_in", "o_in", "q_whi", "kv_whi", "o_whi", "q_wlo", "kv_wlo", "o_wlo")
    kv_full, kv_hi, kv_split, cx_full, cx_hi, cx_split = sems("kv_full", "kv_hi", "kv_split", "cx_full", "cx_hi", "cx_split")
    q_full, q_copied, pv_full, pv_hi, pv_split, d_full, x_added = sems(
        "q_full", "q_copied", "pv_full", "pv_hi", "pv_split", "d_full", "x_added")
    t_full, t_hi, t_split, kt_full, kt_hi, kt_split, qt_full, qt_hi, qt_split = sems(
        "t_full", "t_hi", "t_split", "kt_full", "kt_hi", "kt_split", "qt_full", "qt_hi", "qt_split")
    ssk_ready, rk_ms, rk_ready, k_scaled, ssq_ready, rq_ms, rq_ready = sems(
        "ssk", "rk_ms", "rk", "k_scaled", "ssq", "rq_ms", "rq")
    s_full, mx_ready, nb_ready, exp_done, rinv_ready, p_scaled, pad_zero = sems(
        "s_full", "mx", "nb", "exp", "rinv", "p_scaled", "pad_zero")

    CONV = {"kv": 2, "q": 4, "o": 4}
    KEYS, UNITS = SEQ + CTX, NKV * BATCH
    bx, by = k.bank[4:6], k.bank[6:8]
    PAIRS = [(0, 0), (0, 1), (1, 0), (1, 1)]
    ctx4 = [w[:, :].rearrange("p (c n) -> p c n", c=CH) for w in k.ctxT]
    flat = {"kv": [w[:, :, :].rearrange("p a b -> p (a b)") for w in k.w_kv],
            "q": [w[:, :, :].rearrange("p a b -> p (a b)") for w in k.w_q],
            "o": [w[:, :, :].rearrange("p a b -> p (a b)") for w in k.w_o]}
    cols = {"kv": CH * 2 * HD, "q": CH * GH * HD, "o": GH * HID}
    raw = {"kv": k.raw_kv, "q": k.raw_q, "o": k.raw_o}
    arrived = {"kv": kv_in, "q": q_in, "o": o_in}
    whi, wlo = {"kv": kv_whi, "q": q_whi, "o": o_whi}, {"kv": kv_wlo, "q": q_wlo, "o": o_wlo}

    def y_start(b):
        return (0, 8, 15, 23)[b]

    def y_bank(b, kind, j=0):
        order = ["kv"] + (["cx"] if b % 2 == 0 else []) + ["q0", "q1", "pv0", "pv1", "d0", "d1"]
        name = kind if kind in ("kv", "cx") else f"{kind}{j}"
        return by[(y_start(b) + order.index(name)) % 2]

    def x_bank(b, kind, j=0):
        at = {"t": j, "k": 6, "q": 7 + j}[kind]
        return bx[(9 * b + at) % 2]

    def ln_bank(b, i):
        return bx[(9 * b + 1 + i) % 2] if b < BATCH else bx[i]

    def s_pair(j):
        return k.psum[:, (j % 2) * 1024:(j % 2) * 1024 + 1024].rearrange("p (h n) -> p h n", h=2)[:, :, 0:KEYS]

    def stat(j):
        tile, hp = PAIRS[j]
        return slice(tile * GH + 2 * hp, tile * GH + 2 * hp + 2)

    def loop(eng, body, tail):
        body(0, True, True)
        with eng.Fori(1, NKV - 1) as g:
            body(g, False, True)
        body(NKV - 1, False, False)
        tail(NKV * BATCH)

    with nc.Block() as block:
        @block.sync
        def _(sp):
            for kind, src in (("kv", "w1kv"), ("q", "w1q"), ("o", "w1o")):
                sp.dma_start(raw[kind][:, 0:cols[kind]], k.d[src][0:PART, :]).then_inc(arrived[kind], 16)
            with sp.Fori(1, NKV) as g:
                for kind, src in (("o", "w1o"), ("kv", "w1kv"), ("q", "w1q")):
                    sp.wait_ge(wlo[kind], g * CONV[kind])
                    sp.dma_start(raw[kind][:, 0:cols[kind]], k.d[src][bass.ts(g, PART), :]).then_inc(arrived[kind], 16)

        @block.gpsimd
        def _(pool):
            def w_lo(kind, g):
                n = cols[kind] // CONV[kind]
                pool.wait_ge(whi[kind], g + 1)
                for i in range(CONV[kind]):
                    s = slice(i * n, (i + 1) * n)
                    pool.tensor_tensor(flat[kind][1][:, s], raw[kind][:, s], f(flat[kind][0][:, s]),
                                       ALU.subtract).then_inc(wlo[kind], 1)

            def body(g, first, nxt):
                for b in range(BATCH):
                    n = BATCH * g + b
                    pool.wait_ge(ssk_ready, n + 1)
                    pool.tensor_tensor(k.rk[:, :], k.ssk[:, :], k.rms_eps[:, 0:3], ALU.add).then_inc(rk_ms, 1)
                    pool.wait_ge(rk_ms, n + 1)
                    pool.tensor_tensor(k.rk[:, :], k.rk[:, :], k.minus_half[:, 0:3], ALU.pow).then_inc(rk_ready, 1)
                    if not nxt and b >= 2:
                        ln.pool_rstd(pool, 3, 2 * b - 4)
                        ln.pool_rstd(pool, 3, 2 * b - 3)
                    if b == 1:
                        w_lo("o", g)
                    pool.wait_ge(ssq_ready, n + 1)
                    pool.tensor_tensor(k.rq[:, :], k.ssq[:, :], k.rms_eps[:, :], ALU.add).then_inc(rq_ms, 1)
                    pool.wait_ge(rq_ms, n + 1)
                    pool.tensor_tensor(k.rq[:, :], k.rq[:, :], k.minus_half[:, 0:8], ALU.pow).then_inc(rq_ready, 1)
                    if b == BATCH - 1 and nxt:
                        w_lo("kv", g + 1)
                        w_lo("q", g + 1)

            pool.memset(f(k.v[0][64:PART, :, 2, :]), 0.0)
            pool.memset(f(k.v[1][64:PART, :, 2, :]), 0.0)
            pool.memset(f(k.pT[0][64:PART, 2, :, :]), 0.0)
            pool.memset(f(k.pT[1][64:PART, 2, :, :]), 0.0).then_inc(pad_zero, 1)
            pool.wait_ge(pad_zero, 1)
            pool.memset(k.rms_eps[:, :], HD * RMS_EPS)
            pool.memset(k.ssk[:, :], 1.0).then_inc(pad_zero, 1)
            w_lo("kv", 0)
            w_lo("q", 0)
            loop(pool, body, lambda n: [ln.pool_rstd(pool, 3, t) for t in range(4, NT)])

        @block.vector
        def _(dve):
            def w_hi(kind, g):
                dve.wait_ge(arrived[kind], 16 * g + 16)
                dve.tensor_copy(flat[kind][0][:, :], raw[kind][:, 0:cols[kind]]).then_inc(whi[kind], 1)

            def t_lo(n, b, j):
                hp, kt = divmod(j, 3)
                p = slice(0, 64 if kt == 2 else PART)
                dve.wait_ge(t_hi, 6 * (n - 1) + j + 1)
                dve.tensor_tensor(k.pT[1][p, kt, 2 * hp:2 * hp + 2, :],
                                  x_bank(b, "t", j)[p, :].rearrange("p (h q) -> p h q", h=2),
                                  f(k.pT[0][p, kt, 2 * hp:2 * hp + 2, :]), ALU.subtract).then_inc(t_split, 1)

            def pv_lo(n, b, hp):
                dve.wait_ge(pv_hi, 2 * (n - 1) + hp + 1)
                dve.tensor_tensor(k.oT[1][:, 2 * hp:2 * hp + 2, :],
                                  y_bank(b, "pv", hp)[:, :].rearrange("p (h q) -> p h q", h=2),
                                  f(k.oT[0][:, 2 * hp:2 * hp + 2, :]), ALU.subtract).then_inc(pv_split, 1)

            def x_add(n, b, j):
                t = 2 * ((b - 1) % BATCH) + j
                dve.wait_ge(d_full, 2 * (n - 1) + j + 1)
                dve.scalar_tensor_tensor(out=k.x[:, t, :], in0=y_bank(b, "d", j)[:, :], scalar=k.gate[:, 1:2],
                                         in1=k.x[:, t, :], op0=ALU.mult, op1=ALU.add).then_inc(x_added, 1)

            def q_squares(n, b, tile):
                dve.wait_ge(q_copied, 2 * n + tile + 1)
                for h in range(GH):
                    q = k.q_raw[:, tile, h * HD:(h + 1) * HD]
                    last = dve.tensor_tensor_reduce(k.dump[:, tile * GH + h, :], q, q, 1.0, 0.0, ALU.mult, ALU.add,
                                                    k.ssq[:, tile * GH + h:tile * GH + h + 1])
                if tile == 1:
                    last.then_inc(ssq_ready, 1)

            def row_max(n, j):
                dve.wait_ge(s_full, 4 * n + j + 1)
                dve.tensor_reduce(k.mx[:, stat(j)], s_pair(j), AX.X, ALU.max).then_inc(mx_ready, 1)
                if j == 0:
                    dve.wait_ge(rq_ready, n + 1)
                dve.wait_ge(mx_ready, 4 * n + j + 1)
                dve.scalar_tensor_tensor(out=k.nb[:, stat(j)], in0=k.mx[:, stat(j)], scalar=-1.0, in1=k.rq[:, stat(j)],
                                         op0=ALU.mult, op1=ALU.mult).then_inc(nb_ready, 1)

            def scale_p(n, j):
                tile, hp = PAIRS[j]
                dve.wait_ge(exp_done, 4 * n + j + 1)
                dve.reciprocal(k.rinv[:, stat(j)], k.rs[:, stat(j)]).then_inc(rinv_ready, 1)
                dve.wait_ge(rinv_ready, 4 * n + j + 1)
                for h in (2 * hp, 2 * hp + 1):
                    last = dve.tensor_scalar(k.p1[:, tile, h, :], k.p1[:, tile, h, :],
                                             k.rinv[:, tile * GH + h:tile * GH + h + 1], None, ALU.mult)
                last.then_inc(p_scaled, 1)

            def body(g, first, nxt):
                for b in range(BATCH):
                    n, prev = BATCH * g + b, not (first and b == 0)
                    dve.wait_ge(kv_hi, n + 1)
                    bank = y_bank(b, "kv")[:, :].rearrange("p (t n) -> p t n", t=2)
                    dve.tensor_tensor(k.v[1][:, b, 0:2, :], bank[:, :, HD:2 * HD], f(k.v[0][:, b, 0:2, :]),
                                      ALU.subtract).then_inc(kv_split, 1)
                    if b % 2 == 0:
                        dve.wait_ge(cx_hi, 2 * g + b // 2 + 1)
                        for i in range(2):
                            last = dve.tensor_tensor(k.v[1][0:64, b + i, 2, :],
                                                     y_bank(b, "cx")[64 * i:64 * i + 64, HD:2 * HD],
                                                     f(k.v[0][0:64, b + i, 2, :]), ALU.subtract)
                        last.then_inc(cx_split, 1)
                    nk = 3 if b % 2 == 0 else 2
                    for i in range(nk):
                        last = dve.tensor_tensor_reduce(k.dump[:, 2 * GH + i, :], k.k_raw[:, i, :], k.k_raw[:, i, :], 1.0, 0.0,
                                                        ALU.mult, ALU.add, k.ssk[:, i:i + 1])
                    last.then_inc(ssk_ready, 1)
                    if not nxt and b >= 2:
                        ln.dve_stats(dve, 3, 2 * b - 4)
                        ln.dve_stats(dve, 3, 2 * b - 3)
                    if prev:
                        t_lo(n, b, 0)
                        t_lo(n, b, 1)
                    dve.wait_ge(rk_ready, n + 1)
                    for i in range(nk):
                        last = dve.tensor_scalar(k.k_raw[:, i, :], k.k_raw[:, i, :], k.rk[:, i:i + 1], None, ALU.mult)
                    last.then_inc(k_scaled, 1)
                    q_squares(n, b, 0)
                    if prev:
                        t_lo(n, b, 2)
                        t_lo(n, b, 3)
                    q_squares(n, b, 1)
                    if prev:
                        t_lo(n, b, 4)
                        t_lo(n, b, 5)
                        pv_lo(n, b, 0)
                    if not nxt and b >= 2:
                        ln.dve_norm(dve, 3, 2 * b - 4)
                        ln.dve_norm(dve, 3, 2 * b - 3)
                    dve.wait_ge(kt_hi, n + 1)
                    bank = x_bank(b, "k")
                    last = dve.scalar_tensor_tensor(out=k.kT[1][:, b, 0:SEQ], in0=bank[:, 0:SEQ], scalar=k.qkw[:, 0:1],
                                                    in1=f(k.kT[0][:, b, 0:SEQ]), op0=ALU.mult, op1=ALU.subtract)
                    if b % 2 == 0:
                        last = dve.scalar_tensor_tensor(
                            out=k.kT[1][:, b:b + 2, SEQ:KEYS], in0=bank[:, SEQ:SEQ + 128].rearrange("p (b k) -> p b k", b=2),
                            scalar=k.qkw[:, 0:1], in1=f(k.kT[0][:, b:b + 2, SEQ:KEYS]), op0=ALU.mult, op1=ALU.subtract)
                    last.then_inc(kt_split, 1)
                    for tile in range(2):
                        dve.wait_ge(qt_hi, 2 * n + tile + 1)
                        dve.tensor_tensor(k.qT[1][:, tile, :, :],
                                          x_bank(b, "q", tile)[:, :].rearrange("p (h q) -> p h q", h=GH),
                                          f(k.qT[0][:, tile, :, :]), ALU.subtract).then_inc(qt_split, 1)
                        if prev and tile == 0:
                            pv_lo(n, b, 1)
                    if b == BATCH - 1 and nxt:
                        w_hi("kv", g + 1)
                    row_max(n, 0)
                    row_max(n, 1)
                    scale_p(n, 0)
                    if prev:
                        x_add(n, b, 0)
                    if not nxt and b >= 2:
                        ln.dve_lo(dve, 3, 2 * b - 4, ln_bank(b, 0))
                        ln.dve_lo(dve, 3, 2 * b - 3, ln_bank(b, 1))
                    row_max(n, 2)
                    if b == BATCH - 1 and nxt:
                        w_hi("q", g + 1)
                    scale_p(n, 1)
                    if prev:
                        x_add(n, b, 1)
                    row_max(n, 3)
                    scale_p(n, 2)
                    scale_p(n, 3)
                    if b == 0:
                        w_hi("o", g)

            def tail(n):
                ln.dve_stats(dve, 3, 4)
                ln.dve_stats(dve, 3, 5)
                for j in range(6):
                    t_lo(n, 0, j)
                ln.dve_norm(dve, 3, 4)
                ln.dve_norm(dve, 3, 5)
                for hp in range(2):
                    pv_lo(n, 0, hp)
                for i in range(2):
                    ln.dve_lo(dve, 3, 4 + i, ln_bank(4, i))
                for j in range(2):
                    x_add(n, 0, j)
                    dve.wait_ge(x_added, 2 * (n - 1) + j + 1)
                    ln.dve_stats(dve, 3, 6 + j)
                for j in range(2):
                    ln.dve_norm(dve, 3, 6 + j)
                for j in range(2):
                    ln.dve_lo(dve, 3, 6 + j, ln_bank(4, j))

            dve.wait_ge(pad_zero, 2)
            w_hi("kv", 0)
            w_hi("q", 0)
            loop(dve, body, tail)

        @block.scalar
        def _(act):
            def t_evac(n, b, j):
                hp, kt = divmod(j, 3)
                p = slice(0, 64 if kt == 2 else PART)
                act.wait_ge(t_full, 6 * (n - 1) + j + 1)
                act.activation(k.pT[0][p, kt, 2 * hp:2 * hp + 2, :],
                               x_bank(b, "t", j)[p, :].rearrange("p (h q) -> p h q", h=2), ACT.Copy).then_inc(t_hi, 1)

            def pv_evac(n, b, hp):
                act.wait_ge(pv_full, 2 * (n - 1) + hp + 1)
                act.activation(k.oT[0][:, 2 * hp:2 * hp + 2, :],
                               y_bank(b, "pv", hp)[:, :].rearrange("p (h q) -> p h q", h=2), ACT.Copy).then_inc(pv_hi, 1)

            def body(g, first, nxt):
                for b in range(BATCH):
                    n, prev = BATCH * g + b, not (first and b == 0)
                    act.wait_ge(kv_full, n + 1)
                    bank = y_bank(b, "kv")[:, :].rearrange("p (t n) -> p t n", t=2)
                    act.activation(k.k_raw[:, 0:2, :], bank[:, :, 0:HD], ACT.Copy)
                    act.activation(k.v[0][:, b, 0:2, :], bank[:, :, HD:2 * HD], ACT.Copy).then_inc(kv_hi, 1)
                    if b % 2 == 0:
                        act.wait_ge(cx_full, 2 * g + b // 2 + 1)
                        act.activation(k.k_raw[:, 2, :], y_bank(b, "cx")[:, 0:HD], ACT.Copy)
                        for i in range(2):
                            last = act.activation(k.v[0][0:64, b + i, 2, :],
                                                  y_bank(b, "cx")[64 * i:64 * i + 64, HD:2 * HD], ACT.Copy)
                        last.then_inc(cx_hi, 1)
                    for j in range(6):
                        if prev:
                            t_evac(n, b, j)
                            if j == 5:
                                pv_evac(n, b, 0)
                        if j in (1, 3):
                            act.wait_ge(q_full, 2 * n + j // 2 + 1)
                            act.activation(k.q_raw[:, j // 2, :], y_bank(b, "q", j // 2)[:, :], ACT.Copy)\
                               .then_inc(q_copied, 1)
                    act.wait_ge(kt_full, n + 1)
                    bank = x_bank(b, "k")
                    last = act.activation(k.kT[0][:, b, 0:SEQ], bank[:, 0:SEQ], ACT.Copy, scale=k.qkw[:, 0:1])
                    if b % 2 == 0:
                        last = act.activation(k.kT[0][:, b:b + 2, SEQ:KEYS],
                                              bank[:, SEQ:SEQ + 128].rearrange("p (b k) -> p b k", b=2),
                                              ACT.Copy, scale=k.qkw[:, 0:1])
                    last.then_inc(kt_hi, 1)
                    for tile in range(2):
                        act.wait_ge(qt_full, 2 * n + tile + 1)
                        act.activation(k.qT[0][:, tile, :, :],
                                       x_bank(b, "q", tile)[:, :].rearrange("p (h q) -> p h q", h=GH),
                                       ACT.Copy).then_inc(qt_hi, 1)
                        if prev and tile == 0:
                            pv_evac(n, b, 1)
                    for j, (tile, hp) in enumerate(PAIRS):
                        act.wait_ge(nb_ready, 4 * n + j + 1)
                        for h in (2 * hp, 2 * hp + 1):
                            i = tile * GH + h
                            last = act.activation(k.p1[:, tile, h, :], s_pair(j)[:, h % 2, :], ACT.Exp,
                                                  bias=k.nb[:, i:i + 1], scale=k.rq[:, i:i + 1],
                                                  accum_out=k.rs[:, i:i + 1])
                        last.then_inc(exp_done, 1)
                        if j == 1 and not nxt and b >= 2:
                            ln.act_hi(act, 3, 2 * b - 4, ln_bank(b, 0))
                            ln.act_hi(act, 3, 2 * b - 3, ln_bank(b, 1))

            def tail(n):
                for j in range(6):
                    t_evac(n, 0, j)
                for hp in range(2):
                    pv_evac(n, 0, hp)
                for t in range(4, NT):
                    ln.act_hi(act, 3, t, ln_bank(4, t % 2))

            act.wait_ge(pad_zero, 2)
            loop(act, body, tail)

        @block.tensor
        def _(pe):
            def turn(n, b, j, alone=False):
                hp, kt = divmod(j, 3)
                if kt == 0:
                    pe.wait_ge(p_scaled, 4 * (n - 1) + 3 + hp)
                if isinstance(n, int) and n >= UNITS - 1 and j < 2:
                    pe.wait_ge(ln.split, NT * 3 + 2 * (n - UNITS + 1) + j + 1)
                elif j < 2:
                    pe.wait_ge(qt_split, 2 * n - 1 + j)
                elif j == 4:
                    pe.wait_ge(t_split, 6 * (n - 1) + 4)
                elif j == 3 or alone and j == 2:
                    pe.wait_ge(t_split, 6 * (n - 1) + j - 1)
                rows = 64 if kt == 2 else PART
                for hh in range(2):
                    for tile in range(2):
                        last = pe.transpose(x_bank(b, "t", j)[0:rows, (2 * hh + tile) * PART:(2 * hh + tile + 1) * PART],
                                            k.p1[:, tile, 2 * hp + hh, kt * PART:kt * PART + rows], k.ident[:, :])
                last.then_inc(t_full, 1)

            def p_v(n, b, hp, alone=False):
                pb = (b - 1) % BATCH
                pe.wait_ge(t_split, 6 * (n - 1) + 3 * (hp + 1))
                if not alone:
                    pe.wait_ge(q_copied, 2 * n + hp + 1)
                for kt in range(3):
                    last = mm3(pe, y_bank(b, "pv", hp)[:, :], [w[:, pb, kt, :] for w in k.v],
                               [w[:, kt, 2 * hp:2 * hp + 2, :] for w in k.pT], kt == 0, kt == 2)
                last.then_inc(pv_full, 1)

            def out(n, b, j):
                pe.wait_ge(pv_split, 2 * n)
                for h in range(GH):
                    last = mm3(pe, y_bank(b, "d", j)[:, :], [w[:, h, j * PART:(j + 1) * PART] for w in k.oT],
                               [w[:, h, :] for w in k.w_o], h == 0, h == GH - 1)
                last.then_inc(d_full, 1)

            def scores(n, b, j):
                tile, hp = PAIRS[j]
                if j == 0:
                    pe.wait_ge(kt_split, n + 1)
                if hp == 0:
                    pe.wait_ge(qt_split, 2 * n + tile + 1)
                if not (isinstance(n, int) and 4 * n + j < 2):
                    pe.wait_ge(exp_done, 4 * n + j - 1)
                for hh in range(2):
                    last = mm3(pe, s_pair(j)[:, hh, :], [w[:, tile, 2 * hp + hh, :] for w in k.qT],
                               [w[:, b, :] for w in k.kT], True, True)
                last.then_inc(s_full, 1)

            def body(g, first, nxt):
                for b in range(BATCH):
                    n, prev = BATCH * g + b, not (first and b == 0)
                    deep = not (first and b < 2)
                    if b == 0:
                        pe.wait_ge(kv_wlo, CONV["kv"] * (g + 1))
                    if deep:
                        pe.wait_ge(x_added, 2 * (n - 2) + 1)
                    for tile in range(2):
                        t = 2 * b + tile
                        for c in range(CH):
                            last = mm3(pe, y_bank(b, "kv")[:, tile * 256:tile * 256 + 256],
                                       [w[:, c, t * PART:(t + 1) * PART] for w in k.xnT],
                                       [w[:, c, :] for w in k.w_kv], c == 0, c == CH - 1)
                    last.then_inc(kv_full, 1)
                    if deep:
                        pe.wait_ge(x_added, 2 * (n - 2) + 2)
                    if b % 2 == 0:
                        for c in range(CH):
                            last = mm3(pe, y_bank(b, "cx")[:, 0:256], [w[:, c, b * CTX:(b + 2) * CTX] for w in ctx4],
                                       [w[:, c, :] for w in k.w_kv], c == 0, c == CH - 1)
                        last.then_inc(cx_full, 1)
                    if b == 0:
                        pe.wait_ge(q_wlo, CONV["q"] * (g + 1))
                    for tile in range(2):
                        if prev:
                            turn(n, b, 2 * tile)
                            turn(n, b, 2 * tile + 1)
                        if b % 2 == 0:
                            pe.wait_ge(kv_split if tile == 0 else cx_split, n + 1 if tile == 0 else 2 * g + b // 2 + 1)
                        elif tile == 1:
                            pe.wait_ge(kv_split, n + 1)
                        t = 2 * b + tile
                        for c in range(CH):
                            if prev and tile == 0 and c == CH - 1:
                                pe.wait_ge(t_split, 6 * (n - 1) + 1)
                            last = mm3(pe, y_bank(b, "q", tile)[:, :], [w[:, c, t * PART:(t + 1) * PART] for w in k.xnT],
                                       [w[:, c, :] for w in k.w_q], c == 0, c == CH - 1)
                        last.then_inc(q_full, 1)
                    if prev:
                        turn(n, b, 4)
                        turn(n, b, 5)
                        p_v(n, b, 0)
                        pe.wait_ge(t_split, 6 * (n - 1) + 5)
                    pe.wait_ge(k_scaled, n + 1)
                    nk = 3 if b % 2 == 0 else 2
                    for i in range(nk):
                        last = pe.transpose(x_bank(b, "k")[:, i * PART:(i + 1) * PART], k.k_raw[:, i, :], k.ident[:, :])
                    last.then_inc(kt_full, 1)
                    for tile in range(2):
                        pe.wait_ge(q_copied, 2 * n + tile + 1)
                        if tile == 1:
                            pe.wait_ge(kt_split, n + 1)
                        elif prev:
                            pe.wait_ge(t_split, 6 * n)
                        for h in range(GH):
                            last = pe.transpose(x_bank(b, "q", tile)[:, h * PART:(h + 1) * PART],
                                                k.q_raw[:, tile, h * HD:(h + 1) * HD], k.ident[:, :])
                        last.then_inc(qt_full, 1)
                        if prev and tile == 0:
                            p_v(n, b, 1)
                    scores(n, b, 0)
                    scores(n, b, 1)
                    if not nxt and b >= 2:
                        pe.wait_ge(qt_split, 2 * n + 2)
                        ln.pe_turn(pe, 3, 2 * b - 4, ln_bank(b, 0))
                        ln.pe_turn(pe, 3, 2 * b - 3, ln_bank(b, 1))
                    if prev:
                        if b == 1:
                            pe.wait_ge(o_wlo, CONV["o"] * (g + 1))
                        out(n, b, 0)
                    scores(n, b, 2)
                    if prev:
                        out(n, b, 1)
                    scores(n, b, 3)

            def tail(n):
                for j in range(6):
                    turn(n, 0, j, alone=True)
                pe.wait_ge(x_added, 2 * (n - 1))
                for hp in range(2):
                    p_v(n, 0, hp, alone=True)
                for i in range(2):
                    ln.pe_turn(pe, 3, 4 + i, ln_bank(4, i))
                for j in range(2):
                    out(n, 0, j)
                for i in range(2):
                    ln.pe_turn(pe, 3, 6 + i, ln_bank(4, i))

            pe.wait_ge(pad_zero, 2)
            loop(pe, body, tail)


def ffn1_buffers(k, scope, sb, pair):
    k.w_base, k.w_ag, k.w_b = pair(scope, "w_base", [CH, HID]), pair(scope, "w_ag", [CH, 256]), pair(scope, "w_b", [2, HID])
    k.ag = sb(scope, "ag", [2, 256])
    k.top, k.idx, k.idxf = sb(scope, "top", [2, 8]), sb(scope, "idx", [2, 8], mybir.dt.uint32), sb(scope, "idxf", [2, 2])
    k.iota_i, k.iota = sb(scope, "iota_i", [NEXP], mybir.dt.int32), sb(scope, "iota", [NEXP])
    k.gap, k.eg, k.pr = sb(scope, "gap", [2, 1]), sb(scope, "eg", [2, 1]), sb(scope, "pr", [2, 4])
    k.ga, k.gb, k.gm = (sb(scope, n, [2, NEXP]) for n in ("ga", "gb", "gm"))
    k.hg = sb(scope, "hg", [2, LR])
    k.hgT = pair(scope, "hgT", [2, 2, PART])


def ffn1_phase(nc, k, sem):
    def sems(*names):
        return [sem("f1_" + n) for n in names]

    w_in, b_in, ag_in, base_hi, ag_hi, b_hi, w_lo, pad = sems("w_in", "b_in", "ag_in", "base_hi", "ag_hi", "b_hi", "w_lo", "pad")
    ag_full, ag_out, o_full, t_full, t_hi, t_lo, x_done, stored = sems(
        "ag_full", "ag_out", "o_full", "t_full", "t_hi", "t_lo", "x_done", "stored")
    route, t_gap, exp_done, hg_done, iota_i = sems("route", "gap", "exp", "hg", "iota_i")
    R1 = LR - PART
    o_bank, ag_bank, t_bank = k.bank[0:3], k.bank[3:5], k.bank[5:7]

    with nc.Block() as block:
        @block.sync
        def _(sp):
            sp.dma_start(k.raw_kv[:, 0:CH * (LR + NEXP)], k.d["w_ag"]).then_inc(ag_in, 16)
            sp.dma_start(k.raw_q[:, :], k.d["w_base"]).then_inc(w_in, 16)
            sp.dma_start(k.raw_o[:, 0:HID], k.d["w_b"][0:PART, :]).then_inc(b_in, 16)
            sp.dma_start(k.raw_o[0:R1, HID:2 * HID], k.d["w_b"][PART:LR, :]).then_inc(b_in, 16)
            for t in range(NT):
                sp.wait_ge(x_done, t + 1)
                sp.dma_start(k.out[t * PART:(t + 1) * PART, :], k.x[:, t, :]).then_inc(stored, 16)
            sp.wait_ge(stored, 16 * NT)

        raw_ag = k.raw_kv[:, 0:CH * (LR + NEXP)].rearrange("p (c n) -> p c n", c=CH)
        raw_base = k.raw_q[:, :].rearrange("p (c n) -> p c n", c=CH)

        @block.gpsimd
        def _(pool):
            pool.iota(k.iota_i[:, :], pattern=[[1, NEXP]], base=0, channel_multiplier=0).then_inc(iota_i, 1)
            for w in k.w_ag:
                last = pool.memset(f(w[:, :, LR + NEXP:256]), 0.0)
            last.then_inc(pad, 1)
            pool.wait_ge(ag_hi, 1)
            pool.tensor_tensor(k.w_ag[1][:, :, 0:LR + NEXP], raw_ag, f(k.w_ag[0][:, :, 0:LR + NEXP]),
                               ALU.subtract).then_inc(w_lo, 1)
            pool.wait_ge(base_hi, 1)
            pool.tensor_tensor(k.w_base[1][:, :, :], raw_base, f(k.w_base[0][:, :, :]), ALU.subtract).then_inc(w_lo, 1)
            pool.wait_ge(b_hi, 1)
            pool.tensor_tensor(k.w_b[1][:, 0, :], k.raw_o[:, 0:HID], f(k.w_b[0][:, 0, :]), ALU.subtract)
            pool.tensor_tensor(k.w_b[1][0:R1, 1, :], k.raw_o[0:R1, HID:2 * HID], f(k.w_b[0][0:R1, 1, :]),
                               ALU.subtract).then_inc(w_lo, 1)

        @block.vector
        def _(dve):
            links = [0]

            def link(ins):
                links[0] += 1
                ins.then_inc(route, 1)
                dve.wait_ge(route, links[0])

            dve.wait_ge(ag_in, 16)
            dve.tensor_copy(k.w_ag[0][:, :, 0:LR + NEXP], raw_ag).then_inc(ag_hi, 1)
            dve.wait_ge(w_in, 16)
            dve.tensor_copy(k.w_base[0][:, :, :], raw_base).then_inc(base_hi, 1)
            dve.wait_ge(b_in, 32)
            dve.tensor_copy(k.w_b[0][:, 0, :], k.raw_o[:, 0:HID])
            dve.tensor_copy(k.w_b[0][0:R1, 1, :], k.raw_o[0:R1, HID:2 * HID]).then_inc(b_hi, 1)
            dve.wait_ge(iota_i, 1)
            link(dve.tensor_copy(k.iota[:, :], k.iota_i[:, :]))

            for s in range(NT + 2):
                if s < NT:
                    u = s % 2
                    logits = k.ag[:, u, LR:LR + NEXP]
                    dve.wait_ge(ag_out, s + 1)
                    link(dve.max(k.top[:, u, :], logits))
                    dve.tensor_scalar(k.gap[:, u, :], k.top[:, u, 1:2], k.top[:, u, 0:1], None, ALU.subtract)\
                       .then_inc(t_gap, 1)
                    link(dve.max_index(k.idx[:, u, :], k.top[:, u, :], logits))
                    link(dve.tensor_copy(k.idxf[:, u, :], k.idx[:, u, 0:2]))
                    dve.wait_ge(exp_done, s + 1)
                    link(dve.tensor_scalar(k.pr[:, u, 0:1], k.eg[:, u, :], 1.0, 1.0 / LORA_SCALE, ALU.add, ALU.mult))
                    link(dve.reciprocal(k.pr[:, u, 1:2], k.pr[:, u, 0:1]))
                    link(dve.tensor_tensor(k.pr[:, u, 2:3], k.pr[:, u, 1:2], k.eg[:, u, :], ALU.mult))
                    dve.tensor_scalar(k.ga[:, u, :], k.iota[:, :], k.idxf[:, u, 0:1], k.pr[:, u, 1:2],
                                      ALU.is_equal, ALU.mult)
                    link(dve.tensor_scalar(k.gb[:, u, :], k.iota[:, :], k.idxf[:, u, 1:2], k.pr[:, u, 2:3],
                                           ALU.is_equal, ALU.mult))
                    link(dve.tensor_tensor(k.gm[:, u, :], k.ga[:, u, :], k.gb[:, u, :], ALU.add))
                    if s >= 2:
                        dve.wait_ge(t_full, s - 1)
                    dve.tensor_tensor(k.hg[:, u, :].rearrange("p (e r) -> p e r", r=RANK),
                                      k.ag[:, u, 0:LR].rearrange("p (e r) -> p e r", r=RANK),
                                      k.gm[:, u, :].unsqueeze(2).to_broadcast([PART, NEXP, RANK]),
                                      ALU.mult).then_inc(hg_done, 1)
                if 1 <= s <= NT:
                    u = (s - 1) % 2
                    dve.wait_ge(t_hi, s)
                    dve.tensor_tensor(k.hgT[1][:, u, 0, :], t_bank[u][:, 0:PART], f(k.hgT[0][:, u, 0, :]), ALU.subtract)
                    dve.tensor_tensor(k.hgT[1][0:R1, u, 1, :], t_bank[u][0:R1, PART:2 * PART],
                                      f(k.hgT[0][0:R1, u, 1, :]), ALU.subtract).then_inc(t_lo, 1)
                if s >= 2:
                    t = s - 2
                    dve.wait_ge(o_full, t + 1)
                    dve.scalar_tensor_tensor(out=k.x[:, t, :], in0=o_bank[t % 3][:, :], scalar=k.gate[:, 3:4],
                                             in1=k.x[:, t, :], op0=ALU.mult, op1=ALU.add).then_inc(x_done, 1)

        @block.scalar
        def _(act):
            for s in range(NT + 1):
                if s < NT:
                    act.wait_ge(ag_full, s + 1)
                    if s >= 2:
                        act.wait_ge(hg_done, s - 1)
                    act.activation(k.ag[:, s % 2, :], ag_bank[s % 2][:, 0:256], ACT.Copy).then_inc(ag_out, 1)
                    act.wait_ge(t_gap, s + 1)
                    act.activation(k.eg[:, s % 2, :], k.gap[:, s % 2, :], ACT.Exp).then_inc(exp_done, 1)
                if s >= 1:
                    u = (s - 1) % 2
                    act.wait_ge(t_full, s)
                    act.activation(k.hgT[0][:, u, 0, :], t_bank[u][:, 0:PART], ACT.Copy)
                    act.activation(k.hgT[0][0:R1, u, 1, :], t_bank[u][0:R1, PART:2 * PART], ACT.Copy).then_inc(t_hi, 1)

        @block.tensor
        def _(pe):
            pe.wait_ge(pad, 1)
            for s in range(NT + 2):
                if s < NT:
                    tok = slice(s * PART, (s + 1) * PART)
                    if s == 0:
                        pe.wait_ge(w_lo, 1)
                    if s >= 2:
                        pe.wait_ge(ag_out, s - 1)
                    for c in range(CH):
                        last = mm3(pe, ag_bank[s % 2][:, 0:256], [w[:, c, tok] for w in k.xnT],
                                   [w[:, c, :] for w in k.w_ag], c == 0, c == CH - 1)
                    last.then_inc(ag_full, 1)
                    if s == 0:
                        pe.wait_ge(w_lo, 2)
                    if s >= 3:
                        pe.wait_ge(x_done, s - 2)
                    for c in range(CH):
                        mm3(pe, o_bank[s % 3][:, :], [w[:, c, tok] for w in k.xnT], [w[:, c, :] for w in k.w_base],
                            c == 0, False)
                if 1 <= s <= NT:
                    u = (s - 1) % 2
                    pe.wait_ge(hg_done, s)
                    if s >= 3:
                        pe.wait_ge(t_lo, s - 2)
                    pe.transpose(t_bank[u][:, 0:PART], k.hg[:, u, 0:PART], k.ident[:, :])
                    pe.transpose(t_bank[u][0:R1, PART:2 * PART], k.hg[:, u, PART:LR], k.ident[:, :]).then_inc(t_full, 1)
                if s >= 2:
                    t = s - 2
                    if s == 2:
                        pe.wait_ge(w_lo, 3)
                    pe.wait_ge(t_lo, t + 1)
                    mm3(pe, o_bank[t % 3][:, :], [w[:, t % 2, 0, :] for w in k.hgT], [w[:, 0, :] for w in k.w_b], False, False)
                    mm3(pe, o_bank[t % 3][:, :], [w[0:R1, t % 2, 1, :] for w in k.hgT],
                        [w[0:R1, 1, :] for w in k.w_b], False, True).then_inc(o_full, 1)


def build(nc, d, out, phases=("attn0", "ffn0", "attn1", "ffn1")):
    k = Kernel()
    k.d = d
    with ExitStack() as stack:
        def sem(name):
            return stack.enter_context(nc.semaphore(name))

        def sb(scope, name, shape, dtype=F32):
            return scope.enter_context(nc.sbuf_tensor(name, [PART] + shape, dtype))

        def pair(scope, name, shape):
            return [sb(scope, name + part, shape, F32R) for part in ("_hi", "_lo")]

        k.x = sb(stack, "x", [NT, HID])
        k.ctxT = pair(stack, "ctxT", [CH * BATCH * CTX])
        k.xnT = pair(stack, "xnT", [CH, BATCH * SEQ])
        k.ident, k.ones_f = sb(stack, "ident", [PART]), sb(stack, "ones_f", [PART])
        k.ones = sb(stack, "ones", [PART], F32R)
        k.minus_half = sb(stack, "minus_half", [16])
        k.gate_raw, k.gate = sb(stack, "gate_raw", [4]), sb(stack, "gate", [4])
        k.normw, k.qkw = sb(stack, "normw", [2]), sb(stack, "qkw", [1])
        k.raw_q, k.raw_o = sb(stack, "raw_q", [GH * HID]), sb(stack, "raw_o", [GH * HID])
        k.raw_kv = sb(stack, "raw_kv", [CH * 2 * HD + GH + 2])
        k.psum = stack.enter_context(nc.psum_tensor("psum", [PART, 8 * 512], F32))
        k.bank = [k.psum[:, n * 512:(n + 1) * 512] for n in range(8)]
        k.out = out
        k.ln_st, k.ln_mv, k.ln_rs = sb(stack, "ln_st", [NT, 6]), sb(stack, "ln_mv", [NT, 2]), sb(stack, "ln_rs", [NT])

        k.xn_tok = sb(stack, "xn_tok", [2, HID])
        ln = LayerNorm(k, sem)
        if "attn0" in phases:
            with ExitStack() as scope:
                k.bo, k.gbo = sb(scope, "bo", [HID]), sb(scope, "gbo", [HID])
                k.w_q, k.w_o = pair(scope, "w0q", [QW]), pair(scope, "w0o", [QW])
                k.w_kv = pair(scope, "w0kv", [KVW])
                k.bias, k.bq_rep = sb(scope, "bias", [GH + 2]), pair(scope, "bq_rep", [PART])
                k.bqk = sb(scope, "bqk", [BATCH, GH, CTX], F32R)
                k.kvT = pair(scope, "kvT0", [2, BATCH * CTX])
                k.WK = pair(scope, "WK", [CH, BATCH, GH, CTX])
                k.VW = pair(scope, "VW", [GH // 2, BATCH, HID])
                k.p0 = sb(scope, "p0", [4, GH * CTX])
                k.mx0, k.nb0, k.sum0 = (sb(scope, n, [2, GH]) for n in ("mx0", "nb0", "sum0"))
                k.rinv0 = sb(scope, "rinv0", [4, GH])
                k.pT0 = pair(scope, "pT0", [2, 2 * PART])
                attn0_phase(nc, k, sem, ln)
        if "ffn0" in phases:
            with ExitStack() as scope:
                ffn0_buffers(k, scope, sb, pair)
                ffn0_phase(nc, k, sem, ln)
        if "attn1" in phases:
            with ExitStack() as scope:
                attn1_buffers(k, scope, sb, pair)
                attn1_phase(nc, k, sem, ln)
        if "ffn1" in phases:
            with ExitStack() as scope:
                ffn1_buffers(k, scope, sb, pair)
                ffn1_phase(nc, k, sem)
                return
        done = sem("out_done")
        with nc.Block() as block:
            @block.sync
            def _(sp):
                sp.dma_start(out.rearrange("(t p) c -> p t c", p=PART), k.x[:, :, :]).then_inc(done, 16)
                sp.wait_ge(done, 16)


def layouts(inputs):
    import numpy as np
    a = {n: np.asarray(v) for n, v in inputs.items()}

    def chunked(w):
        return np.ascontiguousarray(w.reshape(-1, PART, w.shape[1]).transpose(1, 0, 2))

    def by_group(w):
        return np.ascontiguousarray(w.reshape(NKV, GH, HD, w.shape[1]).transpose(0, 2, 1, 3)).reshape(NKV * HD, -1)

    def kv_by_group(wk, wv):
        w = np.stack([wk, wv], 0).reshape(2, CH, PART, NKV, HD)
        return np.ascontiguousarray(w.transpose(3, 2, 1, 0, 4)).reshape(NKV * PART, -1)

    wkv, bkv = a["L0_xattn_Wkv"], a["L0_xattn_bkv"]
    half = NKV * HD
    biases = np.concatenate([a["L0_xattn_bq"].reshape(NKV, GH, HD).transpose(0, 2, 1),
                             bkv.reshape(2, NKV, HD).transpose(1, 2, 0)], 2).reshape(NKV * HD, GH + 2)
    gu = a["L0_ffn_w_gate_up"]
    chunks = []
    for i in range(IC):
        s = slice(i * PART, min((i + 1) * PART, INNER))
        chunks.append(np.concatenate([chunked(gu[:INNER][s].T), chunked(gu[INNER:][s].T)], 2).reshape(PART, -1))
    wd = a["L0_ffn_w_down"].T
    return {
        "x": a["x"].reshape(BATCH * SEQ, HID),
        "ctxT": chunked(a["ctx_4096"].reshape(BATCH * CTX, HID).T).reshape(PART, -1),
        "gates": np.concatenate([a["g_xattn"], a["g_ffn"]]).reshape(1, 4),
        "bo": a["L0_xattn_bo"].reshape(1, HID),
        "normw": np.stack([a["L1_xattn_q_norm_w"], a["L1_xattn_k_norm_w"]], 1),
        "w0q": by_group(a["L0_xattn_Wq"].T),
        "w0kv": np.concatenate([kv_by_group(wkv[:, :half], wkv[:, half:]), biases], 1),
        "w0o": by_group(a["L0_xattn_Wo"]),
        "w_gu": np.concatenate(chunks, 1),
        "w_down": wd,
        "w1q": np.ascontiguousarray(a["L1_xattn_Wq"].reshape(CH, PART, NKV, GH * HD).transpose(2, 1, 0, 3)).reshape(NKV * PART, -1),
        "w1kv": kv_by_group(a["L1_xattn_Wk"], a["L1_xattn_Wv"]),
        "w1o": by_group(a["L1_xattn_Wo"]),
        "w_base": chunked(a["L1_ffn_base_W"].T).reshape(PART, -1),
        "w_ag": chunked(np.concatenate([a["L1_ffn_lora_A"].reshape(LR, HID).T, a["L1_ffn_gate_W"].T], 1)).reshape(PART, -1),
        "w_b": np.ascontiguousarray(a["L1_ffn_lora_B"].transpose(0, 2, 1)).reshape(LR, HID),
    }


def kernel(**inputs):
    import numpy as _np
    import concourse.bacc as _bacc
    from concourse import mybir as _mybir
    from concourse.bass_utils import run_bass_kernel_spmd as _run

    nc = _bacc.Bacc("TRN2", target_bir_lowering=False, num_devices=1)
    arrays, d = {}, {}
    for name, a in layouts(inputs).items():
        a = _np.ascontiguousarray(a)
        arrays[f"in_{name}"] = a
        d[name] = nc.dram_tensor(f"in_{name}", a.shape, _mybir.dt.from_np(a.dtype), kind="ExternalInput").ap()
    out = nc.dram_tensor("out_x", (BATCH * SEQ, HID), F32, kind="ExternalOutput").ap()
    build(nc, d, out)
    r = _run(nc, [arrays], core_ids=[0])
    return r.results[0]["out_x"].reshape(BATCH, SEQ, HID)
```

```python
import concourse.bass as bass
from concourse import mybir
from contextlib import ExitStack

F32 = mybir.dt.float32
F32R = mybir.dt.float32r
ALU = mybir.AluOpType
ACT = mybir.ActivationFunctionType
AX = mybir.AxisListType

PART = 128
BATCH, SEQ, HID = 4, 256, 512
CTX = 64
CH = HID // PART
NT = BATCH * SEQ // PART
HD = 128
NKV = 8
GH = 4
INNER = 1376
IC = 11
ILAST = INNER - (IC - 1) * PART
NEXP, RANK = 28, 8
LR = NEXP * RANK
LN_EPS, RMS_EPS = 1e-5, 1e-6
SCALE = float(HD) ** -0.5
LORA_SCALE = 16.0 / RANK
KVW = CH * 2 * HD
QW = GH * HID


def f(ap):
    return ap.bitcast(F32)


def mm3(pe, out, w, m, start, stop):
    pe.matmul(out, w[1], m[0], start=start, stop=False)
    pe.matmul(out, w[0], m[1], start=False, stop=False)
    return pe.matmul(out, w[0], m[0], start=False, stop=stop)


def run(nc, sync, gpsimd, vector, scalar, tensor):
    with nc.Block() as block:
        block.sync(sync)
        block.gpsimd(gpsimd)
        block.vector(vector)
        block.scalar(scalar)
        block.tensor(tensor)


def by_head(ap):
    return ap.rearrange("p (h n) -> p h n", h=GH)


class Kernel:
    pass


class LayerNorm:

    def __init__(self, k, sem):
        self.k = k
        self.stats, self.mv, self.ms, self.rstd, self.xn, self.turned, self.hi_done, self.split = (
            sem("ln_" + n) for n in ("stats", "mv", "ms", "rstd", "xn", "turned", "hi", "split"))

    def dve_stats(self, dve, c, t):
        k, m = self.k, NT * c + t
        dve.bn_stats(k.ln_st[:, t, :], k.x[:, t, :]).then_inc(self.stats, 1)
        dve.wait_ge(self.stats, m + 1)
        dve.bn_aggr(k.ln_mv[:, t, :], k.ln_st[:, t, :]).then_inc(self.mv, 1)

    def pool_rstd(self, pool, c, t):
        k, m = self.k, NT * c + t
        pool.wait_ge(self.mv, m + 1)
        pool.tensor_scalar(k.ln_rs[:, t:t + 1], k.ln_mv[:, t, 1:2], LN_EPS, None, ALU.add)
        pool.tensor_scalar(k.ln_nb[:, t:t + 1], k.ln_mv[:, t, 0:1], -1.0, None, ALU.mult).then_inc(self.ms, 1)
        pool.wait_ge(self.ms, 2 * m + 1)
        pool.tensor_tensor(k.ln_rs[:, t:t + 1], k.ln_rs[:, t:t + 1], k.minus_half[:, 0:1], ALU.pow).then_inc(self.ms, 1)
        pool.wait_ge(self.ms, 2 * m + 2)
        pool.tensor_tensor(k.ln_nb[:, t:t + 1], k.ln_nb[:, t:t + 1], k.ln_rs[:, t:t + 1], ALU.mult).then_inc(self.rstd, 1)

    def act_norm(self, act, c, t):
        k, m = self.k, NT * c + t
        act.wait_ge(self.rstd, m + 1)
        if m >= 2:
            act.wait_ge(self.turned, m - 1)
        act.activation(k.xn_tok[:, t % 2, :], k.x[:, t, :], ACT.Identity, bias=k.ln_nb[:, t:t + 1],
                       scale=k.ln_rs[:, t:t + 1]).then_inc(self.xn, 1)

    def pe_turn(self, pe, c, t, bank):
        k, m = self.k, NT * c + t
        pe.wait_ge(self.xn, m + 1)
        if m >= 2:
            pe.wait_ge(self.split, m - 1)
        for i in range(CH):
            last = pe.transpose(bank[:, i * PART:(i + 1) * PART], k.xn_tok[:, t % 2, i * PART:(i + 1) * PART], k.ident[:, :])
        last.then_inc(self.turned, 1)

    def act_hi(self, act, c, t, bank):
        k, m = self.k, NT * c + t
        act.wait_ge(self.turned, m + 1)
        act.activation(k.xnT[0][:, :, t * PART:(t + 1) * PART], bank.rearrange("p (c q) -> p c q", c=CH),
                       ACT.Copy).then_inc(self.hi_done, 1)

    def dve_lo(self, dve, c, t, bank):
        k, m = self.k, NT * c + t
        dve.wait_ge(self.hi_done, m + 1)
        dve.tensor_tensor(k.xnT[1][:, :, t * PART:(t + 1) * PART], bank.rearrange("p (c q) -> p c q", c=CH),
                          f(k.xnT[0][:, :, t * PART:(t + 1) * PART]), ALU.subtract).then_inc(self.split, 1)


def attn0_phase(nc, k, sem, ln):
    in_ctx, in_x, in_small = sem("in_ctx"), [sem(f"in_x{t}") for t in range(4)], sem("in_small")
    ident0, ident, gates, ones_set, gbo_done, ctx_hi, ctx_lo, bo_added = (
        sem(n) for n in ("ident0", "ident", "gates", "ones_set", "gbo", "ctx_hi", "ctx_lo", "bo_added"))
    kv_in, q_in, o_in, kv_hi, q_hi, o_hi, kv_lo, q_lo, o_lo, bqr_hi, bqr_lo, bias_in, bqk_zero = (
        sem("a0_" + n) for n in ("kv_in", "q_in", "o_in", "kv_hi", "q_hi", "o_hi", "kv_lo", "q_lo", "o_lo",
                                 "bqr_hi", "bqr_lo", "bias_in", "bqk_zero"))
    prep_full, prep_hi, prep_free, s_full, s_max, nb_ready, p_exp, p_rec, p_ready, pt_full, pt_hi, pt_lo, o_full, x_done = (
        sem("a0_" + n) for n in ("prep_full", "prep_hi", "prep_free", "s_full", "s_max", "nb", "p_exp", "p_rec",
                                 "p_ready", "pt_full", "pt_hi", "pt_lo", "o_full", "x_done"))

    NEXT_PREP = {6: [("kv",)], 8: [("wk", 0), ("wk", 1), ("wk", 2), ("bq",)], 9: [("wk", 3), ("wk", 4), ("vw", 0, 0)],
                 10: [("wk", 5), ("wk", 6), ("wk", 7), ("vw", 1, 0)]}
    OWN_PREP = {0: [("vw", 2, 0), ("vw", 3, 0)], 1: [("vw", 0, 1)], 3: [("vw", 1, 1)], 4: [("vw", 2, 1)], 5: [("vw", 3, 1)]}
    ORDER = sum(OWN_PREP.values(), []) + sum(NEXT_PREP.values(), [])
    FILLS, OWN = len(ORDER), sum(map(len, OWN_PREP.values()))
    HEAD = FILLS - OWN
    LN_TILES = 4
    HEAD_ORDER = [("kv",), ("bq",)] + [("wk", j) for j in range(8)] + [("vw", 0, 0), ("vw", 1, 0)]
    FREE0 = 2
    CONV = {"kv": 2, "q": 4, "o": 4}
    wq4, wo4 = [by_head(w[:, :]) for w in k.w_q], [by_head(w[:, :]) for w in k.w_o]
    wkv4 = [w[:, :].rearrange("p (c n) -> p c n", c=CH) for w in k.w_kv]
    ctx4 = [w[:, :].rearrange("p (c n) -> p c n", c=CH) for w in k.ctxT]
    s_bank, pt_bank, o_bank = [k.bank[3], k.bank[4]], k.bank[5], [k.bank[6], k.bank[7]]
    raw = {"kv": k.raw_kv, "q": k.raw_q, "o": k.raw_o}
    wts = {"kv": k.w_kv, "q": k.w_q, "o": k.w_o}
    width = {"kv": KVW, "q": QW, "o": QW}
    arrived, hi_of, lo_of = {"kv": kv_in, "q": q_in, "o": o_in}, {"kv": kv_hi, "q": q_hi, "o": o_hi}, {"kv": kv_lo, "q": q_lo, "o": o_lo}

    def place(base, fill):
        if base is None:
            at = slot = HEAD_ORDER.index(fill)
        else:
            at, slot = base + ORDER.index(fill), HEAD + ORDER.index(fill)
        return at, k.bank[slot % 3]

    def steps_fills(s, nxt):
        return OWN_PREP.get(s, []) + (NEXT_PREP.get(s, []) if nxt else [])

    def wk_view(w, c, hp):
        return w[:, c, :, 2 * hp:2 * hp + 2, :].rearrange("p b h k -> p h b k")

    def wk_bank(bank):
        return bank.rearrange("p (h b k) -> p h b k", h=2, b=BATCH)

    def bq_bank(bank, h):
        return bank[32 * h:32 * h + 1, 0:BATCH * CTX].rearrange("p (b k) -> p b k", b=BATCH)

    def head_bank(t):
        return (s_bank + o_bank)[t % 4]

    def ln_bank(t):
        return k.bank[t % 2]

    def spread(stat):
        return stat.unsqueeze(2).to_broadcast([PART, GH, CTX])

    def sync(sp):
        def weights(kind):
            sp.dma_start(raw[kind][:, :], k.d["w0" + kind][0:PART, :]).then_inc(arrived[kind], 16)

        sp.dma_start(k.xn_tok[:, :, :].rearrange("p a b -> p (a b)"), k.d["ctxT"]).then_inc(in_ctx, 16)
        weights("kv")
        sp.dma_start(k.gate_raw[:, :], k.d["gates"].to_broadcast([PART, 4])).then_inc(in_small, 16)
        sp.dma_start(k.bo[:, :], k.d["bo"].to_broadcast([PART, HID])).then_inc(in_small, 16)
        sp.dma_start(k.normw[:, :], k.d["normw"]).then_inc(in_small, 16)
        weights("q")
        for i in range(4):
            sp.dma_start(k.x[:, 2 * i:2 * i + 2, :],
                         k.d["x"][i * 256:(i + 1) * 256, :].rearrange("(t p) c -> p t c", p=PART)).then_inc(in_x[i], 16)
        weights("o")
        with sp.Fori(1, NKV) as g:
            for kind in ("kv", "q", "o"):
                sp.wait_ge(lo_of[kind], g * CONV[kind])
                sp.dma_start(raw[kind][:, :], k.d["w0" + kind][bass.ts(g, PART), :]).then_inc(arrived[kind], 16)
        sp.wait_ge(kv_lo, NKV * CONV["kv"])
        k.ffn0_gate_up(sp, 0)
        sp.wait_ge(q_lo, NKV * CONV["q"])
        k.ffn0_down(sp, 0)
        sp.wait_ge(o_lo, NKV * CONV["o"])
        k.ffn0_down(sp, 1)

    def gpsimd(pool):
        def lo_piece(kind, g, i):
            n = width[kind] // CONV[kind]
            if i == 0:
                pool.wait_ge(hi_of[kind], g + 1)
            s = slice(i * n, (i + 1) * n)
            pool.tensor_tensor(wts[kind][1][:, s], raw[kind][:, s], f(wts[kind][0][:, s]), ALU.subtract).then_inc(lo_of[kind], 1)

        def bq_rows(g):
            pool.wait_ge(bqr_hi, g + 1)
            pool.tensor_tensor(by_head(k.bq_rep[1][:, :]), k.bias[:, 0:GH].unsqueeze(2).to_broadcast([PART, GH, 32]),
                               by_head(f(k.bq_rep[0][:, :])), ALU.subtract).then_inc(bqr_lo, 1)

        def body(g, nxt):
            sched = {1: [("kv", 0)], 2: [("kv", 1)], 3: [("q", 0)], 4: [("q", 1), ("q", 2)], 5: [("q", 3), ("o", 0)],
                     6: [("o", 1), ("o", 2)], 7: [("o", 3)]}
            for t in range(NT):
                pool.wait_ge(p_rec, NT * g + t + 1)
                p = by_head(k.p0[:, t % 4, :])
                pool.tensor_tensor(p, p, spread(k.rinv0[:, t % 4, :]), ALU.mult).then_inc(p_ready, 1)
                if nxt:
                    for kind, i in sched.get(t, []):
                        lo_piece(kind, g + 1, i)
                    if t == 2:
                        bq_rows(g + 1)
                elif t == 2:
                    k.ffn0_w_lo(pool, 0)
                elif t >= 3:
                    ln.pool_rstd(pool, 1, t - 3)
                if isinstance(g, int) and g == 0:
                    pool.tensor_tensor(k.x[:, t, :], k.x[:, t, :], k.gbo[:, :], ALU.add).then_inc(bo_added, 1)

        pool.memset(k.ident[:, :], 0.0).then_inc(ident0, 1)
        pool.memset(k.minus_half[:, :], -0.5)
        pool.wait_ge(ident0, 1)
        pool.affine_select(out=k.ident[:, :], in_=k.ident[:, :], compare_op=ALU.not_equal, fill=1.0,
                           base=0, pattern=[[-1, PART]], channel_multiplier=1).then_inc(ident, 1)
        pool.memset(f(k.bqk[:, :, :, :]), 0.0).then_inc(bqk_zero, 1)
        pool.wait_ge(ctx_hi, 1)
        pool.tensor_tensor(k.ctxT[1][:, :], k.xn_tok[:, :, :].rearrange("p a b -> p (a b)"), f(k.ctxT[0][:, :]),
                           ALU.subtract).then_inc(ctx_lo, 1)
        bq_rows(0)
        for t in range(NT):
            ln.pool_rstd(pool, 0, t)
        for i in range(CONV["o"]):
            lo_piece("o", 0, i)
        pool.wait_ge(gbo_done, 1)
        pool.wait_ge(ln.xn, NT)
        body(0, True)
        with pool.Fori(1, NKV - 1) as g:
            body(g, True)
        body(NKV - 1, False)

    def vector(dve):
        def conv(kind, g):
            dve.wait_ge(arrived[kind], 16 * g + 16)
            if kind == "kv":
                dve.tensor_copy(k.bias[:, :], k.raw_kv[:, KVW:KVW + GH + 2]).then_inc(bias_in, 1)
            dve.tensor_copy(wts[kind][0][:, :], raw[kind][:, 0:width[kind]]).then_inc(hi_of[kind], 1)
            if kind == "kv":
                dve.wait_ge(bias_in, g + 1)
                dve.tensor_copy(by_head(k.bq_rep[0][:, :]),
                                k.bias[:, 0:GH].unsqueeze(2).to_broadcast([PART, GH, 32])).then_inc(bqr_hi, 1)

        def own_lo(kind, pieces):
            dve.wait_ge(hi_of[kind], 1)
            dve.tensor_tensor(wts[kind][1][:, :], raw[kind][:, 0:width[kind]], f(wts[kind][0][:, :]),
                              ALU.subtract).then_inc(lo_of[kind], pieces)

        def prep(base, fill):
            (at, bank), kind = place(base, fill), fill[0]
            dve.wait_ge(prep_hi, at + 1)
            if kind == "kv":
                for j in range(2):
                    last = dve.scalar_tensor_tensor(
                        out=k.kvT[1][:, j, :], in0=bank[:, j * 256:(j + 1) * 256], scalar=k.bias[:, GH + j:GH + j + 1],
                        in1=f(k.kvT[0][:, j, :]), op0=ALU.add, op1=ALU.subtract)
            elif kind == "bq":
                for h in range(GH):
                    last = dve.tensor_tensor(k.bqk[32:33, :, h, :], bq_bank(bank, h), f(k.bqk[0:1, :, h, :]), ALU.subtract)
            elif kind == "wk":
                c, hp = divmod(fill[1], 2)
                last = dve.tensor_tensor(wk_view(k.WK[1], c, hp), wk_bank(bank), f(wk_view(k.WK[0], c, hp)), ALU.subtract)
            else:
                _, h, pr = fill
                r = slice(64 * (h % 2), 64 * (h % 2) + 64)
                for bp in range(2):
                    last = dve.tensor_tensor(k.VW[1][r, h // 2, 2 * pr + bp, :], bank[64 * bp:64 * bp + 64, :],
                                             f(k.VW[0][r, h // 2, 2 * pr + bp, :]), ALU.subtract)
            last.then_inc(prep_free, 1)

        def row_sums(g, t):
            dve.wait_ge(p_exp, NT * g + t + 1)
            dve.reciprocal(k.rinv0[:, t % 4, :], k.sum0[:, t % 2, :]).then_inc(p_rec, 1)

        def x_add(g, t):
            dve.wait_ge(o_full, NT * g + t + 1)
            if isinstance(g, int) and g == 0:
                dve.wait_ge(bo_added, t + 1)
            dve.scalar_tensor_tensor(out=k.x[:, t, :], in0=o_bank[t % 2], scalar=k.gate[:, 0:1],
                                     in1=k.x[:, t, :], op0=ALU.mult, op1=ALU.add).then_inc(x_done, 1)

        def body(g, nxt):
            base = HEAD + FILLS * g
            for s in range(NT + 3):
                n = NT * g + s
                if s >= 4:
                    x_add(g, s - 4)
                    if not nxt and s - 4 <= LN_TILES:
                        dve.wait_ge(x_done, n - 3)
                        ln.dve_stats(dve, 1, s - 4)
                if 1 <= s <= NT:
                    row_sums(g, s - 1)
                if s < NT:
                    dve.wait_ge(s_full, n + 1)
                    dve.tensor_reduce(k.mx0[:, s % 2, :], by_head(s_bank[s % 2][:, 0:GH * CTX]), AX.X, ALU.max)\
                       .then_inc(s_max, 1)
                    dve.wait_ge(s_max, n + 1)
                    dve.tensor_scalar(k.nb0[:, s % 2, :], k.mx0[:, s % 2, :], -SCALE, None, ALU.mult).then_inc(nb_ready, 1)
                for fill in steps_fills(s, nxt):
                    prep(base, fill)
                if 2 <= s < NT + 2:
                    t = s - 2
                    dve.wait_ge(pt_hi, n - 1)
                    dve.tensor_tensor(k.pT0[1][:, t % 2, :], pt_bank[:, 0:256], f(k.pT0[0][:, t % 2, :]),
                                      ALU.subtract).then_inc(pt_lo, 1)
                if nxt and s in (1, 3, 5):
                    conv({1: "kv", 3: "q", 5: "o"}[s], g + 1)
                if not nxt and s == 1:
                    k.ffn0_w_hi(dve, 0)
                if not nxt and s >= 7:
                    ln.dve_lo(dve, 1, s - 7, ln_bank(s - 7))
            x_add(g, NT - 1)

        def stats(t):
            dve.wait_ge(in_x[t // 2], 16)
            ln.dve_stats(dve, 0, t)

        dve.wait_ge(in_ctx, 16)
        dve.tensor_copy(k.ctxT[0][:, :], k.xn_tok[:, :, :].rearrange("p a b -> p (a b)")).then_inc(ctx_hi, 1)
        conv("kv", 0)
        own_lo("kv", CONV["kv"])
        dve.memset(k.ones_f[:, :], 1.0).then_inc(ones_set, 1)
        conv("q", 0)
        own_lo("q", CONV["q"])
        dve.wait_ge(ones_set, 1)
        dve.tensor_copy(k.ones[:, :], k.ones_f[:, :])
        dve.wait_ge(in_small, 48)
        dve.scalar_tensor_tensor(out=k.qkw[:, :], in0=k.normw[:, 0:1], scalar=float(HD) ** 0.5, in1=k.normw[:, 1:2],
                                 op0=ALU.mult, op1=ALU.mult)
        dve.wait_ge(bqk_zero, 1)
        prep(None, ("kv",))
        stats(0)
        stats(1)
        prep(None, ("bq",))
        stats(2)
        for t in range(NT):
            if t + 3 < NT:
                stats(t + 3)
            ln.dve_lo(dve, 0, t, head_bank(t))
            prep(None, ("wk", t))
            if t == 5:
                conv("o", 0)
        prep(None, ("vw", 0, 0))
        prep(None, ("vw", 1, 0))
        body(0, True)
        with dve.Fori(1, NKV - 1) as g:
            body(g, True)
        body(NKV - 1, False)
        ln.dve_lo(dve, 1, LN_TILES, ln_bank(LN_TILES))

    def scalar(act):
        def prep(base, fill):
            (at, bank), kind = place(base, fill), fill[0]
            act.wait_ge(prep_full, at + 1)
            if kind == "kv":
                for j in range(2):
                    last = act.activation(k.kvT[0][:, j, :], bank[:, j * 256:(j + 1) * 256], ACT.Identity,
                                          bias=k.bias[:, GH + j:GH + j + 1])
            elif kind == "bq":
                for h in range(GH):
                    last = act.activation(k.bqk[0:1, :, h, :], bq_bank(bank, h), ACT.Copy)
            elif kind == "wk":
                c, hp = divmod(fill[1], 2)
                last = act.activation(wk_view(k.WK[0], c, hp), wk_bank(bank), ACT.Copy)
            else:
                _, h, pr = fill
                r = slice(64 * (h % 2), 64 * (h % 2) + 64)
                for bp in range(2):
                    last = act.activation(k.VW[0][r, h // 2, 2 * pr + bp, :], bank[64 * bp:64 * bp + 64, :], ACT.Copy)
            last.then_inc(prep_hi, 1)

        def body(g, nxt):
            base = HEAD + FILLS * g
            for s in range(NT + 3):
                n = NT * g + s
                for fill in steps_fills(s, nxt):
                    prep(base, fill)
                if 2 <= s < NT + 2:
                    act.wait_ge(pt_full, n - 1)
                    act.activation(k.pT0[0][:, s % 2, :], pt_bank[:, 0:256], ACT.Copy).then_inc(pt_hi, 1)
                if s < NT:
                    act.wait_ge(nb_ready, n + 1)
                    for h in range(GH):
                        last = act.activation(k.p0[:, s % 4, h * CTX:(h + 1) * CTX],
                                              s_bank[s % 2][:, h * CTX:(h + 1) * CTX], ACT.Exp, scale=SCALE,
                                              bias=k.nb0[:, s % 2, h:h + 1], accum_out=k.sum0[:, s % 2, h:h + 1])
                    last.then_inc(p_exp, 1)
                if not nxt and 5 <= s <= LN_TILES + 5:
                    ln.act_norm(act, 1, s - 5)
                if not nxt and s >= 6:
                    ln.act_hi(act, 1, s - 6, ln_bank(s - 6))

        act.wait_ge(in_small, 48)
        act.activation(k.gate[:, :], k.gate_raw[:, :], ACT.Tanh).then_inc(gates, 1)
        act.wait_ge(gates, 1)
        act.activation(k.gbo[:, :], k.bo[:, :], ACT.Copy, scale=k.gate[:, 0:1]).then_inc(gbo_done, 1)
        act.wait_ge(bqk_zero, 1)
        act.wait_ge(bias_in, 1)
        prep(None, ("kv",))
        prep(None, ("bq",))
        act.wait_ge(ctx_lo, 1)
        ln.act_norm(act, 0, 0)
        ln.act_norm(act, 0, 1)
        for t in range(NT):
            ln.act_hi(act, 0, t, head_bank(t))
            prep(None, ("wk", t))
            if t + 2 < NT:
                ln.act_norm(act, 0, t + 2)
        prep(None, ("vw", 0, 0))
        prep(None, ("vw", 1, 0))
        body(0, True)
        with act.Fori(1, NKV - 1) as g:
            body(g, True)
        body(NKV - 1, False)

    def tensor(pe):
        def prep(base, fill, g):
            (at, bank), kind = place(base, fill), fill[0]
            if not (isinstance(at, int) and at < 3):
                pe.wait_ge(prep_free, at - 2)
            if kind == "kv":
                pe.wait_ge(kv_lo, CONV["kv"] * (g + 1))
                for j in range(2):
                    for c in range(CH):
                        last = mm3(pe, bank[:, j * 256:(j + 1) * 256], [w[:, c, j * HD:(j + 1) * HD] for w in wkv4],
                                   [w[:, c, :] for w in ctx4], c == 0, c == CH - 1)
            elif kind == "bq":
                pe.wait_ge(prep_free, place(base, ("kv",))[0] + 1)
                pe.wait_ge(bqr_lo, g + 1)
                last = mm3(pe, bank[:, 0:256], [w[:, :] for w in k.bq_rep], [w[:, 0, :] for w in k.kvT], True, True)
            elif kind == "wk":
                c, hp = divmod(fill[1], 2)
                if fill[1] == 0:
                    pe.wait_ge(prep_free, place(base, ("kv",))[0] + 1)
                    pe.wait_ge(q_lo, CONV["q"] * (g + 1))
                for h in range(2):
                    last = mm3(pe, bank[:, h * 256:(h + 1) * 256],
                               [w[:, 2 * hp + h, c * PART:(c + 1) * PART] for w in wq4],
                               [w[:, 0, :] for w in k.kvT], True, True)
            else:
                _, h, pr = fill
                if pr == 0:
                    pe.wait_ge(o_lo, CONV["o"] * g + h + 1)
                last = mm3(pe, bank, [w[:, 1, pr * PART:(pr + 1) * PART] for w in k.kvT],
                           [w[:, h, :] for w in wo4], True, True)
            last.then_inc(prep_full, 1)

        def body(g, first, nxt):
            base = HEAD + FILLS * g
            for s in range(NT + 3):
                n = NT * g + s
                for fill in OWN_PREP.get(s, []):
                    prep(base, fill, g)
                for fill in NEXT_PREP.get(s, []) if nxt else []:
                    prep(base, fill, g + 1)
                if s < NT:
                    if s == 0:
                        pe.wait_ge(prep_free, base)
                    if not (first and s < 2):
                        pe.wait_ge(p_exp, n - 1)
                    S, b = s_bank[s % 2][:, 0:GH * CTX], s // 2
                    for c in range(CH):
                        mm3(pe, S, [w[:, c, s * PART:(s + 1) * PART] for w in k.xnT],
                            [w[:, c, b, :, :] for w in k.WK], c == 0, False)
                    pe.matmul(S, k.ones[:, :], k.bqk[:, b, :, :], start=False, stop=True).then_inc(s_full, 1)
                if 2 <= s < NT + 2:
                    t = s - 2
                    pe.wait_ge(p_ready, n - 1)
                    if not (first and t == 0):
                        pe.wait_ge(pt_lo, n - 2)
                    for hp in range(2):
                        last = pe.transpose(pt_bank[:, hp * PART:(hp + 1) * PART],
                                            k.p0[:, t % 4, hp * PART:(hp + 1) * PART], k.ident[:, :])
                    last.then_inc(pt_full, 1)
                if s >= 3:
                    t = s - 3
                    pe.wait_ge(pt_lo, n - 2)
                    if t == 0:
                        pe.wait_ge(prep_free, base + FREE0)
                    if t == 4:
                        pe.wait_ge(prep_free, base + OWN)
                    if not (first and t < 2):
                        pe.wait_ge(x_done, n - 4)
                    for hp in range(2):
                        last = mm3(pe, o_bank[t % 2], [w[:, t % 2, hp * PART:(hp + 1) * PART] for w in k.pT0],
                                   [w[:, hp, t // 2, :] for w in k.VW], hp == 0, hp == 1)
                    last.then_inc(o_full, 1)
                if not nxt and s == 6:
                    pe.wait_ge(prep_free, base + OWN)
                if not nxt and s >= 6:
                    ln.pe_turn(pe, 1, s - 6, ln_bank(s - 6))

        pe.wait_ge(ctx_lo, 1)
        prep(None, ("kv",), 0)
        prep(None, ("bq",), 0)
        pe.wait_ge(ident, 1)
        for t in range(NT):
            ln.pe_turn(pe, 0, t, head_bank(t))
            prep(None, ("wk", t), 0)
        prep(None, ("vw", 0, 0), 0)
        prep(None, ("vw", 1, 0), 0)
        pe.wait_ge(ln.split, NT)
        body(0, True, True)
        with pe.Fori(1, NKV - 1) as g:
            body(g, False, True)
        body(NKV - 1, False, False)

    run(nc, sync, gpsimd, vector, scalar, tensor)



def ffn0_buffers(k, scope, sb, pair):
    k.raw_gu1 = sb(scope, "raw_gu1", [CH * 2 * PART])
    k.w_gu = [k.w_kv, pair(scope, "w_gu1", [CH * 2 * PART])]
    k.w_dn = pair(scope, "w_dn", [IC, HID])
    k.hT = pair(scope, "hT", [IC, 512])
    k.f_tanh, k.f_a, k.f_h = (sb(scope, n, [2, 512]) for n in ("f_tanh", "f_a", "f_h"))


def ffn0_loads(k, sem):
    k.gu_in = [sem(f"f0_gu_in{n}") for n in range(2)]
    k.gu_wlo, k.dn_in, k.dn_lo = sem("f0_gu_wlo"), [sem(f"f0_dn_in{n}") for n in range(3)], sem("f0_dn_lo")
    k.DN = [(k.raw_q, 0, 4), (k.raw_o, 4, 8), (k.raw_q, 8, 11)]

    def gate_up(sp, n):
        i = n % IC
        w = CH * 2 * (ILAST if i == IC - 1 else PART)
        if n >= 2:
            sp.wait_ge(k.gu_wlo, n - 1)
        sp.dma_start((k.raw_gu1 if n % 2 else k.raw_kv)[:, 0:w], k.d["w_gu"][:, i * 1024:i * 1024 + w]).then_inc(k.gu_in[n % 2], 16)

    def slices(i0, i1):
        full = min(i1, IC - 1) - i0
        return [(slice(0, PART), i0, full)] + ([(slice(0, ILAST), IC - 1, 1)] if i1 == IC else [])

    def down(sp, j):
        raw, i0, i1 = k.DN[j]
        if j == 2:
            sp.wait_ge(k.dn_lo, 4)
        for rows, i, n in slices(i0, i1):
            src = k.d["w_down"][i * PART:i * PART + rows.stop * n, :].rearrange("(n p) c -> p n c", n=n)
            dst = raw[rows, (i - i0) * HID:(i - i0 + n) * HID].rearrange("p (n c) -> p n c", n=n)
            sp.dma_start(dst, src).then_inc(k.dn_in[j], 16)

    def chunk(n):
        w = CH * 2 * (ILAST if n % IC == IC - 1 else PART)
        hi, lo = k.w_gu[n % 2] if n else k.w_kv
        return (k.raw_gu1 if n % 2 else k.raw_kv)[:, 0:w], hi[:, 0:w], lo[:, 0:w]

    def w_hi(dve, n):
        raw, hi, _ = chunk(n)
        dve.wait_ge(k.gu_in[n % 2], 16 * (n // 2 + 1))
        dve.tensor_copy(hi, raw).then_inc(k.gu_whi, 1)

    def w_lo(eng, n):
        raw, hi, lo = chunk(n)
        eng.wait_ge(k.gu_whi, n + 1)
        eng.tensor_tensor(lo, raw, f(hi), ALU.subtract).then_inc(k.gu_wlo, 1)

    k.gu_whi = sem("f0_gu_whi")
    k.ffn0_gate_up, k.ffn0_down, k.ffn0_slices, k.ffn0_w_hi, k.ffn0_w_lo = gate_up, down, slices, w_hi, w_lo


def ffn0_phase(nc, k, sem, ln):
    gu_in, gu_wlo, dn_in, dn_lo, DN, dn_slices = k.gu_in, k.gu_wlo, k.dn_in, k.dn_lo, k.DN, k.ffn0_slices
    dn_hi = sem("f0_dn_hi")
    gu_full, tanh_done, a_done, h_done = sem("f0_gu_full"), sem("f0_tanh"), sem("f0_a"), sem("f0_h")
    h_hi, h_lo, o_full, x_done = sem("f0_h_hi"), sem("f0_h_lo"), sem("f0_o_full"), sem("f0_x_done")
    STEPS = [(half, i) for half in range(2) for i in range(IC)]
    raws = [k.raw_kv, k.raw_gu1]
    gate_bank, up_bank, o_bank = [k.bank[0], k.bank[2]], [k.bank[1], k.bank[3]], k.bank[4:8]

    def ln_bank(j):
        return k.bank[j]

    def width(i):
        return ILAST if i == IC - 1 else PART

    def ln_tiles(n):
        if 0 <= n < 3:
            return 1, 5 + n, o_bank[n]
        if IC + 1 <= n < IC + 5:
            return 2, n - IC - 1, o_bank[n - IC - 1]
        return None

    with nc.Block() as block:
        @block.sync
        def _(sp):
            k.ffn0_gate_up(sp, 1)
            for n in range(2, len(STEPS)):
                k.ffn0_gate_up(sp, n)
                if n == 6:
                    k.ffn0_down(sp, 2)
            sp.wait_ge(dn_lo, IC)
            k.attn1_load(sp, "q")
            k.attn1_load(sp, "o")
            sp.wait_ge(gu_wlo, len(STEPS) - 1)
            k.attn1_load(sp, "kv")

        @block.gpsimd
        def _(pool):
            def dn(i):
                j, p = i // 4, slice(0, width(i))
                raw, i0, _ = DN[j]
                pool.wait_ge(dn_hi, j + 1)
                pool.tensor_tensor(k.w_dn[1][p, i, :], raw[p, (i - i0) * HID:(i - i0 + 1) * HID],
                                   f(k.w_dn[0][p, i, :]), ALU.subtract).then_inc(dn_lo, 1)

            for n, (half, i) in enumerate(STEPS):
                if n + 2 < len(STEPS):
                    k.ffn0_w_lo(pool, n + 2)
                if n < IC - 1:
                    dn(n)
                if n == IC - 2:
                    dn(IC - 1)
                p = slice(0, width(i))
                pool.wait_ge(h_hi, n + 1)
                pool.tensor_tensor(k.hT[1][p, i, :], k.f_h[p, n % 2, :], f(k.hT[0][p, i, :]), ALU.subtract).then_inc(h_lo, 1)
                if ln_tiles(n):
                    ln.pool_rstd(pool, *ln_tiles(n)[:2])
            for t in (4, 5):
                ln.pool_rstd(pool, 2, t)

        @block.vector
        def _(dve):
            def dn(j):
                raw, i0, i1 = DN[j]
                dve.wait_ge(dn_in[j], 16 * len(dn_slices(i0, i1)))
                for rows, i, n in dn_slices(i0, i1):
                    last = dve.tensor_copy(k.w_dn[0][rows, i:i + n, :],
                                           raw[rows, (i - i0) * HID:(i - i0 + n) * HID].rearrange("p (n c) -> p n c", n=n))
                last.then_inc(dn_hi, 1)

            k.ffn0_w_hi(dve, 1)
            k.ffn0_w_lo(dve, 1)
            for n, (half, i) in enumerate(STEPS):
                if n + 2 < len(STEPS):
                    dve.wait_ge(gu_full, n + 1)
                    k.ffn0_w_hi(dve, n + 2)
                if n in (0, 2, 6):
                    dn({0: 0, 2: 1, 6: 2}[n])
                p, s = slice(0, width(i)), n % 2
                dve.wait_ge(tanh_done, n + 1)
                dve.scalar_tensor_tensor(out=k.f_a[p, s, :], in0=k.f_tanh[p, s, :], scalar=1.0, in1=gate_bank[s][p, :],
                                         op0=ALU.add, op1=ALU.mult).then_inc(a_done, 1)
                dve.wait_ge(a_done, n + 1)
                if n >= 2:
                    dve.wait_ge(h_lo, n - 1)
                dve.scalar_tensor_tensor(out=k.f_h[p, s, :], in0=k.f_a[p, s, :], scalar=0.5, in1=up_bank[s][p, :],
                                         op0=ALU.mult, op1=ALU.mult).then_inc(h_done, 1)
                if ln_tiles(n):
                    ln.dve_stats(dve, *ln_tiles(n)[:2])
                if ln_tiles(n - 2):
                    ln.dve_lo(dve, *ln_tiles(n - 2))
                if i == IC - 1:
                    for j in range(4):
                        dve.wait_ge(o_full, 4 * half + j + 1)
                        t = 4 * half + j
                        dve.scalar_tensor_tensor(out=k.x[:, t, :], in0=o_bank[j][:, :], scalar=k.gate[:, 2:3],
                                                 in1=k.x[:, t, :], op0=ALU.mult, op1=ALU.add).then_inc(x_done, 1)
                        dve.wait_ge(x_done, t + 1)
                        if half == 1 and j < 2:
                            ln.dve_stats(dve, 2, t)
                        if half == 1 and j == 1:
                            k.attn1_split_kv(dve)
                        if half == 1 and j >= 2:
                            ln.dve_lo(dve, 2, t - 2, ln_bank(j - 2))

        @block.scalar
        def _(act):
            def hi(n):
                half, i = STEPS[n]
                p = slice(0, width(i))
                act.wait_ge(h_done, n + 1)
                act.activation(k.hT[0][p, i, :], k.f_h[p, n % 2, :], ACT.Copy).then_inc(h_hi, 1)

            for n, (half, i) in enumerate(STEPS):
                p = slice(0, width(i))
                act.wait_ge(gu_full, n + 1)
                act.activation(k.f_tanh[p, n % 2, :], gate_bank[n % 2][p, :], ACT.Tanh, scale=0.5).then_inc(tanh_done, 1)
                hi(n)
                if ln_tiles(n - 1):
                    ln.act_norm(act, *ln_tiles(n - 1)[:2])
                if ln_tiles(n - 2):
                    ln.act_hi(act, *ln_tiles(n - 2))
            for j in range(2):
                ln.act_norm(act, 2, 4 + j)
            for j in range(2):
                ln.act_hi(act, 2, 4 + j, ln_bank(j))

        @block.tensor
        def _(pe):
            for n, (half, i) in enumerate(STEPS):
                w, s = width(i), n % 2
                pe.wait_ge(gu_wlo, n + 1)
                if n >= 2:
                    pe.wait_ge(h_done, n - 1)
                wg = [v[:, 0:CH * 2 * w].rearrange("p (c n) -> p c n", c=CH) for v in k.w_gu[s]]
                for j, bank in enumerate((gate_bank[s], up_bank[s])):
                    for c in range(CH):
                        last = mm3(pe, bank[0:w, :], [v[:, c, j * w:(j + 1) * w] for v in wg],
                                   [v[:, c, half * 512:(half + 1) * 512] for v in k.xnT], c == 0, c == CH - 1)
                last.then_inc(gu_full, 1)
                if ln_tiles(n - 2):
                    ln.pe_turn(pe, *ln_tiles(n - 2))
                if i == IC - 1:
                    if half == 0:
                        pe.wait_ge(dn_lo, IC)
                    for j in range(4):
                        if j < 3 or half == 1:
                            pe.wait_ge(ln.split, 2 * NT + j + 1 if half == 1 else NT + 5 + j + 1)
                        for m in range(IC):
                            p = slice(0, width(m))
                            if j == 0:
                                pe.wait_ge(h_lo, IC * half + m + 1)
                            last = mm3(pe, o_bank[j][:, :], [v[p, m, j * PART:(j + 1) * PART] for v in k.hT],
                                       [v[p, m, :] for v in k.w_dn], m == 0, m == IC - 1)
                        last.then_inc(o_full, 1)
                        if half == 1 and j in (1, 2):
                            pe.wait_ge(h_done, len(STEPS))
                            ln.pe_turn(pe, 2, 3 + j, ln_bank(j - 1))


def attn1_loads(k, sem):
    k.a1_in = {kind: sem("a1_in_" + kind) for kind in ("kv", "q", "o")}
    raw = {"kv": k.raw_kv[:, 0:KVW], "q": k.raw_q[:, :], "o": k.raw_o[:, :]}

    def load(sp, kind):
        sp.dma_start(raw[kind], k.d["w1" + kind][0:PART, :]).then_inc(k.a1_in[kind], 16)

    def split_kv(dve):
        dve.wait_ge(k.a1_in["kv"], 16)
        dve.tensor_copy(k.w_kv[0][:, :], raw["kv"]).then_inc(k.a1_kv_whi, 1)
        dve.wait_ge(k.a1_kv_whi, 1)
        dve.tensor_tensor(k.w_kv[1][:, :], raw["kv"], f(k.w_kv[0][:, :]), ALU.subtract).then_inc(k.a1_kv_wlo, 2)

    k.a1_kv_whi, k.a1_kv_wlo = sem("a1_kv_whi"), sem("a1_kv_wlo")
    k.attn1_load, k.attn1_split_kv = load, split_kv


def attn1_buffers(k, scope, sb, pair):
    k.w_q, k.w_o = pair(scope, "w1q", [CH, GH * HD]), pair(scope, "w1o", [GH, HID])
    k.qT = pair(scope, "qT1", [2, GH, PART])
    k.kT = pair(scope, "kT1", [BATCH, CTX + SEQ + CTX])
    k.v = pair(scope, "v1", [BATCH, 3, HD])
    k.pT = pair(scope, "pT1", [3, GH, SEQ])
    k.oT = pair(scope, "oT1", [GH, SEQ])
    k.q_raw, k.k_raw = sb(scope, "q_raw", [2, GH * HD]), sb(scope, "k_raw", [3, HD])
    k.p1 = sb(scope, "p1", [2, GH, SEQ + CTX])
    k.dump, k.rms_eps = sb(scope, "dump", [2 * GH + 3, HD]), sb(scope, "rms_eps", [2 * GH])
    k.ssk, k.rk = sb(scope, "ssk", [3]), sb(scope, "rk", [3])
    k.ssq, k.rq, k.mx, k.nb, k.rs, k.rinv = (sb(scope, n, [2 * GH]) for n in ("ssq", "rq", "mx", "nb", "rs", "rinv"))


def attn1_phase(nc, k, sem, ln):
    def sems(*names):
        return [sem("a1_" + n) for n in names]

    q_whi, o_whi, q_wlo, o_wlo = sems("q_whi", "o_whi", "q_wlo", "o_wlo")
    kv_whi, kv_wlo = k.a1_kv_whi, k.a1_kv_wlo
    kv_full, kv_hi, kv_split, cx_full, cx_hi, cx_split = sems("kv_full", "kv_hi", "kv_split", "cx_full", "cx_hi", "cx_split")
    q_full, q_copied, pv_full, pv_hi, pv_split, d_full, x_added = sems(
        "q_full", "q_copied", "pv_full", "pv_hi", "pv_split", "d_full", "x_added")
    t_full, t_hi, t_split, kt_full, kt_hi, kt_split, qt_full, qt_hi, qt_split = sems(
        "t_full", "t_hi", "t_split", "kt_full", "kt_hi", "kt_split", "qt_full", "qt_hi", "qt_split")
    ssk_ready, rk_ms, rk_ready, k_scaled, ssq_ready, rq_ms, rq_ready = sems(
        "ssk", "rk_ms", "rk", "k_scaled", "ssq", "rq_ms", "rq")
    s_full, mx_ready, nb_ready, exp_done, rinv_ready, p_scaled, stats_set, p_scaled_pool = sems(
        "s_full", "mx", "nb", "exp", "rinv", "p_scaled", "stats_set", "p_scaled_pool")

    CONV = {"kv": 2, "q": 4, "o": 4}
    KEYS, UNITS = SEQ + CTX, NKV * BATCH
    bx, by = k.bank[4:6], k.bank[6:8]
    halves = (slice(0, 64), slice(64, PART))
    PAIRS = [(0, 0), (0, 1), (1, 0), (1, 1)]
    ctx4 = [w[:, :].rearrange("p (c n) -> p c n", c=CH) for w in k.ctxT]
    w_kv3 = [w[:, :].rearrange("p (c n) -> p c n", c=CH) for w in k.w_kv]
    flat = {"kv": k.w_kv,
            "q": [w[:, :, :].rearrange("p a b -> p (a b)") for w in k.w_q],
            "o": [w[:, :, :].rearrange("p a b -> p (a b)") for w in k.w_o]}
    cols = {"kv": CH * 2 * HD, "q": CH * GH * HD, "o": GH * HID}
    raw = {"kv": k.raw_kv, "q": k.raw_q, "o": k.raw_o}
    arrived = k.a1_in
    whi, wlo = {"kv": kv_whi, "q": q_whi, "o": o_whi}, {"kv": kv_wlo, "q": q_wlo, "o": o_wlo}

    def y_start(b):
        return (0, 8, 15, 23)[b]

    def y_bank(b, kind, j=0):
        order = ["kv"] + (["cx"] if b % 2 == 0 else []) + ["q0", "q1", "pv0", "pv1", "d0", "d1"]
        name = kind if kind in ("kv", "cx") else f"{kind}{j}"
        return by[(y_start(b) + order.index(name)) % 2]

    def x_bank(b, kind, j=0):
        at = {"t": j, "k": 6, "q": 7 + j}[kind]
        return bx[(9 * b + at) % 2]

    def ln_tiles(n):
        if not isinstance(n, int):
            return []
        return {0: [(2, 6), (2, 7)], UNITS - 2: [(3, 0), (3, 1)], UNITS - 1: [(3, 2), (3, 3)]}.get(n, [])

    def ln_bank(b, i):
        return bx[(9 * b + 1 + i) % 2] if b < BATCH else bx[i]

    def s_pair(j):
        return k.psum[:, (j % 2) * 1024:(j % 2) * 1024 + 1024].rearrange("p (h n) -> p h n", h=2)[:, :, 0:KEYS]

    def two(ap):
        return ap.rearrange("p (b k) -> p b k", b=2)

    def p_pair(tile, hp):
        return k.p1[:, tile, 2 * hp:2 * hp + 2, :].rearrange("p h n -> p (h n)")

    def stat(j):
        tile, hp = PAIRS[j]
        return slice(tile * GH + 2 * hp, tile * GH + 2 * hp + 2)

    def loop(eng, body, tail):
        body(0, True, True)
        with eng.Fori(1, NKV - 1) as g:
            body(g, False, True)
        body(NKV - 1, False, False)
        tail(NKV * BATCH)

    with nc.Block() as block:
        @block.sync
        def _(sp):
            with sp.Fori(1, NKV) as g:
                for kind, src in (("o", "w1o"), ("kv", "w1kv"), ("q", "w1q")):
                    sp.wait_ge(wlo[kind], g * CONV[kind])
                    sp.dma_start(raw[kind][:, 0:cols[kind]], k.d[src][bass.ts(g, PART), :]).then_inc(arrived[kind], 16)
            for kind in ("kv", "q", "o"):
                sp.wait_ge(wlo[kind], NKV * CONV[kind])
                k.ffn1_load(sp, kind)

        @block.gpsimd
        def _(pool):
            def w_lo(kind, g):
                n = cols[kind] // CONV[kind]
                pool.wait_ge(whi[kind], g + 1)
                for i in range(CONV[kind]):
                    s = slice(i * n, (i + 1) * n)
                    pool.tensor_tensor(flat[kind][1][:, s], raw[kind][:, s], f(flat[kind][0][:, s]),
                                       ALU.subtract).then_inc(wlo[kind], 1)

            def p_scale(n, j):
                tile, hp = PAIRS[j]
                p = k.p1[:, tile, 2 * hp:2 * hp + 2, :]
                pool.wait_ge(rinv_ready, 4 * n + j + 1)
                pool.tensor_tensor(p, p, k.rinv[:, stat(j)].unsqueeze(2).to_broadcast([PART, 2, KEYS]),
                                   ALU.mult).then_inc(p_scaled_pool, 1)

            def body(g, first, nxt):
                for b in range(BATCH):
                    n = BATCH * g + b
                    pool.wait_ge(ssk_ready, n + 1)
                    pool.tensor_tensor(k.rk[:, :], k.ssk[:, :], k.rms_eps[:, 0:3], ALU.add).then_inc(rk_ms, 1)
                    pool.wait_ge(rk_ms, n + 1)
                    pool.tensor_tensor(k.rk[:, :], k.rk[:, :], k.minus_half[:, 0:3], ALU.pow).then_inc(rk_ready, 1)
                    for tile in ln_tiles(n):
                        ln.pool_rstd(pool, *tile)
                    if b == 1:
                        w_lo("o", g)
                    pool.wait_ge(ssq_ready, n + 1)
                    pool.tensor_tensor(k.rq[:, :], k.ssq[:, :], k.rms_eps[:, :], ALU.add).then_inc(rq_ms, 1)
                    pool.wait_ge(rq_ms, n + 1)
                    pool.tensor_tensor(k.rq[:, :], k.rq[:, :], k.minus_half[:, 0:8], ALU.pow).then_inc(rq_ready, 1)
                    if b == BATCH - 1 and nxt:
                        w_lo("kv", g + 1)
                    p_scale(n, 0)
                    if b == BATCH - 1 and nxt:
                        w_lo("q", g + 1)

            pool.memset(k.rms_eps[:, :], HD * RMS_EPS)
            pool.memset(k.ssk[:, :], 1.0).then_inc(stats_set, 1)
            def tail(n):
                for t in (4, 5):
                    ln.pool_rstd(pool, 3, t)
                for w in k.w_kv:
                    last = pool.memset(f(w[:, :].rearrange("p (c n) -> p c n", c=CH)[:, :, LR + NEXP:256]), 0.0)
                last.then_inc(k.ag_pad, 1)

            loop(pool, body, tail)

        @block.vector
        def _(dve):
            def w_hi(kind, g):
                dve.wait_ge(arrived[kind], 16 * g + 16)
                dve.tensor_copy(flat[kind][0][:, :], raw[kind][:, 0:cols[kind]]).then_inc(whi[kind], 1)

            def t_lo(n, b, j):
                hp, kt = divmod(j, 3)
                bank = x_bank(b, "t", j)
                dve.wait_ge(t_hi, 6 * (n - 1) + j + 1)
                if kt < 2:
                    last = dve.tensor_tensor(k.pT[1][:, kt, 2 * hp:2 * hp + 2, :], bank.rearrange("p (h q) -> p h q", h=2),
                                             f(k.pT[0][:, kt, 2 * hp:2 * hp + 2, :]), ALU.subtract)
                else:
                    for i in range(2):
                        last = dve.tensor_tensor(k.pT[0][halves[1 - i], 2, 2 * hp + i, :], bank[halves[i], 0:SEQ],
                                                 f(k.pT[0][halves[i], 2, 2 * hp + i, :]), ALU.subtract)
                last.then_inc(t_split, 1)

            def pv_lo(n, b, hp):
                dve.wait_ge(pv_hi, 2 * (n - 1) + hp + 1)
                dve.tensor_tensor(k.oT[1][:, 2 * hp:2 * hp + 2, :],
                                  y_bank(b, "pv", hp)[:, :].rearrange("p (h q) -> p h q", h=2),
                                  f(k.oT[0][:, 2 * hp:2 * hp + 2, :]), ALU.subtract).then_inc(pv_split, 1)

            def x_add(n, b, j):
                t = 2 * ((b - 1) % BATCH) + j
                dve.wait_ge(d_full, 2 * (n - 1) + j + 1)
                dve.scalar_tensor_tensor(out=k.x[:, t, :], in0=y_bank(b, "d", j)[:, :], scalar=k.gate[:, 1:2],
                                         in1=k.x[:, t, :], op0=ALU.mult, op1=ALU.add).then_inc(x_added, 1)

            def q_squares(n, b, tile):
                dve.wait_ge(q_copied, 2 * n + tile + 1)
                for h in range(GH):
                    q = k.q_raw[:, tile, h * HD:(h + 1) * HD]
                    last = dve.tensor_tensor_reduce(k.dump[:, tile * GH + h, :], q, q, 1.0, 0.0, ALU.mult, ALU.add,
                                                    k.ssq[:, tile * GH + h:tile * GH + h + 1])
                if tile == 1:
                    last.then_inc(ssq_ready, 1)

            def row_max(n, j):
                dve.wait_ge(s_full, 4 * n + j + 1)
                dve.tensor_reduce(k.mx[:, stat(j)], s_pair(j), AX.X, ALU.max).then_inc(mx_ready, 1)
                if j == 0:
                    dve.wait_ge(rq_ready, n + 1)
                dve.wait_ge(mx_ready, 4 * n + j + 1)
                dve.scalar_tensor_tensor(out=k.nb[:, stat(j)], in0=k.mx[:, stat(j)], scalar=-1.0, in1=k.rq[:, stat(j)],
                                         op0=ALU.mult, op1=ALU.mult).then_inc(nb_ready, 1)

            def scale_p(n, j):
                tile, hp = PAIRS[j]
                dve.wait_ge(exp_done, 4 * n + j + 1)
                dve.reciprocal(k.rinv[:, stat(j)], k.rs[:, stat(j)]).then_inc(rinv_ready, 1)
                if j == 0:
                    return
                dve.wait_ge(rinv_ready, 4 * n + j + 1)
                for h in (2 * hp, 2 * hp + 1):
                    last = dve.tensor_scalar(k.p1[:, tile, h, :], k.p1[:, tile, h, :],
                                             k.rinv[:, tile * GH + h:tile * GH + h + 1], None, ALU.mult)
                last.then_inc(p_scaled, 1)

            def body(g, first, nxt):
                for b in range(BATCH):
                    n, prev = BATCH * g + b, not (first and b == 0)
                    dve.wait_ge(kv_hi, n + 1)
                    bank = y_bank(b, "kv")[:, :].rearrange("p (t n) -> p t n", t=2)
                    dve.tensor_tensor(k.v[1][:, b, 0:2, :], bank[:, :, HD:2 * HD], f(k.v[0][:, b, 0:2, :]),
                                      ALU.subtract).then_inc(kv_split, 1)
                    if b % 2 == 0:
                        dve.wait_ge(cx_hi, 2 * g + b // 2 + 1)
                        for i in range(2):
                            for half in (slice(0, 64), slice(64, PART)):
                                last = dve.tensor_tensor(k.v[1][half, b + i, 2, :],
                                                         y_bank(b, "cx")[64 * i:64 * i + 64, HD:2 * HD],
                                                         f(k.v[0][64 * i:64 * i + 64, b + i, 2, :]), ALU.subtract)
                        last.then_inc(cx_split, 1)
                    if prev:
                        t_lo(n, b, 0)
                    nk = 3 if b % 2 == 0 else 2
                    for i in range(nk):
                        last = dve.tensor_tensor_reduce(k.dump[:, 2 * GH + i, :], k.k_raw[:, i, :], k.k_raw[:, i, :], 1.0, 0.0,
                                                        ALU.mult, ALU.add, k.ssk[:, i:i + 1])
                    last.then_inc(ssk_ready, 1)
                    if not nxt and b >= 2:
                        ln.dve_stats(dve, 3, 2 * b - 4)
                        ln.dve_stats(dve, 3, 2 * b - 3)
                    if not prev:
                        ln.dve_stats(dve, 2, 6)
                        ln.dve_stats(dve, 2, 7)
                    if prev:
                        t_lo(n, b, 1)
                    dve.wait_ge(rk_ready, n + 1)
                    for i in range(nk):
                        last = dve.tensor_scalar(k.k_raw[:, i, :], k.k_raw[:, i, :], k.rk[:, i:i + 1], None, ALU.mult)
                    last.then_inc(k_scaled, 1)
                    if prev:
                        t_lo(n, b, 2)
                        t_lo(n, b, 3)
                    q_squares(n, b, 0)
                    if prev:
                        t_lo(n, b, 4)
                        t_lo(n, b, 5)
                    q_squares(n, b, 1)
                    if prev:
                        pv_lo(n, b, 0)
                    dve.wait_ge(kt_hi, n + 1)
                    bank = x_bank(b, "k")
                    last = dve.scalar_tensor_tensor(out=k.kT[1][:, b, CTX:KEYS], in0=bank[:, 0:SEQ], scalar=k.qkw[:, 0:1],
                                                    in1=f(k.kT[0][:, b, CTX:KEYS]), op0=ALU.mult, op1=ALU.subtract)
                    if b % 2 == 0:
                        for at in (slice(0, CTX), slice(KEYS, KEYS + CTX)):
                            last = dve.scalar_tensor_tensor(
                                out=k.kT[1][:, b:b + 2, at], in0=two(bank[:, SEQ:SEQ + 2 * CTX]), scalar=k.qkw[:, 0:1],
                                in1=f(k.kT[0][:, b:b + 2, at]), op0=ALU.mult, op1=ALU.subtract)
                    last.then_inc(kt_split, 1)
                    for tile in range(2):
                        dve.wait_ge(qt_hi, 2 * n + tile + 1)
                        dve.tensor_tensor(k.qT[1][:, tile, :, :],
                                          x_bank(b, "q", tile)[:, :].rearrange("p (h q) -> p h q", h=GH),
                                          f(k.qT[0][:, tile, :, :]), ALU.subtract).then_inc(qt_split, 1)
                        if prev and tile == 0:
                            pv_lo(n, b, 1)
                    if b == BATCH - 1 and nxt:
                        w_hi("kv", g + 1)
                    row_max(n, 0)
                    row_max(n, 1)
                    scale_p(n, 0)
                    if prev:
                        x_add(n, b, 0)
                    for i, tile in enumerate(ln_tiles(n)):
                        ln.dve_lo(dve, *tile, ln_bank(b, i))
                    row_max(n, 2)
                    if b == BATCH - 1 and nxt:
                        w_hi("q", g + 1)
                    scale_p(n, 1)
                    if prev:
                        x_add(n, b, 1)
                    row_max(n, 3)
                    scale_p(n, 2)
                    scale_p(n, 3)
                    if b == 0:
                        w_hi("o", g)

            def tail(n):
                for j in range(4):
                    t_lo(n, 0, j)
                ln.dve_stats(dve, 3, 4)
                pv_lo(n, 0, 0)
                ln.dve_stats(dve, 3, 5)
                for j in (4, 5):
                    t_lo(n, 0, j)
                pv_lo(n, 0, 1)
                for i in range(2):
                    ln.dve_lo(dve, 3, 4 + i, ln_bank(4, i))
                k.ffn1_split_ag(dve)
                for j in range(2):
                    x_add(n, 0, j)

            def own_lo(kind):
                dve.wait_ge(whi[kind], 1)
                dve.tensor_tensor(flat[kind][1][:, :], raw[kind][:, 0:cols[kind]], f(flat[kind][0][:, :]),
                                  ALU.subtract).then_inc(wlo[kind], CONV[kind])

            w_hi("q", 0)
            own_lo("q")
            dve.wait_ge(stats_set, 1)
            loop(dve, body, tail)

        @block.scalar
        def _(act):
            def t_evac(n, b, j):
                hp, kt = divmod(j, 3)
                bank = x_bank(b, "t", j)
                act.wait_ge(t_full, 6 * (n - 1) + j + 1)
                if kt < 2:
                    last = act.activation(k.pT[0][:, kt, 2 * hp:2 * hp + 2, :], bank.rearrange("p (h q) -> p h q", h=2), ACT.Copy)
                else:
                    for i in range(2):
                        last = act.activation(k.pT[0][halves[i], 2, 2 * hp + i, :], bank[halves[i], 0:SEQ], ACT.Copy)
                last.then_inc(t_hi, 1)

            def pv_evac(n, b, hp):
                act.wait_ge(pv_full, 2 * (n - 1) + hp + 1)
                act.activation(k.oT[0][:, 2 * hp:2 * hp + 2, :],
                               y_bank(b, "pv", hp)[:, :].rearrange("p (h q) -> p h q", h=2), ACT.Copy).then_inc(pv_hi, 1)

            def body(g, first, nxt):
                for b in range(BATCH):
                    n, prev = BATCH * g + b, not (first and b == 0)
                    act.wait_ge(kv_full, n + 1)
                    bank = y_bank(b, "kv")[:, :].rearrange("p (t n) -> p t n", t=2)
                    act.activation(k.k_raw[:, 0:2, :], bank[:, :, 0:HD], ACT.Copy)
                    act.activation(k.v[0][:, b, 0:2, :], bank[:, :, HD:2 * HD], ACT.Copy).then_inc(kv_hi, 1)
                    if b % 2 == 0:
                        act.wait_ge(cx_full, 2 * g + b // 2 + 1)
                        act.activation(k.k_raw[:, 2, :], y_bank(b, "cx")[:, 0:HD], ACT.Copy)
                        for i in range(2):
                            for half in (slice(0, 64), slice(64, PART)):
                                last = act.activation(k.v[0][half, b + i, 2, :],
                                                      y_bank(b, "cx")[64 * i:64 * i + 64, HD:2 * HD], ACT.Copy)
                        last.then_inc(cx_hi, 1)
                    for j in range(6):
                        if prev:
                            t_evac(n, b, j)
                            if j == 5:
                                pv_evac(n, b, 0)
                        if j in (1, 3):
                            act.wait_ge(q_full, 2 * n + j // 2 + 1)
                            act.activation(k.q_raw[:, j // 2, :], y_bank(b, "q", j // 2)[:, :], ACT.Copy)\
                               .then_inc(q_copied, 1)
                    act.wait_ge(kt_full, n + 1)
                    bank = x_bank(b, "k")
                    last = act.activation(k.kT[0][:, b, CTX:KEYS], bank[:, 0:SEQ], ACT.Copy, scale=k.qkw[:, 0:1])
                    if b % 2 == 0:
                        for at in (slice(0, CTX), slice(KEYS, KEYS + CTX)):
                            last = act.activation(k.kT[0][:, b:b + 2, at], two(bank[:, SEQ:SEQ + 2 * CTX]),
                                                  ACT.Copy, scale=k.qkw[:, 0:1])
                    last.then_inc(kt_hi, 1)
                    for tile in range(2):
                        act.wait_ge(qt_full, 2 * n + tile + 1)
                        act.activation(k.qT[0][:, tile, :, :],
                                       x_bank(b, "q", tile)[:, :].rearrange("p (h q) -> p h q", h=GH),
                                       ACT.Copy).then_inc(qt_hi, 1)
                        if prev and tile == 0:
                            pv_evac(n, b, 1)
                        if tile == 0:
                            for late in ln_tiles(n):
                                ln.act_norm(act, *late)
                    for j, (tile, hp) in enumerate(PAIRS):
                        act.wait_ge(nb_ready, 4 * n + j + 1)
                        for h in (2 * hp, 2 * hp + 1):
                            i = tile * GH + h
                            last = act.activation(k.p1[:, tile, h, :], s_pair(j)[:, h % 2, :], ACT.Exp,
                                                  bias=k.nb[:, i:i + 1], scale=k.rq[:, i:i + 1],
                                                  accum_out=k.rs[:, i:i + 1])
                        last.then_inc(exp_done, 1)
                        if j == 1:
                            for i, tile in enumerate(ln_tiles(n)):
                                ln.act_hi(act, *tile, ln_bank(b, i))

            def tail(n):
                for j in range(6):
                    t_evac(n, 0, j)
                    if j == 3:
                        pv_evac(n, 0, 0)
                pv_evac(n, 0, 1)
                for t in (4, 5):
                    ln.act_norm(act, 3, t)
                for t in (4, 5):
                    ln.act_hi(act, 3, t, ln_bank(4, t % 2))

            loop(act, body, tail)

        @block.tensor
        def _(pe):
            def turn(n, b, j, alone=False):
                hp, kt = divmod(j, 3)
                if kt == 0:
                    if hp == 0:
                        pe.wait_ge(p_scaled_pool, n)
                    pe.wait_ge(p_scaled, 3 * (n - 1) + 2 + hp)
                if ln_tiles(n - 1) and j < 2:
                    c, t = ln_tiles(n - 1)[j]
                    pe.wait_ge(ln.split, NT * c + t + 1)
                elif j < 2:
                    pe.wait_ge(qt_split, 2 * n - 1 + j)
                elif j == 4:
                    pe.wait_ge(t_split, 6 * (n - 1) + 4)
                elif j == 3 or alone and j == 2:
                    pe.wait_ge(t_split, 6 * (n - 1) + j - 1)
                bank = x_bank(b, "t", j)
                if kt == 2:
                    for tile in range(2):
                        last = pe.transpose(bank[:, tile * PART:(tile + 1) * PART],
                                            p_pair(tile, hp)[:, SEQ:SEQ + 2 * CTX], k.ident[:, :])
                else:
                    for hh in range(2):
                        for tile in range(2):
                            last = pe.transpose(bank[:, (2 * hh + tile) * PART:(2 * hh + tile + 1) * PART],
                                                k.p1[:, tile, 2 * hp + hh, CTX * hh + kt * PART:CTX * hh + (kt + 1) * PART],
                                                k.ident[:, :])
                last.then_inc(t_full, 1)

            def p_v(n, b, hp, alone=False):
                pb = (b - 1) % BATCH
                pe.wait_ge(t_split, 6 * (n - 1) + 3 * (hp + 1))
                if not alone:
                    pe.wait_ge(q_copied, 2 * n + hp + 1)
                for kt in range(2):
                    mm3(pe, y_bank(b, "pv", hp)[:, :], [w[:, pb, kt, :] for w in k.v],
                        [w[:, kt, 2 * hp:2 * hp + 2, :] for w in k.pT], kt == 0, False)
                for w in (k.v[1], k.v[0]):
                    last = pe.matmul(y_bank(b, "pv", hp)[:, :], w[:, pb, 2, :], k.pT[0][:, 2, 2 * hp:2 * hp + 2, :],
                                     start=False, stop=w is k.v[0])
                last.then_inc(pv_full, 1)

            def out(n, b, j):
                pe.wait_ge(pv_split, 2 * n)
                for h in range(GH):
                    last = mm3(pe, y_bank(b, "d", j)[:, :], [w[:, h, j * PART:(j + 1) * PART] for w in k.oT],
                               [w[:, h, :] for w in k.w_o], h == 0, h == GH - 1)
                last.then_inc(d_full, 1)

            def scores(n, b, j):
                tile, hp = PAIRS[j]
                if j == 0:
                    pe.wait_ge(kt_split, n + 1)
                if hp == 0:
                    pe.wait_ge(qt_split, 2 * n + tile + 1)
                if not (isinstance(n, int) and 4 * n + j < 2):
                    pe.wait_ge(exp_done, 4 * n + j - 1)
                for hh in range(2):
                    last = mm3(pe, s_pair(j)[:, hh, :], [w[:, tile, 2 * hp + hh, :] for w in k.qT],
                               [w[:, b, CTX * (1 - hh):CTX * (1 - hh) + KEYS] for w in k.kT], True, True)
                last.then_inc(s_full, 1)

            def body(g, first, nxt):
                for b in range(BATCH):
                    n, prev = BATCH * g + b, not (first and b == 0)
                    deep = not (first and b < 2)
                    if b == 0:
                        pe.wait_ge(kv_wlo, CONV["kv"] * (g + 1))
                    if deep:
                        pe.wait_ge(x_added, 2 * (n - 2) + 1)
                    for tile in range(2):
                        t = 2 * b + tile
                        for c in range(CH):
                            last = mm3(pe, y_bank(b, "kv")[:, tile * 256:tile * 256 + 256],
                                       [w[:, c, t * PART:(t + 1) * PART] for w in k.xnT],
                                       [w[:, c, :] for w in w_kv3], c == 0, c == CH - 1)
                    last.then_inc(kv_full, 1)
                    if deep:
                        pe.wait_ge(x_added, 2 * (n - 2) + 2)
                    if b % 2 == 0:
                        for c in range(CH):
                            last = mm3(pe, y_bank(b, "cx")[:, 0:256], [w[:, c, b * CTX:(b + 2) * CTX] for w in ctx4],
                                       [w[:, c, :] for w in w_kv3], c == 0, c == CH - 1)
                        last.then_inc(cx_full, 1)
                    if b == 0:
                        pe.wait_ge(q_wlo, CONV["q"] * (g + 1))
                    for tile in range(2):
                        if prev:
                            turn(n, b, 2 * tile)
                            turn(n, b, 2 * tile + 1)
                        if b % 2 == 0:
                            pe.wait_ge(kv_split if tile == 0 else cx_split, n + 1 if tile == 0 else 2 * g + b // 2 + 1)
                        elif tile == 1:
                            pe.wait_ge(kv_split, n + 1)
                        t = 2 * b + tile
                        for c in range(CH):
                            if prev and tile == 0 and c == CH - 1:
                                pe.wait_ge(t_split, 6 * (n - 1) + 1)
                            last = mm3(pe, y_bank(b, "q", tile)[:, :], [w[:, c, t * PART:(t + 1) * PART] for w in k.xnT],
                                       [w[:, c, :] for w in k.w_q], c == 0, c == CH - 1)
                        last.then_inc(q_full, 1)
                    if prev:
                        turn(n, b, 4)
                        turn(n, b, 5)
                        p_v(n, b, 0)
                        pe.wait_ge(t_split, 6 * (n - 1) + 5)
                    pe.wait_ge(k_scaled, n + 1)
                    nk = 3 if b % 2 == 0 else 2
                    for i in range(nk):
                        last = pe.transpose(x_bank(b, "k")[:, i * PART:(i + 1) * PART], k.k_raw[:, i, :], k.ident[:, :])
                    last.then_inc(kt_full, 1)
                    for tile in range(2):
                        pe.wait_ge(q_copied, 2 * n + tile + 1)
                        if tile == 1:
                            pe.wait_ge(kt_split, n + 1)
                        elif prev:
                            pe.wait_ge(t_split, 6 * n)
                        for h in range(GH):
                            last = pe.transpose(x_bank(b, "q", tile)[:, h * PART:(h + 1) * PART],
                                                k.q_raw[:, tile, h * HD:(h + 1) * HD], k.ident[:, :])
                        last.then_inc(qt_full, 1)
                        if prev and tile == 0:
                            p_v(n, b, 1)
                    scores(n, b, 0)
                    scores(n, b, 1)
                    if ln_tiles(n):
                        pe.wait_ge(qt_split, 2 * n + 2)
                    for i, tile in enumerate(ln_tiles(n)):
                        ln.pe_turn(pe, *tile, ln_bank(b, i))
                    if prev:
                        if b == 1:
                            pe.wait_ge(o_wlo, CONV["o"] * (g + 1))
                        out(n, b, 0)
                    scores(n, b, 2)
                    if prev:
                        out(n, b, 1)
                    scores(n, b, 3)

            def tail(n):
                for j in range(6):
                    turn(n, 0, j, alone=True)
                    if j == 3:
                        pe.wait_ge(x_added, 2 * (n - 1))
                        p_v(n, 0, 0, alone=True)
                p_v(n, 0, 1, alone=True)
                for i in range(2):
                    ln.pe_turn(pe, 3, 4 + i, ln_bank(4, i))
                for j in range(2):
                    out(n, 0, j)

            loop(pe, body, tail)


def ffn1_loads(k, sem):
    k.f1_in = {kind: sem("f1_in_" + kind) for kind in ("kv", "q", "o")}

    def load(sp, kind):
        done = k.f1_in[kind]
        if kind == "kv":
            sp.dma_start(k.raw_kv[:, 0:CH * (LR + NEXP)], k.d["w_ag"]).then_inc(done, 16)
        elif kind == "q":
            sp.dma_start(k.raw_q[:, :], k.d["w_base"]).then_inc(done, 16)
        else:
            sp.dma_start(k.raw_o[:, 0:HID], k.d["w_b"][0:PART, :]).then_inc(done, 16)
            sp.dma_start(k.raw_o[0:LR - PART, HID:2 * HID], k.d["w_b"][PART:LR, :]).then_inc(done, 16)

    def split_ag(dve):
        raw = k.raw_kv[:, 0:CH * (LR + NEXP)].rearrange("p (c n) -> p c n", c=CH)
        hi, lo = [w[:, :].rearrange("p (c n) -> p c n", c=CH)[:, :, 0:LR + NEXP] for w in k.w_kv]
        dve.wait_ge(k.f1_in["kv"], 16)
        dve.tensor_copy(hi, raw).then_inc(k.ag_hi, 1)
        dve.wait_ge(k.ag_hi, 1)
        dve.tensor_tensor(lo, raw, f(hi), ALU.subtract).then_inc(k.ag_lo, 1)

    k.ag_hi, k.ag_lo, k.ag_pad = sem("f1_ag_hi"), sem("f1_ag_lo"), sem("f1_ag_pad")
    k.ffn1_load, k.ffn1_split_ag = load, split_ag


def ffn1_buffers(k, scope, sb, pair):
    k.w_base, k.w_b = pair(scope, "w_base", [CH, HID]), pair(scope, "w_b", [2, HID])
    k.w_ag = [w[:, :].rearrange("p (c n) -> p c n", c=CH) for w in k.w_kv]
    k.ag = sb(scope, "ag", [2, 256])
    k.top, k.idx, k.idxf = sb(scope, "top", [2, 8]), sb(scope, "idx", [2, 8], mybir.dt.uint32), sb(scope, "idxf", [2, 2])
    k.iota_i, k.iota = sb(scope, "iota_i", [NEXP], mybir.dt.int32), sb(scope, "iota", [NEXP])
    k.gap, k.eg, k.pr = sb(scope, "gap", [2, 1]), sb(scope, "eg", [2, 1]), sb(scope, "pr", [2, 4])
    k.ga, k.gb, k.gm = (sb(scope, n, [2, NEXP]) for n in ("ga", "gb", "gm"))
    k.hg = sb(scope, "hg", [2, LR])
    k.hgT = pair(scope, "hgT", [2, 2, PART])


def ffn1_phase(nc, k, sem, ln):
    def sems(*names):
        return [sem("f1_" + n) for n in names]

    w_in, b_in = k.f1_in["q"], k.f1_in["o"]
    w_hi, w_lo, b_hi, b_lo = sems("w_hi", "w_lo", "b_hi", "b_lo")
    ag_full, ag_out, o_full, t_full, t_hi, t_lo, x_done, stored = sems(
        "ag_full", "ag_out", "o_full", "t_full", "t_hi", "t_lo", "x_done", "stored")
    route, t_gap, exp_done, hg_done, iota_i = sems("route", "gap", "exp", "hg", "iota_i")
    R1 = LR - PART
    o_bank, ag_bank, t_bank = k.bank[0:3], k.bank[3:5], k.bank[5:7]
    LATE = [(6, k.bank[7]), (7, k.bank[6])]

    with nc.Block() as block:
        @block.sync
        def _(sp):
            for t in range(NT):
                sp.wait_ge(x_done, t + 1)
                sp.dma_start(k.out[t * PART:(t + 1) * PART, :], k.x[:, t, :]).then_inc(stored, 16)
            sp.wait_ge(stored, 16 * NT)

        raw_base = k.raw_q[:, :].rearrange("p (c n) -> p c n", c=CH)

        @block.gpsimd
        def _(pool):
            pool.iota(k.iota_i[:, :], pattern=[[1, NEXP]], base=0, channel_multiplier=0).then_inc(iota_i, 1)
            pool.wait_ge(b_hi, 1)
            pool.tensor_tensor(k.w_b[1][:, 0, :], k.raw_o[:, 0:HID], f(k.w_b[0][:, 0, :]), ALU.subtract)
            pool.tensor_tensor(k.w_b[1][0:R1, 1, :], k.raw_o[0:R1, HID:2 * HID], f(k.w_b[0][0:R1, 1, :]),
                               ALU.subtract).then_inc(b_lo, 1)
            for t, _ in LATE:
                ln.pool_rstd(pool, 3, t)

        @block.vector
        def _(dve):
            links = [0]

            def link(ins):
                links[0] += 1
                ins.then_inc(route, 1)
                dve.wait_ge(route, links[0])

            dve.wait_ge(w_in, 16)
            dve.tensor_copy(k.w_base[0][:, :, :], raw_base).then_inc(w_hi, 1)
            dve.wait_ge(w_hi, 1)
            dve.tensor_tensor(k.w_base[1][:, :, :], raw_base, f(k.w_base[0][:, :, :]), ALU.subtract).then_inc(w_lo, 1)
            dve.wait_ge(b_in, 32)
            dve.tensor_copy(k.w_b[0][:, 0, :], k.raw_o[:, 0:HID])
            dve.tensor_copy(k.w_b[0][0:R1, 1, :], k.raw_o[0:R1, HID:2 * HID]).then_inc(b_hi, 1)
            for t, _ in LATE:
                ln.dve_stats(dve, 3, t)
            dve.wait_ge(iota_i, 1)
            link(dve.tensor_copy(k.iota[:, :], k.iota_i[:, :]))

            for s in range(NT + 2):
                if s == 2:
                    for t, bank in LATE:
                        ln.dve_lo(dve, 3, t, bank)
                if s < NT:
                    u = s % 2
                    logits = k.ag[:, u, LR:LR + NEXP]
                    dve.wait_ge(ag_out, s + 1)
                    link(dve.max(k.top[:, u, :], logits))
                    dve.tensor_scalar(k.gap[:, u, :], k.top[:, u, 1:2], k.top[:, u, 0:1], None, ALU.subtract)\
                       .then_inc(t_gap, 1)
                    link(dve.max_index(k.idx[:, u, :], k.top[:, u, :], logits))
                    link(dve.tensor_copy(k.idxf[:, u, :], k.idx[:, u, 0:2]))
                    dve.wait_ge(exp_done, s + 1)
                    link(dve.tensor_scalar(k.pr[:, u, 0:1], k.eg[:, u, :], 1.0, 1.0 / LORA_SCALE, ALU.add, ALU.mult))
                    link(dve.reciprocal(k.pr[:, u, 1:2], k.pr[:, u, 0:1]))
                    link(dve.tensor_tensor(k.pr[:, u, 2:3], k.pr[:, u, 1:2], k.eg[:, u, :], ALU.mult))
                    dve.tensor_scalar(k.ga[:, u, :], k.iota[:, :], k.idxf[:, u, 0:1], k.pr[:, u, 1:2],
                                      ALU.is_equal, ALU.mult)
                    link(dve.tensor_scalar(k.gb[:, u, :], k.iota[:, :], k.idxf[:, u, 1:2], k.pr[:, u, 2:3],
                                           ALU.is_equal, ALU.mult))
                    link(dve.tensor_tensor(k.gm[:, u, :], k.ga[:, u, :], k.gb[:, u, :], ALU.add))
                    if s >= 2:
                        dve.wait_ge(t_full, s - 1)
                    dve.tensor_tensor(k.hg[:, u, :].rearrange("p (e r) -> p e r", r=RANK),
                                      k.ag[:, u, 0:LR].rearrange("p (e r) -> p e r", r=RANK),
                                      k.gm[:, u, :].unsqueeze(2).to_broadcast([PART, NEXP, RANK]),
                                      ALU.mult).then_inc(hg_done, 1)
                if 1 <= s <= NT:
                    u = (s - 1) % 2
                    dve.wait_ge(t_hi, s)
                    dve.tensor_tensor(k.hgT[1][:, u, 0, :], t_bank[u][:, 0:PART], f(k.hgT[0][:, u, 0, :]), ALU.subtract)
                    dve.tensor_tensor(k.hgT[1][0:R1, u, 1, :], t_bank[u][0:R1, PART:2 * PART],
                                      f(k.hgT[0][0:R1, u, 1, :]), ALU.subtract).then_inc(t_lo, 1)
                if s >= 2:
                    t = s - 2
                    dve.wait_ge(o_full, t + 1)
                    dve.scalar_tensor_tensor(out=k.x[:, t, :], in0=o_bank[t % 3][:, :], scalar=k.gate[:, 3:4],
                                             in1=k.x[:, t, :], op0=ALU.mult, op1=ALU.add).then_inc(x_done, 1)

        @block.scalar
        def _(act):
            for s in range(NT + 1):
                if s == 1:
                    for t, _ in LATE:
                        ln.act_norm(act, 3, t)
                if s == 2:
                    for t, bank in LATE:
                        ln.act_hi(act, 3, t, bank)
                if s < NT:
                    act.wait_ge(ag_full, s + 1)
                    if s >= 2:
                        act.wait_ge(hg_done, s - 1)
                    act.activation(k.ag[:, s % 2, :], ag_bank[s % 2][:, 0:256], ACT.Copy).then_inc(ag_out, 1)
                    act.wait_ge(t_gap, s + 1)
                    act.activation(k.eg[:, s % 2, :], k.gap[:, s % 2, :], ACT.Exp).then_inc(exp_done, 1)
                if s >= 1:
                    u = (s - 1) % 2
                    act.wait_ge(t_full, s)
                    act.activation(k.hgT[0][:, u, 0, :], t_bank[u][:, 0:PART], ACT.Copy)
                    act.activation(k.hgT[0][0:R1, u, 1, :], t_bank[u][0:R1, PART:2 * PART], ACT.Copy).then_inc(t_hi, 1)

        @block.tensor
        def _(pe):
            pe.wait_ge(k.ag_pad, 1)
            for s in range(NT + 2):
                if s == 2:
                    for t, bank in LATE:
                        ln.pe_turn(pe, 3, t, bank)
                if s < NT:
                    tok = slice(s * PART, (s + 1) * PART)
                    if s == 0:
                        pe.wait_ge(k.ag_lo, 1)
                    if s >= 2:
                        pe.wait_ge(ag_out, s - 1)
                    for c in range(CH):
                        last = mm3(pe, ag_bank[s % 2][:, 0:256], [w[:, c, tok] for w in k.xnT],
                                   [w[:, c, :] for w in k.w_ag], c == 0, c == CH - 1)
                    last.then_inc(ag_full, 1)
                    if s == 0:
                        pe.wait_ge(w_lo, 1)
                    if s >= 3:
                        pe.wait_ge(x_done, s - 2)
                    for c in range(CH):
                        mm3(pe, o_bank[s % 3][:, :], [w[:, c, tok] for w in k.xnT], [w[:, c, :] for w in k.w_base],
                            c == 0, False)
                if 1 <= s <= NT:
                    u = (s - 1) % 2
                    pe.wait_ge(hg_done, s)
                    if s == 2:
                        pe.wait_ge(ln.split, 4 * NT)
                    if s >= 3:
                        pe.wait_ge(t_lo, s - 2)
                    pe.transpose(t_bank[u][:, 0:PART], k.hg[:, u, 0:PART], k.ident[:, :])
                    pe.transpose(t_bank[u][0:R1, PART:2 * PART], k.hg[:, u, PART:LR], k.ident[:, :]).then_inc(t_full, 1)
                if s >= 2:
                    t = s - 2
                    if s == 2:
                        pe.wait_ge(b_lo, 1)
                    pe.wait_ge(t_lo, t + 1)
                    mm3(pe, o_bank[t % 3][:, :], [w[:, t % 2, 0, :] for w in k.hgT], [w[:, 0, :] for w in k.w_b], False, False)
                    mm3(pe, o_bank[t % 3][:, :], [w[0:R1, t % 2, 1, :] for w in k.hgT],
                        [w[0:R1, 1, :] for w in k.w_b], False, True).then_inc(o_full, 1)


def build(nc, d, out, phases=("attn0", "ffn0", "attn1", "ffn1")):
    k = Kernel()
    k.d = d
    with ExitStack() as stack:
        def sem(name):
            return stack.enter_context(nc.semaphore(name))

        def sb(scope, name, shape, dtype=F32):
            return scope.enter_context(nc.sbuf_tensor(name, [PART] + shape, dtype))

        def pair(scope, name, shape):
            return [sb(scope, name + part, shape, F32R) for part in ("_hi", "_lo")]

        k.x = sb(stack, "x", [NT, HID])
        k.ctxT = pair(stack, "ctxT", [CH * BATCH * CTX])
        k.xnT = pair(stack, "xnT", [CH, BATCH * SEQ])
        k.ident, k.ones_f = sb(stack, "ident", [PART]), sb(stack, "ones_f", [PART])
        k.ones = sb(stack, "ones", [PART], F32R)
        k.minus_half = sb(stack, "minus_half", [16])
        k.gate_raw, k.gate = sb(stack, "gate_raw", [4]), sb(stack, "gate", [4])
        k.normw, k.qkw = sb(stack, "normw", [2]), sb(stack, "qkw", [1])
        k.raw_q, k.raw_o = sb(stack, "raw_q", [GH * HID]), sb(stack, "raw_o", [GH * HID])
        k.raw_kv = sb(stack, "raw_kv", [CH * 2 * HD + GH + 2])
        k.psum = stack.enter_context(nc.psum_tensor("psum", [PART, 8 * 512], F32))
        k.bank = [k.psum[:, n * 512:(n + 1) * 512] for n in range(8)]
        k.out = out
        k.ln_st, k.ln_mv, k.ln_rs = sb(stack, "ln_st", [NT, 6]), sb(stack, "ln_mv", [NT, 2]), sb(stack, "ln_rs", [NT])
        k.ln_nb = sb(stack, "ln_nb", [NT])

        k.w_kv = pair(stack, "w_kv", [KVW])
        k.xn_tok = sb(stack, "xn_tok", [2, HID])
        ln = LayerNorm(k, sem)
        ffn0_loads(k, sem)
        attn1_loads(k, sem)
        ffn1_loads(k, sem)
        if "attn0" in phases:
            with ExitStack() as scope:
                k.bo, k.gbo = sb(scope, "bo", [HID]), sb(scope, "gbo", [HID])
                k.w_q, k.w_o = pair(scope, "w0q", [QW]), pair(scope, "w0o", [QW])
                k.bias, k.bq_rep = sb(scope, "bias", [GH + 2]), pair(scope, "bq_rep", [PART])
                k.bqk = sb(scope, "bqk", [BATCH, GH, CTX], F32R)
                k.kvT = pair(scope, "kvT0", [2, BATCH * CTX])
                k.WK = pair(scope, "WK", [CH, BATCH, GH, CTX])
                k.VW = pair(scope, "VW", [GH // 2, BATCH, HID])
                k.p0 = sb(scope, "p0", [4, GH * CTX])
                k.mx0, k.nb0, k.sum0 = (sb(scope, n, [2, GH]) for n in ("mx0", "nb0", "sum0"))
                k.rinv0 = sb(scope, "rinv0", [4, GH])
                k.pT0 = pair(scope, "pT0", [2, 2 * PART])
                attn0_phase(nc, k, sem, ln)
        if "ffn0" in phases:
            with ExitStack() as scope:
                ffn0_buffers(k, scope, sb, pair)
                ffn0_phase(nc, k, sem, ln)
        if "attn1" in phases:
            with ExitStack() as scope:
                attn1_buffers(k, scope, sb, pair)
                attn1_phase(nc, k, sem, ln)
        if "ffn1" in phases:
            with ExitStack() as scope:
                ffn1_buffers(k, scope, sb, pair)
                ffn1_phase(nc, k, sem, ln)
                return
        done = sem("out_done")
        with nc.Block() as block:
            @block.sync
            def _(sp):
                sp.dma_start(out.rearrange("(t p) c -> p t c", p=PART), k.x[:, :, :]).then_inc(done, 16)
                sp.wait_ge(done, 16)


def layouts(inputs):
    import numpy as np
    a = {n: np.asarray(v) for n, v in inputs.items()}

    def chunked(w):
        return np.ascontiguousarray(w.reshape(-1, PART, w.shape[1]).transpose(1, 0, 2))

    def by_group(w):
        return np.ascontiguousarray(w.reshape(NKV, GH, HD, w.shape[1]).transpose(0, 2, 1, 3)).reshape(NKV * HD, -1)

    def kv_by_group(wk, wv):
        w = np.stack([wk, wv], 0).reshape(2, CH, PART, NKV, HD)
        return np.ascontiguousarray(w.transpose(3, 2, 1, 0, 4)).reshape(NKV * PART, -1)

    wkv, bkv = a["L0_xattn_Wkv"], a["L0_xattn_bkv"]
    half = NKV * HD
    biases = np.concatenate([a["L0_xattn_bq"].reshape(NKV, GH, HD).transpose(0, 2, 1),
                             bkv.reshape(2, NKV, HD).transpose(1, 2, 0)], 2).reshape(NKV * HD, GH + 2)
    gu = a["L0_ffn_w_gate_up"]
    chunks = []
    for i in range(IC):
        s = slice(i * PART, min((i + 1) * PART, INNER))
        chunks.append(np.concatenate([chunked(gu[:INNER][s].T), chunked(gu[INNER:][s].T)], 2).reshape(PART, -1))
    wd = a["L0_ffn_w_down"].T
    return {
        "x": a["x"].reshape(BATCH * SEQ, HID),
        "ctxT": chunked(a["ctx_4096"].reshape(BATCH * CTX, HID).T).reshape(PART, -1),
        "gates": np.concatenate([a["g_xattn"], a["g_ffn"]]).reshape(1, 4),
        "bo": a["L0_xattn_bo"].reshape(1, HID),
        "normw": np.stack([a["L1_xattn_q_norm_w"], a["L1_xattn_k_norm_w"]], 1),
        "w0q": by_group(a["L0_xattn_Wq"].T),
        "w0kv": np.concatenate([kv_by_group(wkv[:, :half], wkv[:, half:]), biases], 1),
        "w0o": by_group(a["L0_xattn_Wo"]),
        "w_gu": np.concatenate(chunks, 1),
        "w_down": wd,
        "w1q": np.ascontiguousarray(a["L1_xattn_Wq"].reshape(CH, PART, NKV, GH * HD).transpose(2, 1, 0, 3)).reshape(NKV * PART, -1),
        "w1kv": kv_by_group(a["L1_xattn_Wk"], a["L1_xattn_Wv"]),
        "w1o": by_group(a["L1_xattn_Wo"]),
        "w_base": chunked(a["L1_ffn_base_W"].T).reshape(PART, -1),
        "w_ag": chunked(np.concatenate([a["L1_ffn_lora_A"].reshape(LR, HID).T, a["L1_ffn_gate_W"].T], 1)).reshape(PART, -1),
        "w_b": np.ascontiguousarray(a["L1_ffn_lora_B"].transpose(0, 2, 1)).reshape(LR, HID),
    }


def kernel(**inputs):
    import numpy as _np
    import concourse.bacc as _bacc
    from concourse import mybir as _mybir
    from concourse.bass_utils import run_bass_kernel_spmd as _run

    nc = _bacc.Bacc("TRN2", target_bir_lowering=False, num_devices=1)
    arrays, d = {}, {}
    for name, a in layouts(inputs).items():
        a = _np.ascontiguousarray(a)
        arrays[f"in_{name}"] = a
        d[name] = nc.dram_tensor(f"in_{name}", a.shape, _mybir.dt.from_np(a.dtype), kind="ExternalInput").ap()
    out = nc.dram_tensor("out_x", (BATCH * SEQ, HID), F32, kind="ExternalOutput").ap()
    build(nc, d, out)
    r = _run(nc, [arrays], core_ids=[0])
    return r.results[0]["out_x"].reshape(BATCH, SEQ, HID)
```
